# Optimizing a Trainium2 kernel written in Bass

```python
import numpy as np
import jax
import jax.numpy as jnp

def _softmax(x, axis=-1):
    return jax.nn.softmax(x, axis=axis)

def _gelu(x):
    return jax.nn.gelu(x, approximate=True)

def _silu(x):
    return jax.nn.silu(x)

def _sigmoid(x):
    return jax.nn.sigmoid(x)

def _layernorm(x, axis=-1, eps=1e-05):
    m = jnp.mean(x, axis=axis, keepdims=True)
    v = jnp.var(x, axis=axis, keepdims=True)
    return (x - m) / jnp.sqrt(v + eps)

def _scatter_add(tgt, idx, src, axis=0):
    return tgt.at[idx].add(src)

def _segment_sum(src, seg, n):
    return jax.ops.segment_sum(src, seg, n)
kernel_name = 'mk_xattn_ffn_d2_seqx_r8_9a4541'

def setup_inputs(seed: int=0):
    np.random.seed(seed)
    _w = jnp.asarray

    def _rec_inputs():
        import jax
        import jax.numpy as jnp
        _rk = jax.random.key(seed)
        x = 7.22e-05 + 1 * jax.random.normal(jax.random.fold_in(_rk, 1), (8, 128, 512), jnp.float32)
        _lenS = 128 - jax.random.randint(jax.random.fold_in(_rk, 7), (8,), 0, max(1, 128 // 4) + 1, jnp.int32)
        _lenS2 = 128 - jax.random.randint(jax.random.fold_in(_rk, 8), (8,), 0, max(1, 128 // 4) + 1, jnp.int32)
        _ctx_4096P = jax.random.normal(jax.random.fold_in(_rk, 11), (8, 16, 512), jnp.float32)
        _ctx_4096c = jax.random.dirichlet(jax.random.fold_in(_rk, 511), 0.3 * jnp.ones((16,), jnp.float32), (8, 128))
        _ctx_4096t = jnp.einsum('bsk,bkd->bsd', _ctx_4096c, _ctx_4096P)
        _ctx_4096t = _ctx_4096t * jax.lax.rsqrt(jnp.mean(jnp.square(_ctx_4096t)) + 1e-12) * 0.953939
        ctx_4096 = 4.13588e-05 + 0.999923 * (_ctx_4096t + 0.3 * jax.random.normal(jax.random.fold_in(_rk, 611), (8, 128, 512), jnp.float32))
        _validS = jnp.arange(128)[None, :] < _lenS[:, None]
        _validS2 = jnp.arange(128)[None, :] < _lenS2[:, None]
        _causal = jnp.tril(jnp.ones((128, 128), dtype=bool))
        mask_BxSxS2_bk0 = jnp.logical_not(jnp.broadcast_to(_validS2[:, None, :], (8, 128, 128)))
        mask_1x1xSxS2_bk0 = jnp.logical_not(jnp.broadcast_to(_validS2[0:1, None, None, :], (1, 1, 128, 128)))
        return (x, ctx_4096, mask_BxSxS2_bk0, mask_1x1xSxS2_bk0)
    x, ctx_4096, mask_BxSxS2_bk0, mask_1x1xSxS2_bk0 = _rec_inputs()

    def _L0_xattn_setup():
        import jax, jax.numpy as jnp
        import numpy as np
        B, LQ, LK, D, H, DH = (2, 128, 128, 512, 32, 128)
        EPS = 1e-05

        def _rmsnorm(x, weight):
            var = jnp.mean(jnp.square(x), axis=-1, keepdims=True)
            return x * jax.lax.rsqrt(var + EPS) * weight
        key = jax.random.key(seed)
        ks = jax.random.split(key, 8)
        scale = 0.02
        return {'hidden_states': jax.random.normal(ks[0], (B, LQ, D), jnp.float32), 'key_value_states': jax.random.normal(ks[1], (B, LK, D), jnp.float32), 'attention_mask': jax.random.randint(ks[2], (B, LQ, LK), 0, 2) > 0, 'position_bias': jax.random.normal(ks[3], (H, LQ, LK), jnp.float32), 'ln_weight': jnp.ones((D,), jnp.float32), 'w_q': jax.random.normal(ks[4], (H * DH, D), jnp.float32) * scale, 'w_k': jax.random.normal(ks[5], (H * DH, D), jnp.float32) * scale, 'w_v': jax.random.normal(ks[6], (H * DH, D), jnp.float32) * scale, 'w_out': jax.random.normal(ks[7], (D, H * DH), jnp.float32) * scale}
    _L0_xattn_all = _L0_xattn_setup()
    _L0_xattn_in = {k: v for k, v in _L0_xattn_all.items() if k in ('position_bias', 'ln_weight', 'w_q', 'w_k', 'w_v', 'w_out')}
    del _L0_xattn_all

    def _L0_ffn_setup():
        import jax, jax.numpy as jnp
        import numpy as np
        HIDDEN = 512
        INTER = 1376
        BATCH, SEQ = (2, 256)
        key = jax.random.key(seed)
        ks = jax.random.split(key, 7)
        s_h = 1.0 / np.sqrt(HIDDEN)
        s_i = 1.0 / np.sqrt(INTER)
        return {'hidden_states': jax.random.normal(ks[0], (BATCH, SEQ, HIDDEN), dtype=jnp.float32), 'w_gate': jax.random.uniform(ks[1], (INTER, HIDDEN), jnp.float32, -s_h, s_h), 'b_gate': jax.random.uniform(ks[2], (INTER,), jnp.float32, -s_h, s_h), 'w_up': jax.random.uniform(ks[3], (INTER, HIDDEN), jnp.float32, -s_h, s_h), 'b_up': jax.random.uniform(ks[4], (INTER,), jnp.float32, -s_h, s_h), 'w_down': jax.random.uniform(ks[5], (HIDDEN, INTER), jnp.float32, -s_i, s_i), 'b_down': jax.random.uniform(ks[6], (HIDDEN,), jnp.float32, -s_i, s_i)}
    _L0_ffn_all = _L0_ffn_setup()
    _L0_ffn_in = {k: v for k, v in _L0_ffn_all.items() if k in ('w_gate', 'b_gate', 'w_up', 'b_up', 'w_down', 'b_down')}
    del _L0_ffn_all

    def _L1_xattn_setup():
        import jax, jax.numpy as jnp
        import numpy as np
        B, T, D_MODEL = (1, 256, 512)
        NUM_Q_HEADS, NUM_KV_HEADS, KEY_SIZE = (32, 8, 128)
        ATTN_MULT = 0.08838834764831845
        MAX_ATTN_VAL = 30.0

        def rotate_half(x):
            x1, x2 = jnp.split(x, 2, axis=-1)
            return jnp.concatenate((-x2, x1), axis=-1)

        def apply_rope(x):
            b, t, h, d = x.shape
            exponents = jnp.arange(0, d, 2, dtype=jnp.float32)
            inv_freq = 1.0 / 10000.0 ** (exponents / d)
            pos = jnp.arange(t, dtype=jnp.float32)
            phase = pos[:, None] * inv_freq[None, :]
            phase = jnp.tile(phase, (1, 2))[None, :, None, :]
            return (x * jnp.cos(phase) + rotate_half(x) * jnp.sin(phase)).astype(x.dtype)
        key = jax.random.key(seed)
        ks = jax.random.split(key, 8)
        query = jax.random.normal(ks[0], (B, T, D_MODEL), dtype=jnp.float32)
        kk = jax.random.normal(ks[1], (B, T, D_MODEL), dtype=jnp.float32)
        vv = jax.random.normal(ks[2], (B, T, D_MODEL), dtype=jnp.float32)
        mask = jnp.tril(jnp.ones((T, T), dtype=bool))[None, None, :, :]
        s = 0.02
        Wq = jax.random.normal(ks[3], (D_MODEL, NUM_Q_HEADS * KEY_SIZE), dtype=jnp.float32) * s
        Wk = jax.random.normal(ks[4], (D_MODEL, NUM_KV_HEADS * KEY_SIZE), dtype=jnp.float32) * s
        Wv = jax.random.normal(ks[5], (D_MODEL, NUM_KV_HEADS * KEY_SIZE), dtype=jnp.float32) * s
        Wo = jax.random.normal(ks[6], (NUM_Q_HEADS * KEY_SIZE, D_MODEL), dtype=jnp.float32) * s
        return {'query': query, 'key': kk, 'value': vv, 'mask': mask, 'Wq': Wq, 'Wk': Wk, 'Wv': Wv, 'Wo': Wo}
    _L1_xattn_all = _L1_xattn_setup()
    _L1_xattn_in = {k: v for k, v in _L1_xattn_all.items() if k in ('Wq', 'Wk', 'Wv', 'Wo')}
    del _L1_xattn_all

    def _L1_ffn_setup():
        import jax, jax.numpy as jnp
        import numpy as np
        B_, S, D_IN, D_OUT = (4, 256, 512, 512)
        N, RANK, ALPHA = (8, 16, 32)
        SCALE = ALPHA / RANK
        key = jax.random.key(seed)
        kx, ka, kb, kw, kbias = jax.random.split(key, 5)
        x = jax.random.normal(kx, (B_, S, D_IN), dtype=jnp.float32)
        lora_A = jax.random.normal(ka, (N, RANK, D_IN), dtype=jnp.float32) * (1.0 / np.sqrt(D_IN))
        lora_B = jax.random.normal(kb, (N, D_OUT, RANK), dtype=jnp.float32) * (1.0 / np.sqrt(RANK))
        W = jax.random.normal(kw, (D_OUT, D_IN), dtype=jnp.float32) * (1.0 / np.sqrt(D_IN))
        bias = jax.random.normal(kbias, (D_OUT,), dtype=jnp.float32) * 0.01
        lora_weights = jnp.full((N,), 1.0 / N, dtype=jnp.float32)
        return {'x': x, 'lora_A': lora_A, 'lora_B': lora_B, 'W': W, 'bias': bias, 'lora_weights': lora_weights}
    _L1_ffn_all = _L1_ffn_setup()
    _L1_ffn_in = {k: v for k, v in _L1_ffn_all.items() if k in ('lora_A', 'lora_B', 'W', 'bias', 'lora_weights')}
    del _L1_ffn_all
    return {'x': x, 'ctx_4096': ctx_4096, 'mask_BxSxS2_bk0': mask_BxSxS2_bk0, 'mask_1x1xSxS2_bk0': mask_1x1xSxS2_bk0, 'L0_xattn_position_bias': _L0_xattn_in['position_bias'], 'L0_xattn_ln_weight': _L0_xattn_in['ln_weight'], 'L0_xattn_w_q': _L0_xattn_in['w_q'], 'L0_xattn_w_k': _L0_xattn_in['w_k'], 'L0_xattn_w_v': _L0_xattn_in['w_v'], 'L0_xattn_w_out': _L0_xattn_in['w_out'], 'L0_ffn_w_gate': _L0_ffn_in['w_gate'], 'L0_ffn_b_gate': _L0_ffn_in['b_gate'], 'L0_ffn_w_up': _L0_ffn_in['w_up'], 'L0_ffn_b_up': _L0_ffn_in['b_up'], 'L0_ffn_w_down': _L0_ffn_in['w_down'], 'L0_ffn_b_down': _L0_ffn_in['b_down'], 'L1_xattn_Wq': _L1_xattn_in['Wq'], 'L1_xattn_Wk': _L1_xattn_in['Wk'], 'L1_xattn_Wv': _L1_xattn_in['Wv'], 'L1_xattn_Wo': _L1_xattn_in['Wo'], 'L1_ffn_lora_A': _L1_ffn_in['lora_A'], 'L1_ffn_lora_B': _L1_ffn_in['lora_B'], 'L1_ffn_W': _L1_ffn_in['W'], 'L1_ffn_bias': _L1_ffn_in['bias'], 'L1_ffn_lora_weights': _L1_ffn_in['lora_weights']}

def reference(x, ctx_4096, mask_BxSxS2_bk0, mask_1x1xSxS2_bk0, L0_xattn_position_bias, L0_xattn_ln_weight, L0_xattn_w_q, L0_xattn_w_k, L0_xattn_w_v, L0_xattn_w_out, L0_ffn_w_gate, L0_ffn_b_gate, L0_ffn_w_up, L0_ffn_b_up, L0_ffn_w_down, L0_ffn_b_down, L1_xattn_Wq, L1_xattn_Wk, L1_xattn_Wv, L1_xattn_Wo, L1_ffn_lora_A, L1_ffn_lora_B, L1_ffn_W, L1_ffn_bias, L1_ffn_lora_weights):
    import jax
    import jax.numpy as jnp

    def _L0_xattn_ref(hidden_states, key_value_states, attention_mask, position_bias, ln_weight, w_q, w_k, w_v, w_out):
        import jax, jax.numpy as jnp
        import numpy as np
        B, LQ, LK, D, H, DH = (2, 128, 128, 512, 32, 128)
        EPS = 1e-05

        def _rmsnorm(x, weight):
            var = jnp.mean(jnp.square(x), axis=-1, keepdims=True)
            return x * jax.lax.rsqrt(var + EPS) * weight
        x = _rmsnorm(hidden_states, ln_weight)
        b, lq, _ = x.shape
        lk = key_value_states.shape[1]
        h_q = (x @ w_q.T).reshape(b, lq, H, DH)
        h_k = (key_value_states @ w_k.T).reshape(b, lk, H, DH)
        h_v = (key_value_states @ w_v.T).reshape(b, lk, H, DH)
        score = jnp.einsum('bqhd,bkhd->bhqk', h_q, h_k)
        score = score + position_bias[None]
        m = attention_mask[:, None]
        score = jnp.where(m, score, -jnp.inf)
        score = jax.nn.softmax(score, axis=-1)
        score = jnp.where(m, score, 0.0)
        attn = jnp.einsum('bhqk,bkhd->bqhd', score, h_v).reshape(b, lq, H * DH)
        out = attn @ w_out.T
        return hidden_states + out

    def _L0_ffn_ref(hidden_states, w_gate, b_gate, w_up, b_up, w_down, b_down):
        import jax, jax.numpy as jnp
        import numpy as np
        HIDDEN = 512
        INTER = 1376
        BATCH, SEQ = (2, 256)
        gate = jax.nn.silu(jnp.einsum('bsh,ih->bsi', hidden_states, w_gate) + b_gate)
        up = jnp.einsum('bsh,ih->bsi', hidden_states, w_up) + b_up
        return jnp.einsum('bsi,hi->bsh', gate * up, w_down) + b_down

    def _L1_xattn_ref(query, key, value, mask, Wq, Wk, Wv, Wo):
        import jax, jax.numpy as jnp
        import numpy as np
        B, T, D_MODEL = (1, 256, 512)
        NUM_Q_HEADS, NUM_KV_HEADS, KEY_SIZE = (32, 8, 128)
        ATTN_MULT = 0.08838834764831845
        MAX_ATTN_VAL = 30.0

        def rotate_half(x):
            x1, x2 = jnp.split(x, 2, axis=-1)
            return jnp.concatenate((-x2, x1), axis=-1)

        def apply_rope(x):
            b, t, h, d = x.shape
            exponents = jnp.arange(0, d, 2, dtype=jnp.float32)
            inv_freq = 1.0 / 10000.0 ** (exponents / d)
            pos = jnp.arange(t, dtype=jnp.float32)
            phase = pos[:, None] * inv_freq[None, :]
            phase = jnp.tile(phase, (1, 2))[None, :, None, :]
            return (x * jnp.cos(phase) + rotate_half(x) * jnp.sin(phase)).astype(x.dtype)
        b, t, _ = query.shape
        d = KEY_SIZE
        h, kv_h = (NUM_Q_HEADS, NUM_KV_HEADS)
        g = h // kv_h
        q = (query @ Wq).reshape(b, t, h, d)
        k = (key @ Wk).reshape(b, t, kv_h, d)
        v = (value @ Wv).reshape(b, t, kv_h, d)
        q = apply_rope(q)
        k = apply_rope(k)
        q = q.reshape(b, t, kv_h, g, d)
        logits = jnp.einsum('btkgd,bTkd->bkgtT', q, k).astype(jnp.float32)
        logits = logits * ATTN_MULT
        logits = MAX_ATTN_VAL * jnp.tanh(logits / MAX_ATTN_VAL)
        m = mask[:, :, None, :, :]
        logits = jnp.where(m, logits, -1e+30)
        weights = jax.nn.softmax(logits, axis=-1).astype(query.dtype)
        attn = jnp.einsum('bkgtT,bTkd->btkgd', weights, v)
        attn = attn.reshape(b, t, h * d)
        return attn @ Wo

    def _L1_ffn_ref(x, lora_A, lora_B, W, bias, lora_weights):
        import jax, jax.numpy as jnp
        import numpy as np
        B_, S, D_IN, D_OUT = (4, 256, 512, 512)
        N, RANK, ALPHA = (8, 16, 32)
        SCALE = ALPHA / RANK
        h = jnp.einsum('bsd,nrd->nbsr', x, lora_A)
        coef = (SCALE * lora_weights)[:, None, None]
        lora_out = jnp.einsum('nbsr,nor->bso', h, lora_B * coef)
        base = jnp.einsum('bsd,od->bso', x, W) + bias
        return base + lora_out
    x = x + _L0_xattn_ref(_layernorm(x, axis=-1), ctx_4096, mask_BxSxS2_bk0, L0_xattn_position_bias, L0_xattn_ln_weight, L0_xattn_w_q, L0_xattn_w_k, L0_xattn_w_v, L0_xattn_w_out)
    x = x + _L0_ffn_ref(_layernorm(x, axis=-1), L0_ffn_w_gate, L0_ffn_b_gate, L0_ffn_w_up, L0_ffn_b_up, L0_ffn_w_down, L0_ffn_b_down)
    x = x + _L1_xattn_ref(_layernorm(x, axis=-1), ctx_4096, ctx_4096, mask_1x1xSxS2_bk0, L1_xattn_Wq, L1_xattn_Wk, L1_xattn_Wv, L1_xattn_Wo)
    x = x + _L1_ffn_ref(_layernorm(x, axis=-1), L1_ffn_lora_A, L1_ffn_lora_B, L1_ffn_W, L1_ffn_bias, L1_ffn_lora_weights)
    return x

_drawn_inputs = setup_inputs


def setup_inputs(seed=0):
    import zlib

    import numpy as np

    out = dict(_drawn_inputs(seed))
    spreads = {'L0_xattn_ln_weight': (1.0, 0.2), 'L1_ffn_lora_weights': (0.125, 0.2)}
    factors = {'L0_ffn_b_gate': 23.528, 'L0_ffn_b_up': 8.0, 'L0_ffn_b_down': 7.861, 'L1_ffn_bias': 8.0}
    for name, (base, spread) in spreads.items():
        noise = np.random.default_rng([zlib.crc32(name.encode()), seed]).standard_normal(out[name].shape)
        drawn = base * np.exp(spread * noise) if base else spread * noise
        out[name] = jnp.asarray(drawn.astype(out[name].dtype))
    for name, factor in factors.items():
        out[name] = (out[name] * factor).astype(out[name].dtype)
    return out
```

```python
from contextlib import ExitStack

import numpy as np
import concourse.bass as bass
from concourse import mybir

F32 = mybir.dt.float32
F32R = mybir.dt.float32r
U8 = mybir.dt.uint8
ALU = mybir.AluOpType
ACT = mybir.ActivationFunctionType
AX_X = mybir.AxisListType.X

P = 128
B = 8
D = 512
DC = D // P
TOK = B * P
HALF = TOK // 2
HB = B // 2
HEADS = 32
KV_HEADS = 8
PAIRS = HEADS // 2
INTER = 1376
FULL = INTER // P
REST = INTER - FULL * P
LORA = 128
RANK = 16
LORA_SCALE = 2.0
EPS = 1e-5
MASKED = 1e30
LOGIT_CAP = 30.0
ATTN_MULT = 0.08838834764831845
DMA = 16


def f32(ap):
    return ap.bitcast(F32)


def product(pe, out, w, x, start, stop):
    pe.matmul(out, w[1], x[0], start=start, stop=False)
    pe.matmul(out, w[0], x[1], start=False, stop=False)
    return pe.matmul(out, w[0], x[0], start=False, stop=stop)


def tok(b, n=1):
    return slice(b * P, (b + n) * P)


class Core:

    def __init__(self, nc, ctx):
        self.nc, self.ctx, self.n_sems = nc, ctx, 0
        self.banks = ctx.enter_context(nc.psum_tensor("banks", [P, 8, 512], F32))
        self.resid = self.sb(ctx, "resid", [P, B, D], F32)
        self.xT = self.pair(ctx, "xT", [P, DC, TOK])
        self.cT = self.pair(ctx, "cT", [P, DC, TOK])
        self.ident = self.sb(ctx, "ident", [P, P], F32)

    def sb(self, ctx, name, shape, dt=F32):
        return ctx.enter_context(self.nc.sbuf_tensor(name, shape, dt))

    def pair(self, ctx, name, shape):
        return (self.sb(ctx, name + "_hi", shape, F32R), self.sb(ctx, name + "_lo", shape, F32R))

    def sem(self, name):
        return self.ctx.enter_context(self.nc.semaphore(name))


def normalise_phase(core, tag, after=None, first=None):
    nc = core.nc
    resid, xT, cT, ident = core.resid, core.xT, core.cT, core.ident
    with ExitStack() as ctx:
        stats = core.sb(ctx, tag + "_stats", [P, B, 6])
        moments = core.sb(ctx, tag + "_moments", [P, B, 2])
        var_eps = core.sb(ctx, tag + "_var_eps", [P, B])
        rstd = core.sb(ctx, tag + "_rstd", [P, B])
        power = core.sb(ctx, tag + "_power", [P, B])
        normed = core.sb(ctx, tag + "_normed", [P, 2, D])
        row = core.sb(ctx, tag + "_row", [P, D]) if after is not None else None

        stats_done = core.sem(tag + "_stats_done")
        moments_done = core.sem(tag + "_moments_done")
        power_set = core.sem(tag + "_power_set")
        pool_steps = core.sem(tag + "_pool_steps")
        rstd_ready = core.sem(tag + "_rstd_ready")
        normed_ready = core.sem(tag + "_normed_ready")
        turned = core.sem(tag + "_turned")
        hi_ready = core.sem(tag + "_hi_ready")
        lo_ready = core.sem(tag + "_lo_ready")
        row_in = core.sem(tag + "_row_in")
        row_added = core.sem(tag + "_row_added")
        if first:
            x_in = core.sem(tag + "_x_in")
            ident_in = core.sem(tag + "_ident_in")
            ln_in = core.sem(tag + "_ln_in")
            ctx_in = core.sem(tag + "_ctx_in")
            ctx_hi = core.sem(tag + "_ctx_hi")
            ctx_lo = core.sem(tag + "_ctx_lo")
            hidden_ready = core.sem(tag + "_hidden_ready")
            hidden_added = core.sem(tag + "_hidden_added")
            rms_ready = core.sem(tag + "_rms_ready")
            hidden = core.sb(ctx, tag + "_hidden", [P, B, D])
            ln_w = core.sb(ctx, tag + "_ln_w", [P, D])
            rms = core.sb(ctx, tag + "_rms", [P, B])
            ctx_raw = core.sb(ctx, tag + "_ctx_raw", [P, DC, TOK])

        with nc.Block() as block:
            @block.sync
            def _(sp):
                if first:
                    x4 = first["x"].rearrange("b p d -> p b d")
                    for q in range(4):
                        sp.dma_start(resid[:, 2 * q:2 * q + 2, :], x4[:, 2 * q:2 * q + 2, :]).then_inc(x_in, DMA)
                    sp.dma_start(ident[:, :], first["ident"]).then_inc(ident_in, DMA)
                    sp.dma_start(ln_w[:, :], first["ln_w"].partition_broadcast(P)).then_inc(ln_in, DMA)
                    c4 = first["ctxT"].rearrange("(c p) t -> p c t", p=P)
                    for c in range(DC):
                        sp.dma_start(ctx_raw[:, c, :], c4[:, c, :]).then_inc(ctx_in, DMA)
                if after is not None:
                    sp.dma_start(row[:, :], after.partition_broadcast(P)).then_inc(row_in, DMA)

            @block.vector
            def _(dve):
                if first:
                    dve.wait_ge(x_in, 4 * DMA)
                for b in range(B):
                    dve.bn_stats(stats[:, b, :], resid[:, b, :]).then_inc(stats_done, 1)
                for b in range(B):
                    dve.wait_ge(stats_done, b + 1)
                    dve.bn_aggr(moments[:, b, :], stats[:, b, :]).then_inc(moments_done, 1)

                def split(b):
                    dve.wait_ge(hi_ready, b + 1)
                    bank = core.banks[:, b % 4, :].rearrange("p (c t) -> p c t", c=DC)
                    dve.tensor_tensor(xT[1][:, :, tok(b)], bank, f32(xT[0][:, :, tok(b)]), ALU.subtract)\
                        .then_inc(lo_ready, 1)

                dve.wait_ge(rstd_ready, 1)
                if first:
                    for b in range(B):
                        dve.tensor_scalar(hidden[:, b, :], resid[:, b, :], moments[:, b, 0:1], rstd[:, b:b + 1],
                                          ALU.subtract, ALU.mult).then_inc(hidden_ready, 1)
                    dve.wait_ge(rms_ready, 1)
                    dve.wait_ge(ln_in, DMA)
                for b in range(B):
                    if b >= 2:
                        dve.wait_ge(turned, b - 1)
                    if first:
                        dve.wait_ge(hidden_ready, b + 1)
                        dve.scalar_tensor_tensor(normed[:, b % 2, :], hidden[:, b, :], rms[:, b:b + 1], ln_w[:, :],
                                                 ALU.mult, ALU.mult).then_inc(normed_ready, 1)
                    else:
                        dve.tensor_scalar(normed[:, b % 2, :], resid[:, b, :], moments[:, b, 0:1], rstd[:, b:b + 1],
                                          ALU.subtract, ALU.mult).then_inc(normed_ready, 1)
                    if b >= 1:
                        split(b - 1)
                split(B - 1)

            @block.gpsimd
            def _(pool):
                pool.memset(power[:, :], -0.5).then_inc(power_set, 1)
                pool.wait_ge(moments_done, B)
                pool.tensor_scalar(var_eps[:, :], moments[:, :, 1], EPS, None, ALU.add).then_inc(pool_steps, 1)
                pool.wait_ge(power_set, 1)
                pool.wait_ge(pool_steps, 1)
                pool.tensor_tensor(rstd[:, :], var_eps[:, :], power[:, :], ALU.pow).then_inc(rstd_ready, 1)
                if first:
                    pool.wait_ge(rstd_ready, 1)
                    pool.tensor_tensor(rms[:, :], moments[:, :, 1], rstd[:, :], ALU.mult).then_inc(pool_steps, 1)
                    pool.wait_ge(pool_steps, 2)
                    pool.tensor_tensor(rms[:, :], rms[:, :], rstd[:, :], ALU.mult).then_inc(pool_steps, 1)
                    pool.wait_ge(pool_steps, 3)
                    pool.tensor_scalar(var_eps[:, :], rms[:, :], EPS, None, ALU.add).then_inc(pool_steps, 1)
                    pool.wait_ge(pool_steps, 4)
                    pool.tensor_tensor(rms[:, :], var_eps[:, :], power[:, :], ALU.pow).then_inc(rms_ready, 1)
                    for b in range(B):
                        pool.wait_ge(hidden_ready, b + 1)
                        pool.tensor_tensor(resid[:, b, :], resid[:, b, :], hidden[:, b, :], ALU.add)\
                            .then_inc(hidden_added, 1)
                    for c in range(DC):
                        pool.wait_ge(ctx_hi, c + 1)
                        pool.tensor_tensor(cT[1][:, c, :], ctx_raw[:, c, :], f32(cT[0][:, c, :]), ALU.subtract)\
                            .then_inc(ctx_lo, 1)
                if after is not None:
                    pool.wait_ge(row_in, DMA)
                    for b in range(B):
                        pool.wait_ge(normed_ready, b + 1)
                        pool.tensor_tensor(resid[:, b, :], resid[:, b, :], row[:, :], ALU.add).then_inc(row_added, 1)

            @block.tensor
            def _(pe):
                if first:
                    pe.wait_ge(ident_in, DMA)
                for b in range(B):
                    pe.wait_ge(normed_ready, b + 1)
                    if b >= 4:
                        pe.wait_ge(lo_ready, b - 3)
                    for c in range(DC):
                        mm = pe.transpose(core.banks[:, b % 4, tok(c)], normed[:, b % 2, tok(c)], ident[:, :])
                    mm.then_inc(turned, 1)

            @block.scalar
            def _(act):
                if first:
                    for c in range(DC):
                        act.wait_ge(ctx_in, DC * DMA)
                        nc.scalar.copy(cT[0][:, c, :], ctx_raw[:, c, :]).then_inc(ctx_hi, 1)
                for b in range(B):
                    act.wait_ge(turned, b + 1)
                    bank = core.banks[:, b % 4, :].rearrange("p (c t) -> p c t", c=DC)
                    nc.scalar.copy(xT[0][:, :, tok(b)], bank).then_inc(hi_ready, 1)


PROJ_BANKS = 4
SCORE_BANK = 4
TURN_BANK = 6


def cross_attention_phase(core, io):
    nc = core.nc
    resid, xT, cT, ident, banks = core.resid, core.xT, core.cT, core.ident, core.banks
    with ExitStack() as ctx:
        sb, pair, sem = core.sb, core.pair, core.sem
        KINDS = ("A", "B", "V", "O")
        raw = {k: sb(ctx, "x_raw" + k, [P, 2 * DC * P]) for k in KINDS}
        wt = {k: pair(ctx, "x_w" + k, [P, 2 * DC * P]) for k in KINDS}
        q = pair(ctx, "x_q", [P, TOK])
        k_ = pair(ctx, "x_k", [P, TOK])
        v = pair(ctx, "x_v", [P, B, 2 * P])
        att = pair(ctx, "x_att", [P, 2, TOK])
        pT = pair(ctx, "x_pT", [P, 2, HALF])
        probs = sb(ctx, "x_probs", [P, B, P])
        bias_in = sb(ctx, "x_bias", [P, 2, P])
        biased = sb(ctx, "x_biased", [P, B, P])
        mask8 = sb(ctx, "x_mask8", [P, B, P], U8)
        mask = sb(ctx, "x_mask", [P, B, P])
        some = sb(ctx, "x_some", [P, B])
        top = sb(ctx, "x_top", [P, B])
        total = sb(ctx, "x_total", [P, B])
        inv = sb(ctx, "x_inv", [P, B])

        raw_in = {k: sem("x_raw_in" + k) for k in KINDS}
        w_hi = {k: sem("x_w_hi" + k) for k in KINDS}
        w_lo = {k: sem("x_w_lo" + k) for k in KINDS}
        bias_loaded = sem("x_bias_loaded")
        mask_in = sem("x_mask_in")
        mask_ready = sem("x_mask_ready")
        some_ready = sem("x_some_ready")
        biased_ready = sem("x_biased_ready")
        proj_ready = sem("x_proj_ready")
        proj_free = sem("x_proj_free")
        qkv_hi = sem("x_qkv_hi")
        scores_ready = sem("x_scores_ready")
        logits_ready = sem("x_logits_ready")
        top_ready = sem("x_top_ready")
        exp_done = sem("x_exp_done")
        raw_inv = sem("x_raw_inv")
        inv_ready = sem("x_inv_ready")
        probs_ready = sem("x_probs_ready")
        turned = sem("x_turned")
        pT_hi = sem("x_pT_hi")
        pT_lo = sem("x_pT_lo")
        pv_ready = sem("x_pv_ready")
        att_hi = sem("x_att_hi")
        att_lo = sem("x_att_lo")

        PER = 20

        def seq_a(g, n):
            return (PER * g - 8 if not isinstance(g, int) or g else 0) + n

        def seq_out(g, n):
            return PER * g - 4 + n if not isinstance(g, int) or g < PAIRS else PER * g - 8 + n

        def seq_v(g, n):
            return PER * g + 4 + n

        def seq_b(g, n):
            return PER * g + 8 + n

        def wqk(kind, hl, which, c):
            return wt[kind][hl][:, (which * DC + c) * P:(which * DC + c + 1) * P]

        def loop(engine, body):
            body(0, True, False)
            with engine.Fori(1, PAIRS - 1) as g:
                body(g, False, False)
            body(PAIRS - 1, False, True)

        with nc.Block() as block:
            @block.sync
            def _(sp):
                sp.dma_start(mask8[:, :, :], io["mask"].rearrange("b q k -> q b k")).then_inc(mask_in, DMA)

                def load(kind, g, first):
                    if not first:
                        sp.wait_ge(w_hi[kind], g)
                        sp.wait_ge(w_lo[kind], g)
                    src = io["w" + kind]
                    sp.dma_start(raw[kind][:, :], src[bass.ds(g, 1), :, :].rearrange("o p n -> p (o n)"))\
                        .then_inc(raw_in[kind], DMA)

                def body(g, first, last):
                    load("A", g, first)
                    if not first:
                        sp.wait_ge(biased_ready, 2 * g)
                    sp.dma_start(bias_in[:, :, :],
                                 io["bias"][bass.ds(g, 1)].rearrange("o h q k -> q (o h) k")).then_inc(bias_loaded, DMA)
                    for kind in ("V", "B", "O"):
                        load(kind, g, first)

                loop(sp, body)

            @block.tensor
            def _(pe):
                def bank_free(s):
                    if not isinstance(s, int) or s >= PROJ_BANKS:
                        pe.wait_ge(proj_free, s - PROJ_BANKS + 1)

                def qk(kind, seq, n):
                    which, half = n // 2, n % 2
                    src = xT if which == 0 else cT
                    bank_free(seq)
                    for c in range(DC):
                        mm = product(pe, banks[:, n, :], (wqk(kind, 0, which, c), wqk(kind, 1, which, c)),
                                     [s[:, c, half * HALF:(half + 1) * HALF] for s in src], c == 0, c == DC - 1)
                    mm.then_inc(proj_ready, 1)

                def values(g):
                    pe.wait_ge(w_hi["V"], g + 1)
                    pe.wait_ge(w_lo["V"], g + 1)
                    for n in range(4):
                        bank_free(seq_v(g, n))
                        for t in range(2):
                            b = 2 * n + t
                            for c in range(DC):
                                mm = product(pe, banks[:, n, t * 256:(t + 1) * 256], [s[:, c, tok(b)] for s in cT],
                                             [w[:, c * 256:(c + 1) * 256] for w in wt["V"]], c == 0, c == DC - 1)
                        mm.then_inc(proj_ready, 1)

                def scores(n, j, seq, first=False):
                    pe.wait_ge(proj_free, seq + 1)
                    if not first:
                        pe.wait_ge(top_ready, 2 * n + j - 1)
                    for i in range(HB):
                        b = HB * j + i
                        mm = product(pe, banks[:, SCORE_BANK + j, tok(i)], [s[:, tok(b)] for s in q],
                                     [s[:, tok(b)] for s in k_], True, True)
                    mm.then_inc(scores_ready, 1)

                def turn(n, j, first=False):
                    pe.wait_ge(probs_ready, 2 * n + j + 1)
                    if not first:
                        pe.wait_ge(att_lo, 2 * n + j - 1)
                    for i in range(HB):
                        mm = pe.transpose(banks[:, TURN_BANK + j, tok(i)], probs[:, HB * j + i, :], ident[:, :])
                    mm.then_inc(turned, 1)

                def pv(n, j, slot, g):
                    pe.wait_ge(pT_lo, 2 * n + j + 1)
                    pe.wait_ge(proj_free, seq_v(g, 3) + 1)
                    for i in range(HB):
                        b = HB * j + i
                        mm = product(pe, banks[:, TURN_BANK + j, tok(i)], [s[:, b, tok(slot)] for s in v],
                                     [s[:, j, tok(i)] for s in pT], True, True)
                    mm.then_inc(pv_ready, 1)

                def output(g):
                    pe.wait_ge(w_hi["O"], g)
                    pe.wait_ge(w_lo["O"], g)
                    for b in range(B):
                        if b % HB == 0:
                            pe.wait_ge(att_lo, 4 * g + b // HB - 1)
                        bank_free(seq_out(g, b))
                        for h in range(2):
                            mm = product(pe, banks[:, b % PROJ_BANKS, :], [s[:, h, tok(b)] for s in att],
                                         [w[:, h * D:(h + 1) * D] for w in wt["O"]], h == 0, h == 1)
                        mm.then_inc(proj_ready, 1)

                def body(g, first, last):
                    a, bb = 2 * g, 2 * g + 1
                    pe.wait_ge(w_hi["A"], g + 1)
                    pe.wait_ge(w_lo["A"], g + 1)
                    qk("A", seq_a(g, 0), 0)
                    qk("A", seq_a(g, 1), 1)
                    if not first:
                        turn(a - 1, 0)
                    qk("A", seq_a(g, 2), 2)
                    if not first:
                        turn(a - 1, 1)
                    qk("A", seq_a(g, 3), 3)
                    scores(a, 0, seq_a(g, 2), first)
                    if not first:
                        pv(a - 1, 0, 1, g - 1)
                    scores(a, 1, seq_a(g, 3), first)
                    if not first:
                        pv(a - 1, 1, 1, g - 1)
                        output(g)
                    values(g)
                    pe.wait_ge(w_hi["B"], g + 1)
                    pe.wait_ge(w_lo["B"], g + 1)
                    qk("B", seq_b(g, 0), 0)
                    turn(a, 0, first)
                    qk("B", seq_b(g, 1), 1)
                    turn(a, 1, first)
                    qk("B", seq_b(g, 2), 2)
                    qk("B", seq_b(g, 3), 3)
                    pv(a, 0, 0, g)
                    scores(bb, 0, seq_b(g, 2))
                    pv(a, 1, 0, g)
                    scores(bb, 1, seq_b(g, 3))

                loop(pe, body)
                tail = HEADS - 1
                turn(tail, 0)
                turn(tail, 1)
                pv(tail, 0, 1, PAIRS - 1)
                pv(tail, 1, 1, PAIRS - 1)
                output(PAIRS)

            @block.scalar
            def _(act):
                def exps(n, j):
                    act.wait_ge(top_ready, 2 * n + j + 1)
                    for i in range(HB):
                        b = HB * j + i
                        e = nc.scalar.activation(probs[:, b, :], probs[:, b, :], ACT.Exp, bias=top[:, b:b + 1],
                                                 accum_out=total[:, b:b + 1])
                    e.then_inc(exp_done, 1)

                def keep(dst, bank, seq, done):
                    act.wait_ge(proj_ready, seq + 1)
                    nc.scalar.copy(dst, banks[:, bank, :]).then_inc(done, 1)

                def qk(seq, n, head, first=False):
                    if n == 0 and not first:
                        act.wait_ge(scores_ready, 2 * head)
                    dst = (q if n < 2 else k_)[0]
                    keep(dst[:, (n % 2) * HALF:(n % 2 + 1) * HALF], n, seq, qkv_hi)

                def probs_hi(n, j, first=False):
                    act.wait_ge(turned, 2 * n + j + 1)
                    if not first:
                        act.wait_ge(pv_ready, 2 * n + j - 1)
                    nc.scalar.copy(pT[0][:, j, :], banks[:, TURN_BANK + j, :]).then_inc(pT_hi, 1)

                def attn_hi(n, j, slot):
                    act.wait_ge(pv_ready, 2 * n + j + 1)
                    nc.scalar.copy(att[0][:, slot, j * HALF:(j + 1) * HALF], banks[:, TURN_BANK + j, :])\
                        .then_inc(att_hi, 1)

                def weights(kind, g, used=None):
                    act.wait_ge(raw_in[kind], DMA * (g + 1))
                    if used is not None:
                        act.wait_ge(proj_ready, used + 1)
                    nc.scalar.copy(wt[kind][0][:, :], raw[kind][:, :]).then_inc(w_hi[kind], 1)

                def body(g, first, last):
                    a = 2 * g
                    if not first:
                        exps(a - 1, 0)
                        exps(a - 1, 1)
                    qk(seq_a(g, 0), 0, a, first)
                    qk(seq_a(g, 1), 1, a)
                    if not first:
                        probs_hi(a - 1, 0)
                    qk(seq_a(g, 2), 2, a)
                    if not first:
                        probs_hi(a - 1, 1)
                    qk(seq_a(g, 3), 3, a)
                    if not first:
                        attn_hi(a - 1, 0, 1)
                        attn_hi(a - 1, 1, 1)
                    exps(a, 0)
                    exps(a, 1)
                    if not last:
                        weights("A", g + 1, seq_a(g, 3))
                    weights("O", g, None if first else seq_out(g, 7))
                    for n in range(4):
                        if n == 0 and not first:
                            act.wait_ge(pv_ready, 4 * g)
                        keep(v[0][:, 2 * n:2 * n + 2, :].rearrange("p b f -> p (b f)"), n, seq_v(g, n), qkv_hi)
                    qk(seq_b(g, 0), 0, a + 1)
                    probs_hi(a, 0, first)
                    qk(seq_b(g, 1), 1, a + 1)
                    probs_hi(a, 1, first)
                    qk(seq_b(g, 2), 2, a + 1)
                    qk(seq_b(g, 3), 3, a + 1)
                    if not first:
                        act.wait_ge(proj_ready, seq_out(g, 7) + 1)
                    attn_hi(a, 0, 0)
                    attn_hi(a, 1, 0)
                    if not last:
                        weights("V", g + 1, seq_v(g, 3))
                        weights("B", g + 1, seq_b(g, 3))

                weights("A", 0)
                weights("V", 0)
                weights("B", 0)
                loop(act, body)
                tail = HEADS - 1
                exps(tail, 0)
                exps(tail, 1)
                probs_hi(tail, 0)
                probs_hi(tail, 1)
                attn_hi(tail, 0, 1)
                attn_hi(tail, 1, 1)

            @block.vector
            def _(dve):
                def logits(n, j):
                    dve.wait_ge(scores_ready, 2 * n + j + 1)
                    dve.wait_ge(biased_ready, n + 1)
                    if not isinstance(n, int) or n:
                        dve.wait_ge(turned, 2 * n + j - 1)
                    part = slice(HB * j, HB * (j + 1))
                    bank = banks[:, SCORE_BANK + j, :].rearrange("p (b k) -> p b k", b=HB)
                    dve.tensor_tensor(probs[:, part, :], bank, biased[:, part, :], ALU.add).then_inc(logits_ready, 1)
                    dve.wait_ge(logits_ready, 2 * n + j + 1)
                    dve.tensor_reduce(top[:, part], probs[:, part, :], AX_X, ALU.max, negate=True)\
                        .then_inc(top_ready, 1)

                def inverse(n, j):
                    dve.wait_ge(exp_done, 2 * n + j + 1)
                    part = slice(HB * j, HB * (j + 1))
                    dve.reciprocal(inv[:, part], total[:, part]).then_inc(raw_inv, 1)
                    dve.wait_ge(raw_inv, 2 * n + j + 1)
                    dve.tensor_tensor(inv[:, part], inv[:, part], some[:, part], ALU.mult).then_inc(inv_ready, 1)

                def low(dst, src, hi, done):
                    dve.tensor_tensor(dst, src, f32(hi), ALU.subtract).then_inc(done, 1)

                def keep(dst, bank, nth):
                    dve.wait_ge(qkv_hi, nth + 1)
                    low(dst[1], banks[:, bank, :], dst[0], proj_free)

                def qk(nth, n):
                    src = q if n < 2 else k_
                    keep([s[:, (n % 2) * HALF:(n % 2 + 1) * HALF] for s in src], n, nth)

                def probs_lo(n, j):
                    dve.wait_ge(pT_hi, 2 * n + j + 1)
                    low(pT[1][:, j, :], banks[:, TURN_BANK + j, :], pT[0][:, j, :], pT_lo)

                def attn_lo(n, j, slot):
                    dve.wait_ge(att_hi, 2 * n + j + 1)
                    cut = slice(j * HALF, (j + 1) * HALF)
                    low(att[1][:, slot, cut], banks[:, TURN_BANK + j, :], att[0][:, slot, cut], att_lo)

                def output(g):
                    for b in range(B):
                        dve.wait_ge(proj_ready, seq_out(g, b) + 1)
                        dve.tensor_tensor(resid[:, b, :], banks[:, b % PROJ_BANKS, :], resid[:, b, :], ALU.add)\
                            .then_inc(proj_free, 1)

                def body(g, first, last):
                    a = 2 * g
                    if not first:
                        logits(a - 1, 0)
                        logits(a - 1, 1)
                        inverse(a - 1, 0)
                    qk(12 * g, 0)
                    if not first:
                        inverse(a - 1, 1)
                    qk(12 * g + 1, 1)
                    if not first:
                        probs_lo(a - 1, 0)
                    qk(12 * g + 2, 2)
                    if not first:
                        probs_lo(a - 1, 1)
                    qk(12 * g + 3, 3)
                    logits(a, 0)
                    if not first:
                        attn_lo(a - 1, 0, 1)
                    logits(a, 1)
                    if not first:
                        attn_lo(a - 1, 1, 1)
                    inverse(a, 0)
                    inverse(a, 1)
                    if not first:
                        output(g)
                    for n in range(4):
                        keep([s[:, 2 * n:2 * n + 2, :].rearrange("p b f -> p (b f)") for s in v], n, 12 * g + 4 + n)
                    qk(12 * g + 8, 0)
                    probs_lo(a, 0)
                    qk(12 * g + 9, 1)
                    probs_lo(a, 1)
                    qk(12 * g + 10, 2)
                    qk(12 * g + 11, 3)
                    attn_lo(a, 0, 0)
                    attn_lo(a, 1, 0)

                dve.wait_ge(mask_in, DMA)
                dve.tensor_reduce(some[:, :], mask8[:, :, :], AX_X, ALU.max).then_inc(some_ready, 1)
                dve.wait_ge(some_ready, 1)
                loop(dve, body)
                tail = HEADS - 1
                logits(tail, 0)
                logits(tail, 1)
                inverse(tail, 0)
                inverse(tail, 1)
                probs_lo(tail, 0)
                probs_lo(tail, 1)
                attn_lo(tail, 0, 1)
                attn_lo(tail, 1, 1)
                output(PAIRS)

            @block.gpsimd
            def _(pool):
                def weights(kind, g):
                    pool.wait_ge(w_hi[kind], g + 1)
                    pool.tensor_tensor(wt[kind][1][:, :], raw[kind][:, :], f32(wt[kind][0][:, :]), ALU.subtract)\
                        .then_inc(w_lo[kind], 1)

                def bias(n, slot, first=False):
                    pool.wait_ge(bias_loaded, 8 * (n - slot) + DMA)
                    if not first:
                        pool.wait_ge(top_ready, 2 * n)
                    row = bias_in[:, slot, :].unsqueeze(1).to_broadcast([P, B, P])
                    pool.tensor_tensor(biased[:, :, :], mask[:, :, :], row, ALU.add).then_inc(biased_ready, 1)

                def normalise(n, j):
                    pool.wait_ge(inv_ready, 2 * n + j + 1)
                    part = slice(HB * j, HB * (j + 1))
                    rows = inv[:, part].unsqueeze(2).to_broadcast([P, HB, P])
                    pool.tensor_tensor(probs[:, part, :], probs[:, part, :], rows, ALU.mult).then_inc(probs_ready, 1)

                def body(g, first, last):
                    a = 2 * g
                    if not first:
                        normalise(a - 1, 0)
                        normalise(a - 1, 1)
                    bias(a, 0, first)
                    normalise(a, 0)
                    normalise(a, 1)
                    if not last:
                        weights("A", g + 1)
                    weights("O", g)
                    bias(a + 1, 1)
                    if not last:
                        weights("V", g + 1)
                        weights("B", g + 1)

                pool.wait_ge(mask_in, DMA)
                pool.tensor_scalar(mask[:, :, :], mask8[:, :, :], MASKED, -MASKED, ALU.mult, ALU.add)\
                    .then_inc(mask_ready, 1)
                pool.wait_ge(mask_ready, 1)
                weights("A", 0)
                weights("V", 0)
                weights("B", 0)
                loop(pool, body)
                normalise(HEADS - 1, 0)
                normalise(HEADS - 1, 1)


def ffn_phase(core, io):
    nc = core.nc
    resid, xT, banks = core.resid, core.xT, core.banks
    with ExitStack() as ctx:
        sb, pair, sem = core.sb, core.pair, core.sem
        gu_raw = sb(ctx, "f_gu_raw", [P, 2, 2 * DC * P])
        d_raw = sb(ctx, "f_d_raw", [P, 2, D])
        gu = pair(ctx, "f_gu", [P, 2, 2 * DC * P])
        dn = pair(ctx, "f_dn", [P, 2, D])
        gate = sb(ctx, "f_gate", [P, 2, TOK])
        hidden = sb(ctx, "f_hidden", [P, 2, TOK])
        hid = pair(ctx, "f_hid", [P, 2, TOK])
        bias = sb(ctx, "f_bias", [P, 2, 2])

        bias_in = [sem(f"f_bias_in{par}") for par in range(2)]
        gu_in = [sem(f"f_gu_in{par}") for par in range(2)]
        d_in = [sem(f"f_d_in{par}") for par in range(2)]
        gu_hi = sem("f_gu_hi")
        gu_lo = sem("f_gu_lo")
        d_hi = sem("f_d_hi")
        d_lo = sem("f_d_lo")
        proj_ready = sem("f_proj_ready")
        down_free = sem("f_down_free")
        gate_ready = sem("f_gate_ready")
        hidden_ready = sem("f_hidden_ready")
        hid_hi = sem("f_hid_hi")
        hid_lo = sem("f_hid_lo")

        def seq_gu(c, n):
            return (12 * c - 8 if not isinstance(c, int) or c else 0) + n

        def seq_down(c, n):
            return 12 * c + 8 + n if not isinstance(c, int) or c < FULL else 12 * c + 4 + n

        def rows(c):
            return REST if isinstance(c, int) and c == FULL else P

        def loop(engine, body):
            body(0, 0, 0)
            body(1, 1, 0)
            body(2, 0, 1)
            with engine.Fori(1, FULL // 2 - 1) as i:
                body(2 * i + 1, 1, i)
                body(2 * i + 2, 0, i + 1)
            body(FULL - 1, 1, FULL // 2 - 1)
            body(FULL, 0, FULL // 2)

        with nc.Block() as block:
            @block.sync
            def _(sp):
                def body(c, par, turn):
                    m = rows(c)
                    if not isinstance(c, int) or c >= 2:
                        sp.wait_ge(gu_hi, c - 1)
                        sp.wait_ge(gu_lo, c - 1)
                    src = io["f_gu_rest"] if m == REST else \
                        io["f_gu"][bass.ds(c, 1)].rearrange("o p n -> p (o n)")
                    sp.dma_start(gu_raw[:, par, 0:2 * DC * m], src).then_inc(gu_in[par], DMA)
                    if not isinstance(c, int) or c >= 2:
                        sp.wait_ge(d_hi, c - 1)
                        sp.wait_ge(d_lo, c - 1)
                    src = io["f_d_rest"] if m == REST else io["f_d"][bass.ds(c, 1)].rearrange("o p n -> p (o n)")
                    sp.dma_start(d_raw[0:m, par, :], src).then_inc(d_in[par], DMA)
                    if not isinstance(c, int) or c >= 2:
                        sp.wait_ge(hidden_ready, 2 * c - 2)
                    src = io["f_b_rest"] if m == REST else io["f_b"][bass.ds(c, 1)].rearrange("o p n -> p (o n)")
                    sp.dma_start(bias[0:m, par, :], src).then_inc(bias_in[par], DMA)

                loop(sp, body)

            @block.tensor
            def _(pe):
                def down(c, par, last=False):
                    m = rows(c)
                    pe.wait_ge(d_hi, c + 1)
                    pe.wait_ge(d_lo, c + 1)
                    for b in range(B):
                        if b % HB == 0:
                            pe.wait_ge(hid_lo, 2 * c + b // HB + 1)
                        if b >= PROJ_BANKS or last:
                            pe.wait_ge(down_free, B * c + b - PROJ_BANKS + 1)
                        else:
                            pe.wait_ge(hidden_ready, 2 * (c + 1) + b % 2 + 1)
                        product(pe, banks[:, b % PROJ_BANKS, :], [s[0:m, par, tok(b)] for s in hid],
                                [w[0:m, par, :] for w in dn], True, True).then_inc(proj_ready, 1)

                def body(c, par, turn):
                    m = rows(c)
                    pe.wait_ge(gu_hi, c + 1)
                    pe.wait_ge(gu_lo, c + 1)
                    for n in range(4):
                        which, half = n // 2, n % 2
                        if not isinstance(c, int) or c >= 2:
                            pe.wait_ge(down_free, B * (c - 2) + PROJ_BANKS + n + 1)
                        elif c == 1:
                            pe.wait_ge(hidden_ready, half + 1)
                        for k in range(DC):
                            at = (which * DC + k) * m
                            mm = product(pe, banks[0:m, n, :], [w[:, par, at:at + m] for w in gu],
                                         [s[:, k, half * HALF:(half + 1) * HALF] for s in xT], k == 0, k == DC - 1)
                        mm.then_inc(proj_ready, 1)
                    if not isinstance(c, int) or c:
                        down(c - 1, 1 - par)

                loop(pe, body)
                down(FULL, 0, last=True)

            @block.scalar
            def _(act):
                def weights(c, par, turn):
                    m = rows(c)
                    act.wait_ge(gu_in[par], DMA * (turn + 1))
                    if not isinstance(c, int) or c >= 2:
                        act.wait_ge(proj_ready, seq_gu(c - 2, 3) + 1)
                    nc.scalar.copy(gu[0][:, par, 0:2 * DC * m], gu_raw[:, par, 0:2 * DC * m]).then_inc(gu_hi, 1)
                    act.wait_ge(d_in[par], DMA * (turn + 1))
                    if not isinstance(c, int) or c >= 2:
                        act.wait_ge(proj_ready, seq_down(c - 2, 7) + 1)
                    nc.scalar.copy(dn[0][0:m, par, :], d_raw[0:m, par, :]).then_inc(d_hi, 1)

                def body(c, par, turn):
                    m = rows(c)
                    act.wait_ge(bias_in[par], DMA * (turn + 1))
                    for half in range(2):
                        cut = slice(half * HALF, (half + 1) * HALF)
                        act.wait_ge(proj_ready, seq_gu(c, half) + 1)
                        if not isinstance(c, int) or c >= 2:
                            act.wait_ge(hidden_ready, 2 * c - 2 + half - 1)
                        nc.scalar.activation(gate[0:m, par, cut], banks[0:m, half, :], ACT.Silu,
                                             bias=bias[0:m, par, 0:1])\
                            .then_inc(gate_ready, 1)
                    if not isinstance(c, int) or c < FULL:
                        weights(c + 1, 1 - par, turn + par)
                    for half in range(2):
                        cut = slice(half * HALF, (half + 1) * HALF)
                        act.wait_ge(hidden_ready, 2 * c + half + 1)
                        if not isinstance(c, int) or c >= 2:
                            act.wait_ge(proj_ready, seq_down(c - 2, 7) + 1)
                        nc.scalar.copy(hid[0][0:m, par, cut], hidden[0:m, par, cut]).then_inc(hid_hi, 1)

                weights(0, 0, 0)
                loop(act, body)

            @block.vector
            def _(dve):
                def down(c):
                    for b in range(B):
                        dve.wait_ge(proj_ready, seq_down(c, b) + 1)
                        dve.tensor_tensor(resid[:, b, :], banks[:, b % PROJ_BANKS, :], resid[:, b, :], ALU.add)\
                            .then_inc(down_free, 1)

                def body(c, par, turn):
                    m = rows(c)
                    dve.wait_ge(bias_in[par], DMA * (turn + 1))
                    for half in range(2):
                        cut = slice(half * HALF, (half + 1) * HALF)
                        dve.wait_ge(gate_ready, 2 * c + half + 1)
                        dve.wait_ge(proj_ready, seq_gu(c, 2 + half) + 1)
                        if not isinstance(c, int) or c >= 2:
                            dve.wait_ge(hid_lo, 2 * (c - 2) + half + 1)
                        dve.scalar_tensor_tensor(hidden[0:m, par, cut], banks[0:m, 2 + half, :], bias[0:m, par, 1:2],
                                                 gate[0:m, par, cut], ALU.add, ALU.mult).then_inc(hidden_ready, 1)
                    if not isinstance(c, int) or c:
                        down(c - 1)

                loop(dve, body)
                down(FULL)

            @block.gpsimd
            def _(pool):
                def weights(c, par):
                    m = rows(c)
                    n = 2 * DC * m
                    pool.wait_ge(gu_hi, c + 1)
                    pool.tensor_tensor(gu[1][:, par, 0:n], gu_raw[:, par, 0:n], f32(gu[0][:, par, 0:n]), ALU.subtract)\
                        .then_inc(gu_lo, 1)
                    pool.wait_ge(d_hi, c + 1)
                    pool.tensor_tensor(dn[1][0:m, par, :], d_raw[0:m, par, :], f32(dn[0][0:m, par, :]), ALU.subtract)\
                        .then_inc(d_lo, 1)

                def body(c, par, turn):
                    m = rows(c)
                    if not isinstance(c, int) or c < FULL:
                        weights(c + 1, 1 - par)
                    for half in range(2):
                        cut = slice(half * HALF, (half + 1) * HALF)
                        pool.wait_ge(hid_hi, 2 * c + half + 1)
                        pool.tensor_tensor(hid[1][0:m, par, cut], hidden[0:m, par, cut], f32(hid[0][0:m, par, cut]),
                                           ALU.subtract).then_inc(hid_lo, 1)

                weights(0, 0)
                loop(pool, body)


def grouped_attention_phase(core, io):
    nc = core.nc
    resid, xT, cT, ident, banks = core.resid, core.xT, core.cT, core.ident, core.banks
    ROUNDS = PAIRS // 4
    with ExitStack() as ctx:
        sb, pair, sem = core.sb, core.pair, core.sem
        SIZE = {"Q": 2 * DC * P, "K": DC * P, "V": 2 * DC * P, "O": 2 * D}
        raw = {k: sb(ctx, "g_raw" + k, [P, n]) for k, n in SIZE.items()}
        wt = {k: pair(ctx, "g_w" + k, [P, n]) for k, n in SIZE.items()}
        q = pair(ctx, "g_q", [P, 2, TOK])
        k_ = pair(ctx, "g_k", [P, TOK])
        v = pair(ctx, "g_v", [P, B, 2 * P])
        att = pair(ctx, "g_att", [P, 2, TOK])
        pT = pair(ctx, "g_pT", [P, 2, HALF])
        probs = sb(ctx, "g_probs", [P, B, P])
        swapped = sb(ctx, "g_swapped", [P, 2, HALF])
        turned_by = sb(ctx, "g_turned_by", [P, 2, HALF])
        cos = sb(ctx, "g_cos", [P, P])
        sin = sb(ctx, "g_sin", [P, P])
        mask8 = sb(ctx, "g_mask8", [P, P], U8)
        mask = sb(ctx, "g_mask", [P, P])
        mask_raw = sb(ctx, "g_mask_raw", [P, P])
        some = sb(ctx, "g_some", [P, 1])
        cap = sb(ctx, "g_cap", [P, 1])
        total = sb(ctx, "g_total", [P, B])
        inv = sb(ctx, "g_inv", [P, B])

        raw_in = {k: sem("g_raw_in" + k) for k in SIZE}
        w_hi = {k: sem("g_w_hi" + k) for k in SIZE}
        w_lo = {k: sem("g_w_lo" + k) for k in SIZE}
        consts_in = sem("g_consts_in")
        mask_steps = sem("g_mask_steps")
        cap_ready = sem("g_cap_ready")
        mask_ready = sem("g_mask_ready")
        proj_ready = sem("g_proj_ready")
        proj_free = sem("g_proj_free")
        v_hi = sem("g_v_hi")
        swap_done = sem("g_swap_done")
        sin_done = sem("g_sin_done")
        rope_done = sem("g_rope_done")
        qk_hi = sem("g_qk_hi")
        qk_lo = sem("g_qk_lo")
        scores_ready = sem("g_scores_ready")
        tanh_done = sem("g_tanh_done")
        logits_ready = sem("g_logits_ready")
        exp_done = sem("g_exp_done")
        sum_done = sem("g_sum_done")
        inv_ready = sem("g_inv_ready")
        probs_ready = sem("g_probs_ready")
        turned = sem("g_turned")
        pT_hi = sem("g_pT_hi")
        pT_lo = sem("g_pT_lo")
        pv_ready = sem("g_pv_ready")
        att_hi = sem("g_att_hi")
        att_lo = sem("g_att_lo")

        PER = 56
        Q_AT = (2, 18, 32, 44)
        K_AT = {0: 0, 2: 30}
        OUT_AT = (6, 22, 36, 48)
        V_AT = 14
        ROPES = 20
        ROPE_AT = (0, 6, 10, 16)

        def is_first(r, u):
            return isinstance(r, int) and r == 0 and u == 0

        def seq(r, u, at):
            if is_first(r, u) and at < OUT_AT[0]:
                return at
            return PER * r - 8 + at

        def seq_out(r, u, n):
            return PER * r - 8 + (OUT_AT[u] if not (isinstance(r, int) and r == ROUNDS) else 0) + n

        def ropes(u):
            blocks = [(K_AT[u] + h, None, h) for h in range(2)] if u in K_AT else []
            return blocks + [(Q_AT[u] + 2 * s + h, s, h) for s in range(2) for h in range(2)]

        def rope_of(r, u, slot, half):
            return ROPES * r + ROPE_AT[u] + (2 if u in K_AT else 0) + 2 * slot + half

        def dst(which, slot, half, hl):
            cut = slice(half * HALF, (half + 1) * HALF)
            return k_[hl][:, cut] if slot is None else q[hl][:, slot, cut]

        def loop(engine, body):
            for u in range(4):
                body(0, u, u == 0, False)
            with engine.Fori(1, ROUNDS - 1) as r:
                for u in range(4):
                    body(r, u, False, False)
            for u in range(4):
                body(ROUNDS - 1, u, False, u == 3)

        with nc.Block() as block:
            @block.sync
            def _(sp):
                sp.dma_start(mask8[:, :], io["g_mask"]).then_inc(consts_in, DMA)
                sp.dma_start(cos[:, :], io["g_cos"]).then_inc(consts_in, DMA)
                sp.dma_start(sin[:, :], io["g_sin"]).then_inc(consts_in, DMA)

                def load(kind, n):
                    if not isinstance(n, int) or n:
                        sp.wait_ge(w_hi[kind], n)
                        sp.wait_ge(w_lo[kind], n)
                    sp.dma_start(raw[kind][:, :], io["g_w" + kind][bass.ds(n, 1)].rearrange("o p n -> p (o n)"))\
                        .then_inc(raw_in[kind], DMA)

                def body(r, u, first, last):
                    final_round = isinstance(r, int) and r == ROUNDS - 1
                    if not last:
                        load("Q", 4 * r + u + 1)
                    if u == 0 or (u == 2 and not final_round):
                        load("K", 2 * r + u // 2 + 1)
                    if u == 1 and not final_round:
                        load("V", r + 1)
                    load("O", 4 * r + u)

                load("K", 0)
                load("Q", 0)
                load("V", 0)
                loop(sp, body)

            @block.tensor
            def _(pe):
                def bank_free(s):
                    if not isinstance(s, int) or s >= PROJ_BANKS:
                        pe.wait_ge(proj_free, s - PROJ_BANKS + 1)

                def weights_ready(kind, n):
                    pe.wait_ge(w_hi[kind], n + 1)
                    pe.wait_ge(w_lo[kind], n + 1)

                def project(s, at, kind, slot, half):
                    src = cT if kind == "K" else xT
                    bank_free(s)
                    for c in range(DC):
                        col = (slot * DC + c) * P
                        mm = product(pe, banks[:, at % PROJ_BANKS, :], [w[:, col:col + P] for w in wt[kind]],
                                     [x[:, c, half * HALF:(half + 1) * HALF] for x in src], c == 0, c == DC - 1)
                    mm.then_inc(proj_ready, 1)

                def values(r):
                    weights_ready("V", r)
                    for n in range(4):
                        s = seq(r, 0, V_AT + n)
                        bank_free(s)
                        for t in range(2):
                            for c in range(DC):
                                mm = product(pe, banks[:, (V_AT + n) % PROJ_BANKS, t * 256:(t + 1) * 256],
                                             [x[:, c, tok(2 * n + t)] for x in cT],
                                             [w[:, c * 256:(c + 1) * 256] for w in wt["V"]], c == 0, c == DC - 1)
                        mm.then_inc(proj_ready, 1)

                def scores(n, j, slot, rope, first=False):
                    pe.wait_ge(qk_lo, rope + 1)
                    if not first:
                        pe.wait_ge(tanh_done, 2 * n + j - 1)
                    for i in range(HB):
                        b = HB * j + i
                        mm = product(pe, banks[:, SCORE_BANK + j, tok(i)], [s[:, slot, tok(b)] for s in q],
                                     [s[:, tok(b)] for s in k_], True, True)
                    mm.then_inc(scores_ready, 1)

                def turn(n, j, first=False):
                    pe.wait_ge(probs_ready, 2 * n + j + 1)
                    if not first:
                        pe.wait_ge(att_lo, 2 * n + j - 1)
                    for i in range(HB):
                        mm = pe.transpose(banks[:, TURN_BANK + j, tok(i)], probs[:, HB * j + i, :], ident[:, :])
                    mm.then_inc(turned, 1)

                def pv(n, j, kv, v_seq):
                    pe.wait_ge(pT_lo, 2 * n + j + 1)
                    pe.wait_ge(proj_free, v_seq + 1)
                    for i in range(HB):
                        mm = product(pe, banks[:, TURN_BANK + j, tok(i)], [s[:, HB * j + i, tok(kv)] for s in v],
                                     [s[:, j, tok(i)] for s in pT], True, True)
                    mm.then_inc(pv_ready, 1)

                def output(r, u):
                    p = 4 * r + u
                    weights_ready("O", p - 1)
                    for b in range(B):
                        if b % HB == 0:
                            pe.wait_ge(att_lo, 4 * p + b // HB - 1)
                        s = seq_out(r, u, b)
                        bank_free(s)
                        for h in range(2):
                            mm = product(pe, banks[:, (OUT_AT[u] + b) % PROJ_BANKS, :], [x[:, h, tok(b)] for x in att],
                                         [w[:, h * D:(h + 1) * D] for w in wt["O"]], h == 0, h == 1)
                        mm.then_inc(proj_ready, 1)

                def body(r, u, first, last):
                    a = 8 * r + 2 * u
                    before_kv = (u - 1) // 2 % 2
                    before_v = seq(r, 0, V_AT + 3) - (PER if u == 0 else 0)
                    if u in K_AT:
                        weights_ready("K", 2 * r + u // 2)
                        for half in range(2):
                            project(seq(r, u, K_AT[u] + half), K_AT[u] + half, "K", 0, half)
                    weights_ready("Q", 4 * r + u)
                    for n in range(4):
                        project(seq(r, u, Q_AT[u] + n), Q_AT[u] + n, "Q", n // 2, n % 2)
                        if n >= 2 and not first:
                            turn(a - 1, n - 2)
                    for half in range(2):
                        scores(a, half, 0, rope_of(r, u, 0, half), first)
                        if not first:
                            pv(a - 1, half, before_kv, before_v)
                    if not first:
                        output(r, u)
                    if u == 0:
                        values(r)
                    turn(a, 0, first)
                    turn(a, 1, first)
                    for half in range(2):
                        scores(a + 1, half, 1, rope_of(r, u, 1, half))
                        pv(a, half, u // 2, seq(r, 0, V_AT + 3))

                loop(pe, body)
                tail = HEADS - 1
                for half in range(2):
                    turn(tail, half)
                for half in range(2):
                    pv(tail, half, 1, seq(ROUNDS - 1, 0, V_AT + 3))
                output(ROUNDS, 0)

            @block.scalar
            def _(act):
                def part(j):
                    return probs[:, HB * j:HB * (j + 1), :].rearrange("p b k -> p (b k)")

                def tanhs(n, j):
                    act.wait_ge(scores_ready, 2 * n + j + 1)
                    nc.scalar.activation(part(j), banks[:, SCORE_BANK + j, :], ACT.Tanh,
                                         scale=ATTN_MULT / LOGIT_CAP).then_inc(tanh_done, 1)

                def exps(n, j):
                    act.wait_ge(logits_ready, 2 * n + j + 1)
                    nc.scalar.activation(part(j), part(j), ACT.Exp).then_inc(exp_done, 1)

                def swap(s, at, nth, first):
                    act.wait_ge(proj_ready, s + 1)
                    if not (isinstance(nth, int) and nth < 2):
                        act.wait_ge(rope_done, nth - 1)
                    h = P // 2
                    nc.scalar.copy(swapped[0:h, nth_par(at), :], banks[h:P, at[0] % PROJ_BANKS, :])
                    nc.scalar.copy(swapped[h:P, nth_par(at), :], banks[0:h, at[0] % PROJ_BANKS, :])\
                        .then_inc(swap_done, 1)

                def nth_par(at):
                    return at[1] % 2

                def rotated_hi(block, nth, at):
                    act.wait_ge(rope_done, nth + 1)
                    nc.scalar.copy(dst(None, block[1], block[2], 0), turned_by[:, nth_par(at), :]).then_inc(qk_hi, 1)

                def probs_hi(n, j, first=False):
                    act.wait_ge(turned, 2 * n + j + 1)
                    if not first:
                        act.wait_ge(pv_ready, 2 * n + j - 1)
                    nc.scalar.copy(pT[0][:, j, :], banks[:, TURN_BANK + j, :]).then_inc(pT_hi, 1)

                def attn_hi(n, j, slot):
                    act.wait_ge(pv_ready, 2 * n + j + 1)
                    nc.scalar.copy(att[0][:, slot, j * HALF:(j + 1) * HALF], banks[:, TURN_BANK + j, :])\
                        .then_inc(att_hi, 1)

                def weights(kind, n, used=None):
                    act.wait_ge(raw_in[kind], DMA * (n + 1))
                    if used is not None:
                        act.wait_ge(proj_ready, used + 1)
                    nc.scalar.copy(wt[kind][0][:, :], raw[kind][:, :]).then_inc(w_hi[kind], 1)

                def body(r, u, first, last):
                    a = 8 * r + 2 * u
                    final_round = isinstance(r, int) and r == ROUNDS - 1
                    blocks = ropes(u)
                    at = [(blk[0], ROPE_AT[u] + i) for i, blk in enumerate(blocks)]
                    nth = [ROPES * r + x[1] for x in at]
                    if not first:
                        tanhs(a - 1, 0)
                        tanhs(a - 1, 1)
                    for i, blk in enumerate(blocks):
                        swap(seq(r, u, blk[0]), at[i], nth[i], first)
                        if i == 0 and not first:
                            exps(a - 1, 0)
                            exps(a - 1, 1)
                            act.wait_ge(scores_ready, 4 * (4 * r + u))
                        if i:
                            rotated_hi(blocks[i - 1], nth[i - 1], at[i - 1])
                        if i == len(blocks) - 2 and not first:
                            probs_hi(a - 1, 0)
                    rotated_hi(blocks[-1], nth[-1], at[-1])
                    if not first:
                        probs_hi(a - 1, 1)
                    tanhs(a, 0)
                    if not first:
                        attn_hi(a - 1, 0, 1)
                    tanhs(a, 1)
                    if not first:
                        attn_hi(a - 1, 1, 1)
                    exps(a, 0)
                    exps(a, 1)
                    if not last:
                        weights("Q", 4 * r + u + 1, seq(r, u, Q_AT[u] + 3))
                    if u == 0 or (u == 2 and not final_round):
                        weights("K", 2 * r + u // 2 + 1, seq(r, u, K_AT[u] + 1))
                    if u == 1 and not final_round:
                        weights("V", r + 1, seq(r, 0, V_AT + 3))
                    weights("O", 4 * r + u, None if first else seq_out(r, u, 7))
                    if u == 0:
                        for n in range(4):
                            act.wait_ge(proj_ready, seq(r, 0, V_AT + n) + 1)
                            nc.scalar.copy(v[0][:, 2 * n:2 * n + 2, :].rearrange("p b f -> p (b f)"),
                                           banks[:, (V_AT + n) % PROJ_BANKS, :]).then_inc(v_hi, 1)
                    probs_hi(a, 0, first)
                    probs_hi(a, 1, first)
                    attn_hi(a, 0, 0)
                    attn_hi(a, 1, 0)

                weights("K", 0)
                weights("Q", 0)
                weights("V", 0)
                loop(act, body)
                tail = HEADS - 1
                for step in (tanhs, exps, probs_hi):
                    step(tail, 0)
                    step(tail, 1)
                attn_hi(tail, 0, 1)
                attn_hi(tail, 1, 1)

            @block.vector
            def _(dve):
                def wide(table):
                    return table[:, :].unsqueeze(1).to_broadcast([P, HB, P])

                def logits(n, j):
                    dve.wait_ge(tanh_done, 2 * n + j + 1)
                    part = probs[:, HB * j:HB * (j + 1), :]
                    dve.scalar_tensor_tensor(part, part, cap[:, 0:1], wide(mask), ALU.mult, ALU.add)\
                        .then_inc(logits_ready, 1)

                def inverse(n, j):
                    dve.wait_ge(exp_done, 2 * n + j + 1)
                    part = slice(HB * j, HB * (j + 1))
                    dve.tensor_reduce(total[:, part], probs[:, part, :], AX_X, ALU.add).then_inc(sum_done, 1)
                    dve.wait_ge(sum_done, 2 * n + j + 1)
                    dve.reciprocal(inv[:, part], total[:, part]).then_inc(inv_ready, 1)

                def rotate_cos(at, par, nth):
                    dve.wait_ge(swap_done, nth + 1)
                    if not (isinstance(nth, int) and nth < 2):
                        dve.wait_ge(qk_lo, nth - 1)
                    bank = banks[:, at % PROJ_BANKS, :].rearrange("p (b t) -> p b t", b=HB)
                    out = turned_by[:, par, :].rearrange("p (b t) -> p b t", b=HB)
                    dve.tensor_tensor(out, bank, wide(cos), ALU.mult).then_inc(proj_free, 1)

                def rotate_add(s, par, nth):
                    dve.wait_ge(sin_done, nth + 1)
                    dve.wait_ge(proj_free, s + 1)
                    dve.tensor_tensor(turned_by[:, par, :], turned_by[:, par, :], swapped[:, par, :], ALU.add)\
                        .then_inc(rope_done, 1)

                def low(out, src, hi, done):
                    dve.tensor_tensor(out, src, f32(hi), ALU.subtract).then_inc(done, 1)

                def probs_lo(n, j):
                    dve.wait_ge(pT_hi, 2 * n + j + 1)
                    low(pT[1][:, j, :], banks[:, TURN_BANK + j, :], pT[0][:, j, :], pT_lo)

                def attn_lo(n, j, slot):
                    dve.wait_ge(att_hi, 2 * n + j + 1)
                    cut = slice(j * HALF, (j + 1) * HALF)
                    low(att[1][:, slot, cut], banks[:, TURN_BANK + j, :], att[0][:, slot, cut], att_lo)

                def output(r, u):
                    for b in range(B):
                        dve.wait_ge(proj_ready, seq_out(r, u, b) + 1)
                        dve.tensor_tensor(resid[:, b, :], banks[:, (OUT_AT[u] + b) % PROJ_BANKS, :], resid[:, b, :],
                                          ALU.add).then_inc(proj_free, 1)

                def body(r, u, first, last):
                    a = 8 * r + 2 * u
                    blocks = ropes(u)
                    if not first:
                        logits(a - 1, 0)
                        logits(a - 1, 1)
                    for i, blk in enumerate(blocks):
                        at = ROPE_AT[u] + i
                        rotate_cos(blk[0], at % 2, ROPES * r + at)
                        if i < 2 and not first:
                            inverse(a - 1, i)
                        if i:
                            rotate_add(seq(r, u, blocks[i - 1][0]), (at - 1) % 2, ROPES * r + at - 1)
                        if i == len(blocks) - 2 and not first:
                            probs_lo(a - 1, 0)
                    at = ROPE_AT[u] + len(blocks) - 1
                    rotate_add(seq(r, u, blocks[-1][0]), at % 2, ROPES * r + at)
                    if not first:
                        probs_lo(a - 1, 1)
                    logits(a, 0)
                    if not first:
                        attn_lo(a - 1, 0, 1)
                    logits(a, 1)
                    if not first:
                        attn_lo(a - 1, 1, 1)
                    inverse(a, 0)
                    inverse(a, 1)
                    if not first:
                        output(r, u)
                    if u == 0:
                        for n in range(4):
                            dve.wait_ge(v_hi, 4 * r + n + 1)
                            cut = [s[:, 2 * n:2 * n + 2, :].rearrange("p b f -> p (b f)") for s in v]
                            low(cut[1], banks[:, (V_AT + n) % PROJ_BANKS, :], cut[0], proj_free)
                    probs_lo(a, 0)
                    probs_lo(a, 1)
                    attn_lo(a, 0, 0)
                    attn_lo(a, 1, 0)

                dve.wait_ge(consts_in, 3 * DMA)
                dve.tensor_reduce(some[:, :], mask8[:, :], AX_X, ALU.max).then_inc(mask_steps, 1)
                dve.tensor_scalar(mask_raw[:, :], mask8[:, :], MASKED, -MASKED, ALU.mult, ALU.add).then_inc(mask_steps, 1)
                dve.wait_ge(mask_steps, 2)
                dve.tensor_scalar(cap[:, :], some[:, :], LOGIT_CAP, None, ALU.mult).then_inc(cap_ready, 1)
                dve.tensor_scalar(mask[:, :], mask_raw[:, :], some[:, 0:1], None, ALU.mult).then_inc(mask_ready, 1)
                dve.wait_ge(cap_ready, 1)
                dve.wait_ge(mask_ready, 1)
                loop(dve, body)
                tail = HEADS - 1
                for step in (logits, inverse, probs_lo):
                    step(tail, 0)
                    step(tail, 1)
                attn_lo(tail, 0, 1)
                attn_lo(tail, 1, 1)
                output(ROUNDS, 0)

            @block.gpsimd
            def _(pool):
                def weights(kind, n):
                    pool.wait_ge(w_hi[kind], n + 1)
                    pool.tensor_tensor(wt[kind][1][:, :], raw[kind][:, :], f32(wt[kind][0][:, :]), ALU.subtract)\
                        .then_inc(w_lo[kind], 1)

                def normalise(n, j):
                    pool.wait_ge(inv_ready, 2 * n + j + 1)
                    part = slice(HB * j, HB * (j + 1))
                    rows = inv[:, part].unsqueeze(2).to_broadcast([P, HB, P])
                    pool.tensor_tensor(probs[:, part, :], probs[:, part, :], rows, ALU.mult).then_inc(probs_ready, 1)

                def rotate_sin(par, nth):
                    pool.wait_ge(swap_done, nth + 1)
                    part = swapped[:, par, :].rearrange("p (b t) -> p b t", b=HB)
                    pool.tensor_tensor(part, part, sin[:, :].unsqueeze(1).to_broadcast([P, HB, P]), ALU.mult)\
                        .then_inc(sin_done, 1)

                def rotated_lo(blk, par, nth):
                    pool.wait_ge(qk_hi, nth + 1)
                    pool.tensor_tensor(dst(None, blk[1], blk[2], 1), turned_by[:, par, :],
                                       f32(dst(None, blk[1], blk[2], 0)), ALU.subtract).then_inc(qk_lo, 1)

                def body(r, u, first, last):
                    a = 8 * r + 2 * u
                    final_round = isinstance(r, int) and r == ROUNDS - 1
                    blocks = ropes(u)
                    for i, blk in enumerate(blocks):
                        at = ROPE_AT[u] + i
                        rotate_sin(at % 2, ROPES * r + at)
                        if i < 2 and not first:
                            normalise(a - 1, i)
                        if i:
                            rotated_lo(blocks[i - 1], (at - 1) % 2, ROPES * r + at - 1)
                    at = ROPE_AT[u] + len(blocks) - 1
                    rotated_lo(blocks[-1], at % 2, ROPES * r + at)
                    normalise(a, 0)
                    normalise(a, 1)
                    if not last:
                        weights("Q", 4 * r + u + 1)
                    if u == 0 or (u == 2 and not final_round):
                        weights("K", 2 * r + u // 2 + 1)
                    if u == 1 and not final_round:
                        weights("V", r + 1)
                    weights("O", 4 * r + u)

                pool.wait_ge(consts_in, 3 * DMA)
                weights("K", 0)
                weights("Q", 0)
                weights("V", 0)
                loop(pool, body)
                normalise(HEADS - 1, 0)
                normalise(HEADS - 1, 1)


def lora_phase(core, io, out):
    nc = core.nc
    resid, xT, banks = core.resid, core.xT, core.banks
    with ExitStack() as ctx:
        sb, pair, sem = core.sb, core.pair, core.sem
        a_raw = sb(ctx, "l_a_raw", [P, D])
        b_raw = sb(ctx, "l_b_raw", [P, D])
        b_scaled = sb(ctx, "l_b_scaled", [P, D])
        coef = sb(ctx, "l_coef", [P, 1])
        a2 = pair(ctx, "l_a", [P, D])
        b2 = pair(ctx, "l_b", [P, D])
        w_raw = sb(ctx, "l_w_raw", [P, DC, D])
        w = pair(ctx, "l_w", [P, DC, D])

        coef_in = sem("l_coef_in")
        ab_in = sem("l_ab_in")
        w_in = sem("l_w_in")
        b_ready = sem("l_b_ready")
        ab_hi = sem("l_ab_hi")
        ab_lo = sem("l_ab_lo")
        folded = sem("l_folded")
        w_sum = sem("l_w_sum")
        w_hi = sem("l_w_hi")
        w_lo = sem("l_w_lo")
        out_ready = sem("l_out_ready")
        added = sem("l_added")
        stored = sem("l_stored")

        with nc.Block() as block:
            @block.sync
            def _(sp):
                sp.dma_start(a_raw[:, :], io["l_a"]).then_inc(ab_in, DMA)
                sp.dma_start(b_raw[:, :], io["l_b"]).then_inc(ab_in, DMA)
                for n in range(LORA // RANK):
                    sp.dma_start(coef[n * RANK:(n + 1) * RANK, :], io["l_coef"][n:n + 1].partition_broadcast(RANK))\
                        .then_inc(coef_in, DMA)
                sp.dma_start(w_raw[:, :, :], io["l_w"].rearrange("(c p) o -> p c o", p=P)).then_inc(w_in, DMA)
                for b in range(B):
                    sp.wait_ge(added, b + 1)
                    sp.dma_start(out[b, :, :], resid[:, b, :]).then_inc(stored, DMA)
                sp.wait_ge(stored, B * DMA)

            @block.tensor
            def _(pe):
                pe.wait_ge(ab_lo, 2)
                for c in range(DC):
                    product(pe, banks[:, c, :], [s[:, tok(c)] for s in a2], [s[:, :] for s in b2], True, True)\
                        .then_inc(folded, 1)
                for b in range(B):
                    if b >= 4:
                        pe.wait_ge(added, b - 3)
                    for c in range(DC):
                        if b == 0:
                            pe.wait_ge(w_lo, c + 1)
                        mm = product(pe, banks[:, 4 + b % 4, :], [s[:, c, tok(b)] for s in xT],
                                     [s[:, c, :] for s in w], c == 0, c == DC - 1)
                    mm.then_inc(out_ready, 1)

            @block.scalar
            def _(act):
                act.wait_ge(ab_in, 2 * DMA)
                nc.scalar.copy(a2[0][:, :], a_raw[:, :]).then_inc(ab_hi, 1)
                act.wait_ge(b_ready, 1)
                nc.scalar.copy(b2[0][:, :], b_scaled[:, :]).then_inc(ab_hi, 1)
                for c in range(DC):
                    act.wait_ge(w_sum, c + 1)
                    nc.scalar.copy(w[0][:, c, :], w_raw[:, c, :]).then_inc(w_hi, 1)

            @block.vector
            def _(dve):
                dve.wait_ge(ab_in, 2 * DMA)
                dve.wait_ge(coef_in, LORA // RANK * DMA)
                dve.tensor_scalar(b_scaled[:, :], b_raw[:, :], coef[:, 0:1], LORA_SCALE, ALU.mult, ALU.mult)\
                    .then_inc(b_ready, 1)
                for n, (src, dst) in enumerate(((a_raw, a2), (b_scaled, b2))):
                    dve.wait_ge(ab_hi, n + 1)
                    dve.tensor_tensor(dst[1][:, :], src[:, :], f32(dst[0][:, :]), ALU.subtract).then_inc(ab_lo, 1)
                dve.wait_ge(w_in, DMA)
                for c in range(DC):
                    dve.wait_ge(folded, c + 1)
                    dve.tensor_tensor(w_raw[:, c, :], banks[:, c, :], w_raw[:, c, :], ALU.add).then_inc(w_sum, 1)
                for c in range(DC):
                    dve.wait_ge(w_hi, c + 1)
                    dve.tensor_tensor(w[1][:, c, :], w_raw[:, c, :], f32(w[0][:, c, :]), ALU.subtract)\
                        .then_inc(w_lo, 1)
                for b in range(B):
                    dve.wait_ge(out_ready, b + 1)
                    dve.tensor_tensor(resid[:, b, :], banks[:, 4 + b % 4, :], resid[:, b, :], ALU.add)\
                        .then_inc(added, 1)


def store_phase(core, out):
    nc = core.nc
    stored = core.sem("stored")
    with nc.Block() as block:
        @block.sync
        def _(sp):
            sp.dma_start(out.rearrange("b p d -> p b d"), core.resid[:, :, :]).then_inc(stored, DMA)
            sp.wait_ge(stored, DMA)


def build(nc, io, out, STAGES=9):
    with ExitStack() as ctx:
        core = Core(nc, ctx)
        normalise_phase(core, "n0", first={"x": io["x"], "ident": io["ident"], "ln_w": io["x_ln_w"], "ctxT": io["ctxT"]})
        if STAGES >= 1:
            cross_attention_phase(core, {"mask": io["x_mask"], "bias": io["x_bias"], "wA": io["x_wA"], "wB": io["x_wB"],
                                         "wV": io["x_wV"], "wO": io["x_wO"]})
        if STAGES >= 2:
            normalise_phase(core, "n1", after=io["f_b_down"])
            ffn_phase(core, io)
        if STAGES >= 3:
            normalise_phase(core, "n2")
            grouped_attention_phase(core, io)
        if STAGES >= 4:
            normalise_phase(core, "n3", after=io["l_bias"])
            lora_phase(core, io, out)
        else:
            store_phase(core, out)


def head_weights(w):
    return w.reshape(DC, P, -1, P).transpose(2, 1, 0, 3)


def pair_columns(w):
    return w.reshape(DC, P, -1, 2 * P).transpose(2, 1, 0, 3).reshape(-1, P, DC * 2 * P)


def pair_rows(w):
    return w.reshape(-1, 2, P, D).transpose(0, 2, 1, 3).reshape(-1, P, 2 * D)


def lay_out(a):
    q = head_weights(a["L0_xattn_w_q"].T)
    k = head_weights(a["L0_xattn_w_k"].T)
    qk = np.stack([q, k], 2).reshape(HEADS, P, 2 * DC * P)
    io = {
        "x": a["x"],
        "ctxT": a["ctx_4096"].reshape(TOK, D).T,
        "ident": np.eye(P, dtype=np.float32),
        "x_ln_w": a["L0_xattn_ln_weight"],
        "x_mask": a["mask_BxSxS2_bk0"],
        "x_bias": a["L0_xattn_position_bias"].reshape(PAIRS, 2, P, P),
        "x_wA": qk[0::2],
        "x_wB": qk[1::2],
        "x_wV": pair_columns(a["L0_xattn_w_v"].T),
        "x_wO": pair_rows(a["L0_xattn_w_out"].T),
    }
    io.update(lay_out_more(a))
    return {n: np.ascontiguousarray(v) for n, v in io.items()}


def lay_out_more(a):
    gate, up, down = (a["L0_ffn_w_" + n].T for n in ("gate", "up", "down"))
    full = FULL * P
    gu = np.stack([head_weights(gate[:, :full]), head_weights(up[:, :full])], 2)
    rest = np.stack([m[:, full:].reshape(DC, P, REST).transpose(1, 0, 2) for m in (gate, up)], 1)
    biases = np.stack([a["L0_ffn_b_gate"], a["L0_ffn_b_up"]], 1)
    inv_freq = np.float32(1.0) / np.float32(10000.0) ** (np.arange(0, P, 2, dtype=np.float32) / np.float32(P))
    phase = np.tile(np.arange(P, dtype=np.float32)[:, None] * inv_freq[None, :], (1, 2)).T
    sign = np.where(np.arange(P) < P // 2, -1, 1).astype(np.float32)[:, None]
    return {
        "f_gu": gu.reshape(FULL, P, 2 * DC * P),
        "f_gu_rest": rest.reshape(P, 2 * DC * REST),
        "f_d": down[:full].reshape(FULL, P, D),
        "f_d_rest": down[full:],
        "f_b": biases[:full].reshape(FULL, P, 2),
        "f_b_rest": biases[full:],
        "f_b_down": a["L0_ffn_b_down"],
        "g_mask": a["mask_1x1xSxS2_bk0"].reshape(P, P),
        "g_cos": np.cos(phase),
        "g_sin": np.sin(phase) * sign,
        "g_wQ": head_weights(a["L1_xattn_Wq"]).reshape(PAIRS, 2, P, DC * P).transpose(0, 2, 1, 3)
        .reshape(PAIRS, P, 2 * DC * P),
        "g_wK": head_weights(a["L1_xattn_Wk"]).reshape(KV_HEADS, P, DC * P),
        "g_wV": pair_columns(a["L1_xattn_Wv"]),
        "g_wO": pair_rows(a["L1_xattn_Wo"]),
        "l_a": a["L1_ffn_lora_A"].reshape(LORA, D),
        "l_b": a["L1_ffn_lora_B"].transpose(0, 2, 1).reshape(LORA, D),
        "l_coef": a["L1_ffn_lora_weights"],
        "l_w": a["L1_ffn_W"].T,
        "l_bias": a["L1_ffn_bias"],
    }


def kernel(**inputs):
    import concourse.bacc as bacc
    from concourse.bass_utils import run_bass_kernel_spmd

    arrays = lay_out({n: np.asarray(v) for n, v in inputs.items()})
    nc = bacc.Bacc("TRN2", target_bir_lowering=False, num_devices=1)
    io = {n: nc.dram_tensor("in_" + n, v.shape, mybir.dt.from_np(v.dtype), kind="ExternalInput").ap()
          for n, v in arrays.items()}
    out = nc.dram_tensor("out", (B, P, D), F32, kind="ExternalOutput").ap()
    build(nc, io, out)
    run = run_bass_kernel_spmd(nc, [{"in_" + n: v for n, v in arrays.items()}], core_ids=[0])
    return np.asarray(run.results[0]["out"])
```

```python
from contextlib import ExitStack

import numpy as np
import concourse.bass as bass
from concourse import mybir

F32 = mybir.dt.float32
F32R = mybir.dt.float32r
U8 = mybir.dt.uint8
ALU = mybir.AluOpType
ACT = mybir.ActivationFunctionType
AX_X = mybir.AxisListType.X

P = 128
B = 8
D = 512
DC = D // P
TOK = B * P
HALF = TOK // 2
HB = B // 2
HEADS = 32
KV_HEADS = 8
PAIRS = HEADS // 2
INTER = 1376
FULL = INTER // P
REST = INTER - FULL * P
LORA = 128
RANK = 16
LORA_SCALE = 2.0
EPS = 1e-5
MASKED = 1e30
LOGIT_CAP = 30.0
ATTN_MULT = 0.08838834764831845
DMA = 16


def f32(ap):
    return ap.bitcast(F32)


def product(pe, out, w, x, start, stop):
    pe.matmul(out, w[1], x[0], start=start, stop=False)
    pe.matmul(out, w[0], x[1], start=False, stop=False)
    return pe.matmul(out, w[0], x[0], start=False, stop=stop)


def tok(b, n=1):
    return slice(b * P, (b + n) * P)


class Core:

    def __init__(self, nc, ctx):
        self.nc, self.ctx, self.n_sems = nc, ctx, 0
        self.banks = ctx.enter_context(nc.psum_tensor("banks", [P, 8, 512], F32))
        self.resid = self.sb(ctx, "resid", [P, B, D], F32)
        self.xT = self.pair(ctx, "xT", [P, DC, TOK])
        self.cT = self.pair(ctx, "cT", [P, DC, TOK])
        self.ident = self.sb(ctx, "ident", [P, P], F32)

    def sb(self, ctx, name, shape, dt=F32):
        return ctx.enter_context(self.nc.sbuf_tensor(name, shape, dt))

    def pair(self, ctx, name, shape):
        return (self.sb(ctx, name + "_hi", shape, F32R), self.sb(ctx, name + "_lo", shape, F32R))

    def sem(self, name):
        return self.ctx.enter_context(self.nc.semaphore(name))


def normalise_phase(core, tag, after=None, first=None):
    nc = core.nc
    resid, xT, cT, ident = core.resid, core.xT, core.cT, core.ident
    with ExitStack() as ctx:
        stats = core.sb(ctx, tag + "_stats", [P, B, 6])
        moments = core.sb(ctx, tag + "_moments", [P, B, 2])
        var_eps = core.sb(ctx, tag + "_var_eps", [P, B])
        rstd = core.sb(ctx, tag + "_rstd", [P, B])
        power = core.sb(ctx, tag + "_power", [P, B])
        normed = core.sb(ctx, tag + "_normed", [P, 2, D])
        row = core.sb(ctx, tag + "_row", [P, D]) if after is not None else None

        stats_done = core.sem(tag + "_stats_done")
        moments_done = core.sem(tag + "_moments_done")
        power_set = core.sem(tag + "_power_set")
        pool_steps = core.sem(tag + "_pool_steps")
        rstd_ready = core.sem(tag + "_rstd_ready")
        normed_ready = core.sem(tag + "_normed_ready")
        turned = core.sem(tag + "_turned")
        hi_ready = core.sem(tag + "_hi_ready")
        lo_ready = core.sem(tag + "_lo_ready")
        row_in = core.sem(tag + "_row_in")
        row_added = core.sem(tag + "_row_added")
        if first:
            x_in = core.sem(tag + "_x_in")
            ident_in = core.sem(tag + "_ident_in")
            ln_in = core.sem(tag + "_ln_in")
            ctx_in = core.sem(tag + "_ctx_in")
            ctx_hi = core.sem(tag + "_ctx_hi")
            ctx_lo = core.sem(tag + "_ctx_lo")
            hidden_ready = core.sem(tag + "_hidden_ready")
            hidden_added = core.sem(tag + "_hidden_added")
            rms_ready = core.sem(tag + "_rms_ready")
            hidden = core.sb(ctx, tag + "_hidden", [P, B, D])
            ln_w = core.sb(ctx, tag + "_ln_w", [P, D])
            rms = core.sb(ctx, tag + "_rms", [P, B])
            ctx_raw = core.sb(ctx, tag + "_ctx_raw", [P, DC, TOK])

        with nc.Block() as block:
            @block.sync
            def _(sp):
                if first:
                    x4 = first["x"].rearrange("b p d -> p b d")
                    for q in range(4):
                        sp.dma_start(resid[:, 2 * q:2 * q + 2, :], x4[:, 2 * q:2 * q + 2, :]).then_inc(x_in, DMA)
                    sp.dma_start(ident[:, :], first["ident"]).then_inc(ident_in, DMA)
                    sp.dma_start(ln_w[:, :], first["ln_w"].partition_broadcast(P)).then_inc(ln_in, DMA)
                    c4 = first["ctxT"].rearrange("(c p) t -> p c t", p=P)
                    for c in range(DC):
                        sp.dma_start(ctx_raw[:, c, :], c4[:, c, :]).then_inc(ctx_in, DMA)
                if after is not None:
                    sp.dma_start(row[:, :], after.partition_broadcast(P)).then_inc(row_in, DMA)

            @block.vector
            def _(dve):
                if first:
                    dve.wait_ge(x_in, 4 * DMA)
                for b in range(B):
                    dve.bn_stats(stats[:, b, :], resid[:, b, :]).then_inc(stats_done, 1)
                for b in range(B):
                    dve.wait_ge(stats_done, b + 1)
                    dve.bn_aggr(moments[:, b, :], stats[:, b, :]).then_inc(moments_done, 1)

                def split(b):
                    dve.wait_ge(hi_ready, b + 1)
                    bank = core.banks[:, b % 4, :].rearrange("p (c t) -> p c t", c=DC)
                    dve.tensor_tensor(xT[1][:, :, tok(b)], bank, f32(xT[0][:, :, tok(b)]), ALU.subtract)\
                        .then_inc(lo_ready, 1)

                dve.wait_ge(rstd_ready, 1)
                if first:
                    for b in range(B):
                        dve.tensor_scalar(hidden[:, b, :], resid[:, b, :], moments[:, b, 0:1], rstd[:, b:b + 1],
                                          ALU.subtract, ALU.mult).then_inc(hidden_ready, 1)
                    dve.wait_ge(rms_ready, 1)
                    dve.wait_ge(ln_in, DMA)
                for b in range(B):
                    if b >= 2:
                        dve.wait_ge(turned, b - 1)
                    if first:
                        dve.wait_ge(hidden_ready, b + 1)
                        dve.scalar_tensor_tensor(normed[:, b % 2, :], hidden[:, b, :], rms[:, b:b + 1], ln_w[:, :],
                                                 ALU.mult, ALU.mult).then_inc(normed_ready, 1)
                    else:
                        dve.tensor_scalar(normed[:, b % 2, :], resid[:, b, :], moments[:, b, 0:1], rstd[:, b:b + 1],
                                          ALU.subtract, ALU.mult).then_inc(normed_ready, 1)
                    if b >= 1:
                        split(b - 1)
                split(B - 1)

            @block.gpsimd
            def _(pool):
                pool.memset(power[:, :], -0.5).then_inc(power_set, 1)
                pool.wait_ge(moments_done, B)
                pool.tensor_scalar(var_eps[:, :], moments[:, :, 1], EPS, None, ALU.add).then_inc(pool_steps, 1)
                pool.wait_ge(power_set, 1)
                pool.wait_ge(pool_steps, 1)
                pool.tensor_tensor(rstd[:, :], var_eps[:, :], power[:, :], ALU.pow).then_inc(rstd_ready, 1)
                if first:
                    pool.wait_ge(rstd_ready, 1)
                    pool.tensor_tensor(rms[:, :], moments[:, :, 1], rstd[:, :], ALU.mult).then_inc(pool_steps, 1)
                    pool.wait_ge(pool_steps, 2)
                    pool.tensor_tensor(rms[:, :], rms[:, :], rstd[:, :], ALU.mult).then_inc(pool_steps, 1)
                    pool.wait_ge(pool_steps, 3)
                    pool.tensor_scalar(var_eps[:, :], rms[:, :], EPS, None, ALU.add).then_inc(pool_steps, 1)
                    pool.wait_ge(pool_steps, 4)
                    pool.tensor_tensor(rms[:, :], var_eps[:, :], power[:, :], ALU.pow).then_inc(rms_ready, 1)
                    for b in range(B):
                        pool.wait_ge(hidden_ready, b + 1)
                        pool.tensor_tensor(resid[:, b, :], resid[:, b, :], hidden[:, b, :], ALU.add)\
                            .then_inc(hidden_added, 1)
                    for c in range(DC):
                        pool.wait_ge(ctx_hi, c + 1)
                        pool.tensor_tensor(cT[1][:, c, :], ctx_raw[:, c, :], f32(cT[0][:, c, :]), ALU.subtract)\
                            .then_inc(ctx_lo, 1)
                if after is not None:
                    pool.wait_ge(row_in, DMA)
                    for b in range(B):
                        pool.wait_ge(normed_ready, b + 1)
                        pool.tensor_tensor(resid[:, b, :], resid[:, b, :], row[:, :], ALU.add).then_inc(row_added, 1)

            @block.tensor
            def _(pe):
                if first:
                    pe.wait_ge(ident_in, DMA)
                for b in range(B):
                    pe.wait_ge(normed_ready, b + 1)
                    if b >= 4:
                        pe.wait_ge(lo_ready, b - 3)
                    for c in range(DC):
                        mm = pe.transpose(core.banks[:, b % 4, tok(c)], normed[:, b % 2, tok(c)], ident[:, :])
                    mm.then_inc(turned, 1)

            @block.scalar
            def _(act):
                if first:
                    for c in range(DC):
                        act.wait_ge(ctx_in, DC * DMA)
                        nc.scalar.copy(cT[0][:, c, :], ctx_raw[:, c, :]).then_inc(ctx_hi, 1)
                for b in range(B):
                    act.wait_ge(turned, b + 1)
                    bank = core.banks[:, b % 4, :].rearrange("p (c t) -> p c t", c=DC)
                    nc.scalar.copy(xT[0][:, :, tok(b)], bank).then_inc(hi_ready, 1)


PROJ_BANKS = 4
SCORE_BANK = 4
TURN_BANK = 6
QUARTER_BANK = 4


def cross_attention_phase(core, io):
    nc = core.nc
    resid, xT, cT, ident, banks = core.resid, core.xT, core.cT, core.ident, core.banks
    with ExitStack() as ctx:
        sb, pair, sem = core.sb, core.pair, core.sem
        KINDS = ("A", "B", "V", "O")
        raw = {k: sb(ctx, "x_raw" + k, [P, 2 * DC * P]) for k in KINDS}
        wt = {k: pair(ctx, "x_w" + k, [P, 2 * DC * P]) for k in KINDS}
        q = pair(ctx, "x_q", [P, TOK])
        k_ = pair(ctx, "x_k", [P, TOK])
        v = pair(ctx, "x_v", [P, B, 2 * P])
        att = pair(ctx, "x_att", [P, 2, TOK])
        pT = pair(ctx, "x_pT", [P, 2, HALF])
        probs = sb(ctx, "x_probs", [P, B, P])
        bias_in = sb(ctx, "x_bias", [P, 2, P])
        biased = sb(ctx, "x_biased", [P, B, P])
        mask8 = sb(ctx, "x_mask8", [P, B, P], U8)
        mask = sb(ctx, "x_mask", [P, B, P])
        some = sb(ctx, "x_some", [P, B])
        top = sb(ctx, "x_top", [P, B])
        total = sb(ctx, "x_total", [P, B])
        inv = sb(ctx, "x_inv", [P, B])

        raw_in = {k: sem("x_raw_in" + k) for k in KINDS}
        w_hi = {k: sem("x_w_hi" + k) for k in KINDS}
        w_lo = {k: sem("x_w_lo" + k) for k in KINDS}
        bias_loaded = sem("x_bias_loaded")
        mask_in = sem("x_mask_in")
        mask_ready = sem("x_mask_ready")
        some_ready = sem("x_some_ready")
        biased_ready = sem("x_biased_ready")
        proj_ready = sem("x_proj_ready")
        proj_free = sem("x_proj_free")
        qkv_hi = sem("x_qkv_hi")
        scores_ready = sem("x_scores_ready")
        logits_ready = sem("x_logits_ready")
        top_ready = sem("x_top_ready")
        exp_done = sem("x_exp_done")
        raw_inv = sem("x_raw_inv")
        inv_ready = sem("x_inv_ready")
        probs_ready = sem("x_probs_ready")
        turned = sem("x_turned")
        pT_hi = sem("x_pT_hi")
        pT_lo = sem("x_pT_lo")
        pv_ready = sem("x_pv_ready")
        att_hi = sem("x_att_hi")
        att_lo = sem("x_att_lo")

        PER = 20

        def seq_a(g, n):
            return (PER * g - 8 if not isinstance(g, int) or g else 0) + n

        def seq_out(g, n):
            return PER * g - 4 + n if not isinstance(g, int) or g < PAIRS else PER * g - 8 + n

        def seq_v(g, n):
            return PER * g + 4 + n

        def seq_b(g, n):
            return PER * g + 8 + n

        def wqk(kind, hl, which, c):
            return wt[kind][hl][:, (which * DC + c) * P:(which * DC + c + 1) * P]

        def loop(engine, body):
            body(0, True, False)
            with engine.Fori(1, PAIRS - 1) as g:
                body(g, False, False)
            body(PAIRS - 1, False, True)

        with nc.Block() as block:
            @block.sync
            def _(sp):
                sp.dma_start(mask8[:, :, :], io["mask"].rearrange("b q k -> q b k")).then_inc(mask_in, DMA)

                def load(kind, g, first):
                    if not first:
                        sp.wait_ge(w_hi[kind], g)
                        sp.wait_ge(w_lo[kind], g)
                    src = io["w" + kind]
                    sp.dma_start(raw[kind][:, :], src[bass.ds(g, 1), :, :].rearrange("o p n -> p (o n)"))\
                        .then_inc(raw_in[kind], DMA)

                def body(g, first, last):
                    load("A", g, first)
                    if not first:
                        sp.wait_ge(biased_ready, 2 * g)
                    sp.dma_start(bias_in[:, :, :],
                                 io["bias"][bass.ds(g, 1)].rearrange("o h q k -> q (o h) k")).then_inc(bias_loaded, DMA)
                    for kind in ("V", "B", "O"):
                        load(kind, g, first)

                loop(sp, body)

            @block.tensor
            def _(pe):
                def bank_free(s):
                    if not isinstance(s, int) or s >= PROJ_BANKS:
                        pe.wait_ge(proj_free, s - PROJ_BANKS + 1)

                def qk(kind, seq, n):
                    which, half = n // 2, n % 2
                    src = xT if which == 0 else cT
                    bank_free(seq)
                    for c in range(DC):
                        mm = product(pe, banks[:, n, :], (wqk(kind, 0, which, c), wqk(kind, 1, which, c)),
                                     [s[:, c, half * HALF:(half + 1) * HALF] for s in src], c == 0, c == DC - 1)
                    mm.then_inc(proj_ready, 1)

                def values(g):
                    pe.wait_ge(w_hi["V"], g + 1)
                    pe.wait_ge(w_lo["V"], g + 1)
                    for n in range(4):
                        bank_free(seq_v(g, n))
                        for t in range(2):
                            b = 2 * n + t
                            for c in range(DC):
                                mm = product(pe, banks[:, n, t * 256:(t + 1) * 256], [s[:, c, tok(b)] for s in cT],
                                             [w[:, c * 256:(c + 1) * 256] for w in wt["V"]], c == 0, c == DC - 1)
                        mm.then_inc(proj_ready, 1)

                def scores(n, j, seq, first=False):
                    pe.wait_ge(proj_free, seq + 1)
                    if not first:
                        pe.wait_ge(top_ready, 2 * n + j - 1)
                    for i in range(HB):
                        b = HB * j + i
                        mm = product(pe, banks[:, SCORE_BANK + j, tok(i)], [s[:, tok(b)] for s in q],
                                     [s[:, tok(b)] for s in k_], True, True)
                    mm.then_inc(scores_ready, 1)

                def turn(n, j, first=False):
                    pe.wait_ge(probs_ready, 2 * n + j + 1)
                    if not first:
                        pe.wait_ge(att_lo, 2 * n + j - 1)
                    for i in range(HB):
                        mm = pe.transpose(banks[:, TURN_BANK + j, tok(i)], probs[:, HB * j + i, :], ident[:, :])
                    mm.then_inc(turned, 1)

                def pv(n, j, slot, g):
                    pe.wait_ge(pT_lo, 2 * n + j + 1)
                    pe.wait_ge(proj_free, seq_v(g, 3) + 1)
                    for i in range(HB):
                        b = HB * j + i
                        mm = product(pe, banks[:, TURN_BANK + j, tok(i)], [s[:, b, tok(slot)] for s in v],
                                     [s[:, j, tok(i)] for s in pT], True, True)
                    mm.then_inc(pv_ready, 1)

                def output(g):
                    pe.wait_ge(w_hi["O"], g)
                    pe.wait_ge(w_lo["O"], g)
                    for b in range(B):
                        if b % HB == 0:
                            pe.wait_ge(att_lo, 4 * g + b // HB - 1)
                        bank_free(seq_out(g, b))
                        for h in range(2):
                            mm = product(pe, banks[:, b % PROJ_BANKS, :], [s[:, h, tok(b)] for s in att],
                                         [w[:, h * D:(h + 1) * D] for w in wt["O"]], h == 0, h == 1)
                        mm.then_inc(proj_ready, 1)

                def body(g, first, last):
                    a, bb = 2 * g, 2 * g + 1
                    pe.wait_ge(w_hi["A"], g + 1)
                    pe.wait_ge(w_lo["A"], g + 1)
                    qk("A", seq_a(g, 0), 0)
                    qk("A", seq_a(g, 1), 1)
                    qk("A", seq_a(g, 2), 2)
                    if not first:
                        turn(a - 1, 0)
                    qk("A", seq_a(g, 3), 3)
                    if not first:
                        turn(a - 1, 1)
                    scores(a, 0, seq_a(g, 2), first)
                    if not first:
                        pv(a - 1, 0, 1, g - 1)
                    scores(a, 1, seq_a(g, 3), first)
                    if not first:
                        pv(a - 1, 1, 1, g - 1)
                        output(g)
                    values(g)
                    pe.wait_ge(w_hi["B"], g + 1)
                    pe.wait_ge(w_lo["B"], g + 1)
                    qk("B", seq_b(g, 0), 0)
                    turn(a, 0, first)
                    qk("B", seq_b(g, 1), 1)
                    turn(a, 1, first)
                    qk("B", seq_b(g, 2), 2)
                    qk("B", seq_b(g, 3), 3)
                    pv(a, 0, 0, g)
                    scores(bb, 0, seq_b(g, 2))
                    pv(a, 1, 0, g)
                    scores(bb, 1, seq_b(g, 3))

                loop(pe, body)
                tail = HEADS - 1
                turn(tail, 0)
                turn(tail, 1)
                pv(tail, 0, 1, PAIRS - 1)
                pv(tail, 1, 1, PAIRS - 1)
                output(PAIRS)

            @block.scalar
            def _(act):
                def exps(n, j):
                    act.wait_ge(top_ready, 2 * n + j + 1)
                    for i in range(HB):
                        b = HB * j + i
                        e = nc.scalar.activation(probs[:, b, :], probs[:, b, :], ACT.Exp, bias=top[:, b:b + 1],
                                                 accum_out=total[:, b:b + 1])
                    e.then_inc(exp_done, 1)

                def keep(dst, bank, seq, done):
                    act.wait_ge(proj_ready, seq + 1)
                    nc.scalar.copy(dst, banks[:, bank, :]).then_inc(done, 1)

                def qk(seq, n, head, first=False):
                    if n == 0 and not first:
                        act.wait_ge(scores_ready, 2 * head)
                    dst = (q if n < 2 else k_)[0]
                    keep(dst[:, (n % 2) * HALF:(n % 2 + 1) * HALF], n, seq, qkv_hi)

                def probs_hi(n, j, first=False):
                    act.wait_ge(turned, 2 * n + j + 1)
                    if not first:
                        act.wait_ge(pv_ready, 2 * n + j - 1)
                    nc.scalar.copy(pT[0][:, j, :], banks[:, TURN_BANK + j, :]).then_inc(pT_hi, 1)

                def attn_hi(n, j, slot):
                    act.wait_ge(pv_ready, 2 * n + j + 1)
                    nc.scalar.copy(att[0][:, slot, j * HALF:(j + 1) * HALF], banks[:, TURN_BANK + j, :])\
                        .then_inc(att_hi, 1)

                def weights(kind, g, used=None):
                    act.wait_ge(raw_in[kind], DMA * (g + 1))
                    if used is not None:
                        act.wait_ge(proj_ready, used + 1)
                    nc.scalar.copy(wt[kind][0][:, :], raw[kind][:, :]).then_inc(w_hi[kind], 1)

                def body(g, first, last):
                    a = 2 * g
                    if not first:
                        exps(a - 1, 0)
                        exps(a - 1, 1)
                    qk(seq_a(g, 0), 0, a, first)
                    qk(seq_a(g, 1), 1, a)
                    qk(seq_a(g, 2), 2, a)
                    if not first:
                        probs_hi(a - 1, 0)
                    qk(seq_a(g, 3), 3, a)
                    if not first:
                        probs_hi(a - 1, 1)
                        attn_hi(a - 1, 0, 1)
                        attn_hi(a - 1, 1, 1)
                    exps(a, 0)
                    exps(a, 1)
                    if not last:
                        weights("A", g + 1, seq_a(g, 3))
                    weights("O", g, None if first else seq_out(g, 7))
                    for n in range(4):
                        if n == 0 and not first:
                            act.wait_ge(pv_ready, 4 * g)
                        keep(v[0][:, 2 * n:2 * n + 2, :].rearrange("p b f -> p (b f)"), n, seq_v(g, n), qkv_hi)
                    qk(seq_b(g, 0), 0, a + 1)
                    probs_hi(a, 0, first)
                    qk(seq_b(g, 1), 1, a + 1)
                    probs_hi(a, 1, first)
                    qk(seq_b(g, 2), 2, a + 1)
                    qk(seq_b(g, 3), 3, a + 1)
                    if not first:
                        act.wait_ge(proj_ready, seq_out(g, 7) + 1)
                    attn_hi(a, 0, 0)
                    attn_hi(a, 1, 0)
                    if not last:
                        weights("V", g + 1, seq_v(g, 3))
                        weights("B", g + 1, seq_b(g, 3))

                weights("A", 0)
                weights("V", 0)
                weights("B", 0)
                loop(act, body)
                tail = HEADS - 1
                exps(tail, 0)
                exps(tail, 1)
                probs_hi(tail, 0)
                probs_hi(tail, 1)
                attn_hi(tail, 0, 1)
                attn_hi(tail, 1, 1)

            @block.vector
            def _(dve):
                def logits(n, j):
                    dve.wait_ge(scores_ready, 2 * n + j + 1)
                    dve.wait_ge(biased_ready, n + 1)
                    if not isinstance(n, int) or n:
                        dve.wait_ge(turned, 2 * n + j - 1)
                    part = slice(HB * j, HB * (j + 1))
                    bank = banks[:, SCORE_BANK + j, :].rearrange("p (b k) -> p b k", b=HB)
                    dve.tensor_tensor(probs[:, part, :], bank, biased[:, part, :], ALU.add).then_inc(logits_ready, 1)
                    dve.wait_ge(logits_ready, 2 * n + j + 1)
                    dve.tensor_reduce(top[:, part], probs[:, part, :], AX_X, ALU.max, negate=True)\
                        .then_inc(top_ready, 1)

                def inverse(n, j):
                    dve.wait_ge(exp_done, 2 * n + j + 1)
                    part = slice(HB * j, HB * (j + 1))
                    dve.reciprocal(inv[:, part], total[:, part]).then_inc(raw_inv, 1)
                    dve.wait_ge(raw_inv, 2 * n + j + 1)
                    dve.tensor_tensor(inv[:, part], inv[:, part], some[:, part], ALU.mult).then_inc(inv_ready, 1)

                def low(dst, src, hi, done):
                    dve.tensor_tensor(dst, src, f32(hi), ALU.subtract).then_inc(done, 1)

                def keep(dst, bank, nth):
                    dve.wait_ge(qkv_hi, nth + 1)
                    low(dst[1], banks[:, bank, :], dst[0], proj_free)

                def qk(nth, n):
                    src = q if n < 2 else k_
                    keep([s[:, (n % 2) * HALF:(n % 2 + 1) * HALF] for s in src], n, nth)

                def probs_lo(n, j):
                    dve.wait_ge(pT_hi, 2 * n + j + 1)
                    low(pT[1][:, j, :], banks[:, TURN_BANK + j, :], pT[0][:, j, :], pT_lo)

                def attn_lo(n, j, slot):
                    dve.wait_ge(att_hi, 2 * n + j + 1)
                    cut = slice(j * HALF, (j + 1) * HALF)
                    low(att[1][:, slot, cut], banks[:, TURN_BANK + j, :], att[0][:, slot, cut], att_lo)

                def output(g):
                    for b in range(B):
                        dve.wait_ge(proj_ready, seq_out(g, b) + 1)
                        dve.tensor_tensor(resid[:, b, :], banks[:, b % PROJ_BANKS, :], resid[:, b, :], ALU.add)\
                            .then_inc(proj_free, 1)

                def body(g, first, last):
                    a = 2 * g
                    if not first:
                        logits(a - 1, 0)
                        logits(a - 1, 1)
                        inverse(a - 1, 0)
                    qk(12 * g, 0)
                    if not first:
                        inverse(a - 1, 1)
                    qk(12 * g + 1, 1)
                    qk(12 * g + 2, 2)
                    if not first:
                        probs_lo(a - 1, 0)
                    qk(12 * g + 3, 3)
                    if not first:
                        probs_lo(a - 1, 1)
                    logits(a, 0)
                    if not first:
                        attn_lo(a - 1, 0, 1)
                    logits(a, 1)
                    if not first:
                        attn_lo(a - 1, 1, 1)
                    inverse(a, 0)
                    inverse(a, 1)
                    if not first:
                        output(g)
                    for n in range(4):
                        keep([s[:, 2 * n:2 * n + 2, :].rearrange("p b f -> p (b f)") for s in v], n, 12 * g + 4 + n)
                    qk(12 * g + 8, 0)
                    probs_lo(a, 0)
                    qk(12 * g + 9, 1)
                    probs_lo(a, 1)
                    qk(12 * g + 10, 2)
                    qk(12 * g + 11, 3)
                    attn_lo(a, 0, 0)
                    attn_lo(a, 1, 0)

                dve.wait_ge(mask_in, DMA)
                dve.tensor_reduce(some[:, :], mask8[:, :, :], AX_X, ALU.max).then_inc(some_ready, 1)
                dve.wait_ge(some_ready, 1)
                loop(dve, body)
                tail = HEADS - 1
                logits(tail, 0)
                logits(tail, 1)
                inverse(tail, 0)
                inverse(tail, 1)
                probs_lo(tail, 0)
                probs_lo(tail, 1)
                attn_lo(tail, 0, 1)
                attn_lo(tail, 1, 1)
                output(PAIRS)

            @block.gpsimd
            def _(pool):
                def weights(kind, g):
                    pool.wait_ge(w_hi[kind], g + 1)
                    pool.tensor_tensor(wt[kind][1][:, :], raw[kind][:, :], f32(wt[kind][0][:, :]), ALU.subtract)\
                        .then_inc(w_lo[kind], 1)

                def bias(n, slot, first=False):
                    pool.wait_ge(bias_loaded, 8 * (n - slot) + DMA)
                    if not first:
                        pool.wait_ge(top_ready, 2 * n)
                    row = bias_in[:, slot, :].unsqueeze(1).to_broadcast([P, B, P])
                    pool.tensor_tensor(biased[:, :, :], mask[:, :, :], row, ALU.add).then_inc(biased_ready, 1)

                def normalise(n, j):
                    pool.wait_ge(inv_ready, 2 * n + j + 1)
                    part = slice(HB * j, HB * (j + 1))
                    rows = inv[:, part].unsqueeze(2).to_broadcast([P, HB, P])
                    pool.tensor_tensor(probs[:, part, :], probs[:, part, :], rows, ALU.mult).then_inc(probs_ready, 1)

                def body(g, first, last):
                    a = 2 * g
                    if not first:
                        normalise(a - 1, 0)
                        normalise(a - 1, 1)
                    bias(a, 0, first)
                    normalise(a, 0)
                    normalise(a, 1)
                    if not last:
                        weights("A", g + 1)
                    weights("O", g)
                    bias(a + 1, 1)
                    if not last:
                        weights("V", g + 1)
                        weights("B", g + 1)

                pool.wait_ge(mask_in, DMA)
                pool.tensor_scalar(mask[:, :, :], mask8[:, :, :], MASKED, -MASKED, ALU.mult, ALU.add)\
                    .then_inc(mask_ready, 1)
                pool.wait_ge(mask_ready, 1)
                weights("A", 0)
                weights("V", 0)
                weights("B", 0)
                loop(pool, body)
                normalise(HEADS - 1, 0)
                normalise(HEADS - 1, 1)


def ffn_phase(core, io):
    nc = core.nc
    resid, xT, banks = core.resid, core.xT, core.banks
    with ExitStack() as ctx:
        sb, pair, sem = core.sb, core.pair, core.sem
        gu_raw = sb(ctx, "f_gu_raw", [P, 2, 2 * DC * P])
        d_raw = sb(ctx, "f_d_raw", [P, 2, D])
        gu = pair(ctx, "f_gu", [P, 2, 2 * DC * P])
        dn = pair(ctx, "f_dn", [P, 2, D])
        gate = sb(ctx, "f_gate", [P, 2, TOK])
        hidden = sb(ctx, "f_hidden", [P, 2, TOK])
        hid = pair(ctx, "f_hid", [P, 2, TOK])
        bias = sb(ctx, "f_bias", [P, 2, 2])

        bias_in = [sem(f"f_bias_in{par}") for par in range(2)]
        gu_in = [sem(f"f_gu_in{par}") for par in range(2)]
        d_in = [sem(f"f_d_in{par}") for par in range(2)]
        gu_hi = sem("f_gu_hi")
        gu_lo = sem("f_gu_lo")
        d_hi = sem("f_d_hi")
        d_lo = sem("f_d_lo")
        proj_ready = sem("f_proj_ready")
        down_free = sem("f_down_free")
        gate_ready = sem("f_gate_ready")
        hidden_ready = sem("f_hidden_ready")
        hid_hi = sem("f_hid_hi")
        hid_lo = sem("f_hid_lo")

        def seq_gu(c, n):
            return (12 * c - 8 if not isinstance(c, int) or c else 0) + n

        def seq_down(c, n):
            return 12 * c + 8 + n if not isinstance(c, int) or c < FULL else 12 * c + 4 + n

        def rows(c):
            return REST if isinstance(c, int) and c == FULL else P

        def loop(engine, body):
            body(0, 0, 0)
            body(1, 1, 0)
            body(2, 0, 1)
            with engine.Fori(1, FULL // 2 - 1) as i:
                body(2 * i + 1, 1, i)
                body(2 * i + 2, 0, i + 1)
            body(FULL - 1, 1, FULL // 2 - 1)
            body(FULL, 0, FULL // 2)

        with nc.Block() as block:
            @block.sync
            def _(sp):
                def body(c, par, turn):
                    m = rows(c)
                    if not isinstance(c, int) or c >= 2:
                        sp.wait_ge(gu_hi, c - 1)
                        sp.wait_ge(gu_lo, c - 1)
                    src = io["f_gu_rest"] if m == REST else \
                        io["f_gu"][bass.ds(c, 1)].rearrange("o p n -> p (o n)")
                    sp.dma_start(gu_raw[:, par, 0:2 * DC * m], src).then_inc(gu_in[par], DMA)
                    if not isinstance(c, int) or c >= 2:
                        sp.wait_ge(d_hi, c - 1)
                        sp.wait_ge(d_lo, c - 1)
                    src = io["f_d_rest"] if m == REST else io["f_d"][bass.ds(c, 1)].rearrange("o p n -> p (o n)")
                    sp.dma_start(d_raw[0:m, par, :], src).then_inc(d_in[par], DMA)
                    if not isinstance(c, int) or c >= 2:
                        sp.wait_ge(hidden_ready, 2 * c - 2)
                    src = io["f_b_rest"] if m == REST else io["f_b"][bass.ds(c, 1)].rearrange("o p n -> p (o n)")
                    sp.dma_start(bias[0:m, par, :], src).then_inc(bias_in[par], DMA)

                loop(sp, body)

            @block.tensor
            def _(pe):
                def down(c, par, last=False):
                    m = rows(c)
                    pe.wait_ge(d_hi, c + 1)
                    pe.wait_ge(d_lo, c + 1)
                    for b in range(B):
                        if b % HB == 0:
                            pe.wait_ge(hid_lo, 2 * c + b // HB + 1)
                        if b >= PROJ_BANKS or last:
                            pe.wait_ge(down_free, B * c + b - PROJ_BANKS + 1)
                        else:
                            pe.wait_ge(hidden_ready, 2 * (c + 1) + b % 2 + 1)
                        product(pe, banks[:, b % PROJ_BANKS, :], [s[0:m, par, tok(b)] for s in hid],
                                [w[0:m, par, :] for w in dn], True, True).then_inc(proj_ready, 1)

                def body(c, par, turn):
                    m = rows(c)
                    pe.wait_ge(gu_hi, c + 1)
                    pe.wait_ge(gu_lo, c + 1)
                    for n in range(4):
                        which, half = n // 2, n % 2
                        if not isinstance(c, int) or c >= 2:
                            pe.wait_ge(down_free, B * (c - 2) + PROJ_BANKS + n + 1)
                        elif c == 1:
                            pe.wait_ge(hidden_ready, half + 1)
                        for k in range(DC):
                            at = (which * DC + k) * m
                            mm = product(pe, banks[0:m, n, :], [w[:, par, at:at + m] for w in gu],
                                         [s[:, k, half * HALF:(half + 1) * HALF] for s in xT], k == 0, k == DC - 1)
                        mm.then_inc(proj_ready, 1)
                    if not isinstance(c, int) or c:
                        down(c - 1, 1 - par)

                loop(pe, body)
                down(FULL, 0, last=True)

            @block.scalar
            def _(act):
                def weights(c, par, turn):
                    m = rows(c)
                    act.wait_ge(gu_in[par], DMA * (turn + 1))
                    if not isinstance(c, int) or c >= 2:
                        act.wait_ge(proj_ready, seq_gu(c - 2, 3) + 1)
                    nc.scalar.copy(gu[0][:, par, 0:2 * DC * m], gu_raw[:, par, 0:2 * DC * m]).then_inc(gu_hi, 1)
                    act.wait_ge(d_in[par], DMA * (turn + 1))
                    if not isinstance(c, int) or c >= 2:
                        act.wait_ge(proj_ready, seq_down(c - 2, 7) + 1)
                    nc.scalar.copy(dn[0][0:m, par, :], d_raw[0:m, par, :]).then_inc(d_hi, 1)

                def body(c, par, turn):
                    m = rows(c)
                    act.wait_ge(bias_in[par], DMA * (turn + 1))
                    for half in range(2):
                        cut = slice(half * HALF, (half + 1) * HALF)
                        act.wait_ge(proj_ready, seq_gu(c, half) + 1)
                        if not isinstance(c, int) or c >= 2:
                            act.wait_ge(hidden_ready, 2 * c - 2 + half - 1)
                        nc.scalar.activation(gate[0:m, par, cut], banks[0:m, half, :], ACT.Silu,
                                             bias=bias[0:m, par, 0:1])\
                            .then_inc(gate_ready, 1)
                    if not isinstance(c, int) or c < FULL:
                        weights(c + 1, 1 - par, turn + par)
                    for half in range(2):
                        cut = slice(half * HALF, (half + 1) * HALF)
                        act.wait_ge(hidden_ready, 2 * c + half + 1)
                        if not isinstance(c, int) or c >= 2:
                            act.wait_ge(proj_ready, seq_down(c - 2, 7) + 1)
                        nc.scalar.copy(hid[0][0:m, par, cut], hidden[0:m, par, cut]).then_inc(hid_hi, 1)

                weights(0, 0, 0)
                loop(act, body)

            @block.vector
            def _(dve):
                def down(c):
                    for b in range(B):
                        dve.wait_ge(proj_ready, seq_down(c, b) + 1)
                        dve.tensor_tensor(resid[:, b, :], banks[:, b % PROJ_BANKS, :], resid[:, b, :], ALU.add)\
                            .then_inc(down_free, 1)

                def body(c, par, turn):
                    m = rows(c)
                    dve.wait_ge(bias_in[par], DMA * (turn + 1))
                    for half in range(2):
                        cut = slice(half * HALF, (half + 1) * HALF)
                        dve.wait_ge(gate_ready, 2 * c + half + 1)
                        dve.wait_ge(proj_ready, seq_gu(c, 2 + half) + 1)
                        if not isinstance(c, int) or c >= 2:
                            dve.wait_ge(hid_lo, 2 * (c - 2) + half + 1)
                        dve.scalar_tensor_tensor(hidden[0:m, par, cut], banks[0:m, 2 + half, :], bias[0:m, par, 1:2],
                                                 gate[0:m, par, cut], ALU.add, ALU.mult).then_inc(hidden_ready, 1)
                    if not isinstance(c, int) or c:
                        down(c - 1)

                loop(dve, body)
                down(FULL)

            @block.gpsimd
            def _(pool):
                def weights(c, par):
                    m = rows(c)
                    n = 2 * DC * m
                    pool.wait_ge(gu_hi, c + 1)
                    pool.tensor_tensor(gu[1][:, par, 0:n], gu_raw[:, par, 0:n], f32(gu[0][:, par, 0:n]), ALU.subtract)\
                        .then_inc(gu_lo, 1)
                    pool.wait_ge(d_hi, c + 1)
                    pool.tensor_tensor(dn[1][0:m, par, :], d_raw[0:m, par, :], f32(dn[0][0:m, par, :]), ALU.subtract)\
                        .then_inc(d_lo, 1)

                def body(c, par, turn):
                    m = rows(c)
                    if not isinstance(c, int) or c < FULL:
                        weights(c + 1, 1 - par)
                    for half in range(2):
                        cut = slice(half * HALF, (half + 1) * HALF)
                        pool.wait_ge(hid_hi, 2 * c + half + 1)
                        pool.tensor_tensor(hid[1][0:m, par, cut], hidden[0:m, par, cut], f32(hid[0][0:m, par, cut]),
                                           ALU.subtract).then_inc(hid_lo, 1)

                weights(0, 0)
                loop(pool, body)


def grouped_attention_phase(core, io):
    nc = core.nc
    resid, xT, cT, ident, banks = core.resid, core.xT, core.cT, core.ident, core.banks
    ROUNDS = PAIRS // 4
    with ExitStack() as ctx:
        sb, pair, sem = core.sb, core.pair, core.sem
        SIZE = {"Q": 2 * DC * P, "K": DC * P, "V": 2 * DC * P, "O": 2 * D}
        raw = {k: sb(ctx, "g_raw" + k, [P, n]) for k, n in SIZE.items()}
        wt = {k: pair(ctx, "g_w" + k, [P, n]) for k, n in SIZE.items()}
        q = pair(ctx, "g_q", [P, 2, TOK])
        k_ = pair(ctx, "g_k", [P, TOK])
        v = pair(ctx, "g_v", [P, B, 2 * P])
        att = pair(ctx, "g_att", [P, 2, TOK])
        pT = pair(ctx, "g_pT", [P, 2, HALF])
        probs = sb(ctx, "g_probs", [P, 2 * B, P])
        swapped = sb(ctx, "g_swapped", [P, 2, HALF])
        turned_by = sb(ctx, "g_turned_by", [P, 2, HALF])
        cos = sb(ctx, "g_cos", [P, P])
        sin = sb(ctx, "g_sin", [P, P])
        mask8 = sb(ctx, "g_mask8", [P, P], U8)
        mask = sb(ctx, "g_mask", [P, P])
        mask_raw = sb(ctx, "g_mask_raw", [P, P])
        some = sb(ctx, "g_some", [P, 1])
        cap = sb(ctx, "g_cap", [P, 1])
        total = sb(ctx, "g_total", [P, 2 * B])
        inv = sb(ctx, "g_inv", [P, 2 * B])

        raw_in = {k: sem("g_raw_in" + k) for k in SIZE}
        w_hi = {k: sem("g_w_hi" + k) for k in SIZE}
        w_lo = {k: sem("g_w_lo" + k) for k in SIZE}
        consts_in = sem("g_consts_in")
        mask_steps = sem("g_mask_steps")
        cap_ready = sem("g_cap_ready")
        mask_ready = sem("g_mask_ready")
        proj_ready = sem("g_proj_ready")
        proj_free = sem("g_proj_free")
        v_hi = sem("g_v_hi")
        swap_done = sem("g_swap_done")
        sin_done = sem("g_sin_done")
        rope_done = sem("g_rope_done")
        qk_hi = sem("g_qk_hi")
        qk_lo = sem("g_qk_lo")
        scores_ready = sem("g_scores_ready")
        tanh_done = sem("g_tanh_done")
        logits_ready = sem("g_logits_ready")
        exp_done = sem("g_exp_done")
        inv_ready = sem("g_inv_ready")
        probs_ready = sem("g_probs_ready")
        turned = sem("g_turned")
        pT_hi = sem("g_pT_hi")
        pT_lo = sem("g_pT_lo")
        pv_ready = sem("g_pv_ready")
        att_hi = sem("g_att_hi")
        att_lo = sem("g_att_lo")

        PER = 56
        Q_AT = (2, 18, 32, 44)
        K_AT = {0: 0, 2: 30}
        OUT_AT = (6, 22, 36, 48)
        V_AT = 14
        ROPES = 20
        ROPE_AT = (0, 6, 10, 16)

        def is_first(r, u):
            return isinstance(r, int) and r == 0 and u == 0

        def seq(r, u, at):
            if is_first(r, u) and at < OUT_AT[0]:
                return at
            return PER * r - 8 + at

        def seq_out(r, u, n):
            return PER * r - 8 + (OUT_AT[u] if not (isinstance(r, int) and r == ROUNDS) else 0) + n

        def ropes(u):
            blocks = [(K_AT[u] + h, None, h) for h in range(2)] if u in K_AT else []
            return blocks + [(Q_AT[u] + 2 * h + s, s, h) for h in range(2) for s in range(2)]

        def rope_of(r, u, slot, half):
            return ROPES * r + ROPE_AT[u] + (2 if u in K_AT else 0) + 2 * half + slot

        def dst(slot, half, hl):
            cut = slice(half * HALF, (half + 1) * HALF)
            return k_[hl][:, cut] if slot is None else q[hl][:, slot, cut]

        def nth_quarter(p, j, back=0):
            n = 4 * (p - back) + j + 1
            return None if isinstance(n, int) and n <= 0 else n

        def bank_quarter(j):
            return banks[:, QUARTER_BANK + j, :].rearrange("p (b h t) -> p b h t", b=2, h=2)

        def att_quarter(hl, j):
            return att[hl][:, :, tok(2 * j, 2)].rearrange("p h (b t) -> p b h t", b=2)

        def quarter(j):
            return slice(4 * j, 4 * j + 4)

        def loop(engine, body):
            for u in range(4):
                body(0, u, u == 0, False)
            with engine.Fori(1, ROUNDS - 1) as r:
                for u in range(4):
                    body(r, u, False, False)
            for u in range(4):
                body(ROUNDS - 1, u, False, u == 3)

        with nc.Block() as block:
            @block.sync
            def _(sp):
                sp.dma_start(mask8[:, :], io["g_mask"]).then_inc(consts_in, DMA)
                sp.dma_start(cos[:, :], io["g_cos"]).then_inc(consts_in, DMA)
                sp.dma_start(sin[:, :], io["g_sin"]).then_inc(consts_in, DMA)

                def load(kind, n):
                    if not isinstance(n, int) or n:
                        sp.wait_ge(w_hi[kind], n)
                        sp.wait_ge(w_lo[kind], n)
                    sp.dma_start(raw[kind][:, :], io["g_w" + kind][bass.ds(n, 1)].rearrange("o p n -> p (o n)"))\
                        .then_inc(raw_in[kind], DMA)

                def body(r, u, first, last):
                    final_round = isinstance(r, int) and r == ROUNDS - 1
                    if not last:
                        load("Q", 4 * r + u + 1)
                    if u == 0 or (u == 2 and not final_round):
                        load("K", 2 * r + u // 2 + 1)
                    if u == 1 and not final_round:
                        load("V", r + 1)
                    load("O", 4 * r + u)

                load("K", 0)
                load("Q", 0)
                load("V", 0)
                loop(sp, body)

            @block.tensor
            def _(pe):
                def bank_free(s):
                    if not isinstance(s, int) or s >= PROJ_BANKS:
                        pe.wait_ge(proj_free, s - PROJ_BANKS + 1)

                def weights_ready(kind, n):
                    pe.wait_ge(w_hi[kind], n + 1)
                    pe.wait_ge(w_lo[kind], n + 1)

                def project(s, at, kind, slot, half):
                    src = cT if kind == "K" else xT
                    bank_free(s)
                    for c in range(DC):
                        col = (slot * DC + c) * P
                        mm = product(pe, banks[:, at % PROJ_BANKS, :], [w[:, col:col + P] for w in wt[kind]],
                                     [x[:, c, half * HALF:(half + 1) * HALF] for x in src], c == 0, c == DC - 1)
                    mm.then_inc(proj_ready, 1)

                def values(r):
                    weights_ready("V", r)
                    for n in range(4):
                        s = seq(r, 0, V_AT + n)
                        bank_free(s)
                        for t in range(2):
                            for c in range(DC):
                                mm = product(pe, banks[:, (V_AT + n) % PROJ_BANKS, t * 256:(t + 1) * 256],
                                             [x[:, c, tok(2 * n + t)] for x in cT],
                                             [w[:, c * 256:(c + 1) * 256] for w in wt["V"]], c == 0, c == DC - 1)
                        mm.then_inc(proj_ready, 1)

                def scores(p, j, rope, first):
                    pe.wait_ge(qk_lo, rope + 1)
                    if not first:
                        pe.wait_ge(att_lo, nth_quarter(p, j, 1))
                    for t in range(4):
                        b, h = 2 * j + t // 2, t % 2
                        mm = product(pe, banks[:, QUARTER_BANK + j, tok(t)], [s[:, h, tok(b)] for s in q],
                                     [s[:, tok(b)] for s in k_], True, True)
                    mm.then_inc(scores_ready, 1)

                def turn(p, j):
                    pe.wait_ge(probs_ready, nth_quarter(p, j))
                    for t in range(4):
                        mm = pe.transpose(banks[:, QUARTER_BANK + j, tok(t)], probs[:, 4 * j + t, :], ident[:, :])
                    mm.then_inc(turned, 1)

                def pv(p, j, kv):
                    pe.wait_ge(pT_lo, nth_quarter(p, j))
                    for t in range(2):
                        mm = product(pe, banks[:, QUARTER_BANK + j, tok(2 * t, 2)], [s[:, 2 * j + t, tok(kv)] for s in v],
                                     [s[:, j % 2, tok(2 * t, 2)] for s in pT], True, True)
                    mm.then_inc(pv_ready, 1)

                def output(r, u):
                    p = 4 * r + u
                    weights_ready("O", p - 1)
                    for b in range(B):
                        if b % 2 == 0:
                            pe.wait_ge(att_lo, nth_quarter(p, b // 2, 1))
                        s = seq_out(r, u, b)
                        bank_free(s)
                        for h in range(2):
                            mm = product(pe, banks[:, (OUT_AT[u] + b) % PROJ_BANKS, :], [x[:, h, tok(b)] for x in att],
                                         [w[:, h * D:(h + 1) * D] for w in wt["O"]], h == 0, h == 1)
                        mm.then_inc(proj_ready, 1)

                def body(r, u, first, last):
                    p = 4 * r + u
                    before_kv = (u - 1) // 2 % 2
                    if u in K_AT:
                        weights_ready("K", 2 * r + u // 2)
                        for half in range(2):
                            project(seq(r, u, K_AT[u] + half), K_AT[u] + half, "K", 0, half)
                    weights_ready("Q", p)
                    for n in range(4):
                        if n == 3 and not first:
                            turn(p - 1, 0)
                            turn(p - 1, 1)
                        project(seq(r, u, Q_AT[u] + n), Q_AT[u] + n, "Q", n % 2, n // 2)
                    if not first:
                        pe.wait_ge(proj_free, seq(r, 0, V_AT + 3) - (PER if u == 0 else 0) + 1)
                        pv(p - 1, 0, before_kv)
                        turn(p - 1, 2)
                        pv(p - 1, 1, before_kv)
                        turn(p - 1, 3)
                    scores(p, 0, rope_of(r, u, 1, 0), first)
                    if not first:
                        pv(p - 1, 2, before_kv)
                    scores(p, 1, rope_of(r, u, 1, 0), first)
                    if not first:
                        pv(p - 1, 3, before_kv)
                    scores(p, 2, rope_of(r, u, 1, 1), first)
                    scores(p, 3, rope_of(r, u, 1, 1), first)
                    if not first:
                        output(r, u)
                    if u == 0:
                        values(r)

                loop(pe, body)
                tail = PAIRS - 1
                turn(tail, 0)
                turn(tail, 1)
                pv(tail, 0, 1)
                turn(tail, 2)
                pv(tail, 1, 1)
                turn(tail, 3)
                pv(tail, 2, 1)
                pv(tail, 3, 1)
                output(ROUNDS, 0)

            @block.scalar
            def _(act):
                def part(j):
                    return probs[:, quarter(j), :].rearrange("p t k -> p (t k)")

                def tanhs(p, j):
                    act.wait_ge(scores_ready, nth_quarter(p, j))
                    nc.scalar.activation(part(j), banks[:, QUARTER_BANK + j, :], ACT.Tanh,
                                         scale=ATTN_MULT / LOGIT_CAP).then_inc(tanh_done, 1)

                def exps(p, j):
                    act.wait_ge(logits_ready, nth_quarter(p, j))
                    for t in range(4 * j, 4 * j + 4):
                        e = nc.scalar.activation(probs[:, t, :], probs[:, t, :], ACT.Exp, accum_out=total[:, t:t + 1])
                    e.then_inc(exp_done, 1)

                def swap(s, at, nth, first):
                    act.wait_ge(proj_ready, s + 1)
                    if not (isinstance(nth, int) and nth < 2):
                        act.wait_ge(rope_done, nth - 1)
                    h = P // 2
                    nc.scalar.copy(swapped[0:h, nth_par(at), :], banks[h:P, at[0] % PROJ_BANKS, :])
                    nc.scalar.copy(swapped[h:P, nth_par(at), :], banks[0:h, at[0] % PROJ_BANKS, :])\
                        .then_inc(swap_done, 1)

                def nth_par(at):
                    return at[1] % 2

                def rotated_hi(block, nth, at):
                    act.wait_ge(rope_done, nth + 1)
                    nc.scalar.copy(dst(block[1], block[2], 0), turned_by[:, nth_par(at), :]).then_inc(qk_hi, 1)

                def probs_hi(p, j):
                    act.wait_ge(turned, nth_quarter(p, j))
                    if nth_quarter(p, j - 2) is not None:
                        act.wait_ge(pv_ready, nth_quarter(p, j - 2))
                    nc.scalar.copy(pT[0][:, j % 2, :], banks[:, QUARTER_BANK + j, :]).then_inc(pT_hi, 1)

                def attn_hi(p, j):
                    act.wait_ge(pv_ready, nth_quarter(p, j))
                    nc.scalar.copy(att_quarter(0, j), bank_quarter(j)).then_inc(att_hi, 1)

                def weights(kind, n, used=None):
                    act.wait_ge(raw_in[kind], DMA * (n + 1))
                    if used is not None:
                        act.wait_ge(proj_ready, used + 1)
                    nc.scalar.copy(wt[kind][0][:, :], raw[kind][:, :]).then_inc(w_hi[kind], 1)

                def body(r, u, first, last):
                    p = 4 * r + u
                    final_round = isinstance(r, int) and r == ROUNDS - 1
                    blocks = ropes(u)
                    at = [(blk[0], ROPE_AT[u] + i) for i, blk in enumerate(blocks)]
                    nth = [ROPES * r + x[1] for x in at]
                    end = len(blocks) - 1
                    for i, blk in enumerate(blocks):
                        swap(seq(r, u, blk[0]), at[i], nth[i], first)
                        if i == 0 and not first:
                            act.wait_ge(scores_ready, nth_quarter(p, 3, 1))
                        if i and i < end:
                            rotated_hi(blocks[i - 1], nth[i - 1], at[i - 1])
                        if i == end - 1:
                            if not first:
                                probs_hi(p - 1, 0)
                                probs_hi(p - 1, 1)
                    if not first:
                        attn_hi(p - 1, 0)
                        probs_hi(p - 1, 2)
                        attn_hi(p - 1, 1)
                        probs_hi(p - 1, 3)
                    rotated_hi(blocks[end - 1], nth[end - 1], at[end - 1])
                    rotated_hi(blocks[end], nth[end], at[end])
                    if not first:
                        attn_hi(p - 1, 2)
                        attn_hi(p - 1, 3)
                    if not last:
                        weights("Q", p + 1, seq(r, u, Q_AT[u] + 3))
                    if u == 0 or (u == 2 and not final_round):
                        weights("K", 2 * r + u // 2 + 1, seq(r, u, K_AT[u] + 1))
                    softmax(p)
                    if u == 1 and not final_round:
                        weights("V", r + 1, seq(r, 0, V_AT + 3))
                    weights("O", p, None if first else seq_out(r, u, 7))
                    if u == 0:
                        for n in range(4):
                            act.wait_ge(proj_ready, seq(r, 0, V_AT + n) + 1)
                            nc.scalar.copy(v[0][:, 2 * n:2 * n + 2, :].rearrange("p b f -> p (b f)"),
                                           banks[:, (V_AT + n) % PROJ_BANKS, :]).then_inc(v_hi, 1)

                def softmax(p):
                    tanhs(p, 0)
                    tanhs(p, 1)
                    exps(p, 0)
                    tanhs(p, 2)
                    exps(p, 1)
                    tanhs(p, 3)
                    exps(p, 2)
                    exps(p, 3)

                weights("K", 0)
                weights("Q", 0)
                weights("V", 0)
                loop(act, body)
                tail = PAIRS - 1
                probs_hi(tail, 0)
                probs_hi(tail, 1)
                attn_hi(tail, 0)
                probs_hi(tail, 2)
                attn_hi(tail, 1)
                probs_hi(tail, 3)
                attn_hi(tail, 2)
                attn_hi(tail, 3)

            @block.vector
            def _(dve):
                def wide(table):
                    return table[:, :].unsqueeze(1).to_broadcast([P, HB, P])

                def logits(p, j):
                    dve.wait_ge(tanh_done, nth_quarter(p, j))
                    part = probs[:, quarter(j), :]
                    dve.scalar_tensor_tensor(part, part, cap[:, 0:1], wide(mask), ALU.mult, ALU.add)\
                        .then_inc(logits_ready, 1)

                def inverse(p, j):
                    dve.wait_ge(exp_done, nth_quarter(p, j))
                    dve.reciprocal(inv[:, quarter(j)], total[:, quarter(j)]).then_inc(inv_ready, 1)

                def rotate_cos(at, par, nth):
                    dve.wait_ge(swap_done, nth + 1)
                    if not (isinstance(nth, int) and nth < 2):
                        dve.wait_ge(qk_lo, nth - 1)
                    bank = banks[:, at % PROJ_BANKS, :].rearrange("p (b t) -> p b t", b=HB)
                    out = turned_by[:, par, :].rearrange("p (b t) -> p b t", b=HB)
                    dve.tensor_tensor(out, bank, wide(cos), ALU.mult).then_inc(proj_free, 1)

                def rotate_add(s, par, nth):
                    dve.wait_ge(sin_done, nth + 1)
                    dve.wait_ge(proj_free, s + 1)
                    dve.tensor_tensor(turned_by[:, par, :], turned_by[:, par, :], swapped[:, par, :], ALU.add)\
                        .then_inc(rope_done, 1)

                def low(out, src, hi, done):
                    dve.tensor_tensor(out, src, f32(hi), ALU.subtract).then_inc(done, 1)

                def rotated_lo(blk, par, nth):
                    dve.wait_ge(qk_hi, nth + 1)
                    low(dst(blk[1], blk[2], 1), turned_by[:, par, :], dst(blk[1], blk[2], 0), qk_lo)

                def probs_lo(p, j):
                    dve.wait_ge(pT_hi, nth_quarter(p, j))
                    low(pT[1][:, j % 2, :], banks[:, QUARTER_BANK + j, :], pT[0][:, j % 2, :], pT_lo)

                def attn_lo(p, j):
                    dve.wait_ge(att_hi, nth_quarter(p, j))
                    low(att_quarter(1, j), bank_quarter(j), att_quarter(0, j), att_lo)

                def output(r, u, b):
                    dve.wait_ge(proj_ready, seq_out(r, u, b) + 1)
                    dve.tensor_tensor(resid[:, b, :], banks[:, (OUT_AT[u] + b) % PROJ_BANKS, :], resid[:, b, :],
                                      ALU.add).then_inc(proj_free, 1)

                def body(r, u, first, last):
                    p = 4 * r + u
                    blocks = ropes(u)
                    end = len(blocks) - 1

                    def add(i):
                        rotate_add(seq(r, u, blocks[i][0]), (ROPE_AT[u] + i) % 2, ROPES * r + ROPE_AT[u] + i)

                    def split(i):
                        rotated_lo(blocks[i], (ROPE_AT[u] + i) % 2, ROPES * r + ROPE_AT[u] + i)

                    for i, blk in enumerate(blocks):
                        at = ROPE_AT[u] + i
                        if i and i < end:
                            add(i - 1)
                        rotate_cos(blk[0], at % 2, ROPES * r + at)
                        if i and i < end:
                            split(i - 1)
                        if i == end - 1:
                            if not first:
                                probs_lo(p - 1, 0)
                                probs_lo(p - 1, 1)
                            add(i)
                    if not first:
                        attn_lo(p - 1, 0)
                        probs_lo(p - 1, 2)
                    add(end)
                    if not first:
                        attn_lo(p - 1, 1)
                        probs_lo(p - 1, 3)
                    split(end - 1)
                    split(end)
                    if not first:
                        attn_lo(p - 1, 2)
                        attn_lo(p - 1, 3)
                    done = 0
                    for step, j, outs in ((logits, 0, 0), (logits, 1, 1), (logits, 2, 1), (inverse, 0, 0), (logits, 3, 1),
                                          (inverse, 1, 1), (inverse, 2, 1), (inverse, 3, 3)):
                        step(p, j)
                        for _ in range(outs):
                            if not first:
                                output(r, u, done)
                            done = done + 1
                    if u == 0:
                        for n in range(4):
                            dve.wait_ge(v_hi, 4 * r + n + 1)
                            cut = [s[:, 2 * n:2 * n + 2, :].rearrange("p b f -> p (b f)") for s in v]
                            low(cut[1], banks[:, (V_AT + n) % PROJ_BANKS, :], cut[0], proj_free)

                dve.wait_ge(consts_in, 3 * DMA)
                dve.tensor_reduce(some[:, :], mask8[:, :], AX_X, ALU.max).then_inc(mask_steps, 1)
                dve.tensor_scalar(mask_raw[:, :], mask8[:, :], MASKED, -MASKED, ALU.mult, ALU.add).then_inc(mask_steps, 1)
                dve.wait_ge(mask_steps, 2)
                dve.tensor_scalar(cap[:, :], some[:, :], LOGIT_CAP, None, ALU.mult).then_inc(cap_ready, 1)
                dve.tensor_scalar(mask[:, :], mask_raw[:, :], some[:, 0:1], None, ALU.mult).then_inc(mask_ready, 1)
                dve.wait_ge(cap_ready, 1)
                dve.wait_ge(mask_ready, 1)
                loop(dve, body)
                tail = PAIRS - 1
                probs_lo(tail, 0)
                probs_lo(tail, 1)
                attn_lo(tail, 0)
                probs_lo(tail, 2)
                attn_lo(tail, 1)
                probs_lo(tail, 3)
                attn_lo(tail, 2)
                attn_lo(tail, 3)
                for b in range(B):
                    output(ROUNDS, 0, b)

            @block.gpsimd
            def _(pool):
                def weights(kind, n):
                    pool.wait_ge(w_hi[kind], n + 1)
                    pool.tensor_tensor(wt[kind][1][:, :], raw[kind][:, :], f32(wt[kind][0][:, :]), ALU.subtract)\
                        .then_inc(w_lo[kind], 1)

                def normalise(p, j):
                    pool.wait_ge(inv_ready, nth_quarter(p, j))
                    rows = inv[:, quarter(j)].unsqueeze(2).to_broadcast([P, 4, P])
                    pool.tensor_tensor(probs[:, quarter(j), :], probs[:, quarter(j), :], rows, ALU.mult)\
                        .then_inc(probs_ready, 1)

                def rotate_sin(par, nth):
                    pool.wait_ge(swap_done, nth + 1)
                    part = swapped[:, par, :].rearrange("p (b t) -> p b t", b=HB)
                    pool.tensor_tensor(part, part, sin[:, :].unsqueeze(1).to_broadcast([P, HB, P]), ALU.mult)\
                        .then_inc(sin_done, 1)

                def body(r, u, first, last):
                    p = 4 * r + u
                    final_round = isinstance(r, int) and r == ROUNDS - 1
                    for i in range(len(ropes(u))):
                        at = ROPE_AT[u] + i
                        rotate_sin(at % 2, ROPES * r + at)
                    if not last:
                        weights("Q", p + 1)
                    if u == 0 or (u == 2 and not final_round):
                        weights("K", 2 * r + u // 2 + 1)
                    for j in range(4):
                        normalise(p, j)
                    if u == 1 and not final_round:
                        weights("V", r + 1)
                    weights("O", p)

                pool.wait_ge(consts_in, 3 * DMA)
                weights("K", 0)
                weights("Q", 0)
                weights("V", 0)
                loop(pool, body)


def lora_phase(core, io, out):
    nc = core.nc
    resid, xT, banks = core.resid, core.xT, core.banks
    with ExitStack() as ctx:
        sb, pair, sem = core.sb, core.pair, core.sem
        a_raw = sb(ctx, "l_a_raw", [P, D])
        b_raw = sb(ctx, "l_b_raw", [P, D])
        b_scaled = sb(ctx, "l_b_scaled", [P, D])
        coef = sb(ctx, "l_coef", [P, 1])
        a2 = pair(ctx, "l_a", [P, D])
        b2 = pair(ctx, "l_b", [P, D])
        w_raw = sb(ctx, "l_w_raw", [P, DC, D])
        w = pair(ctx, "l_w", [P, DC, D])

        coef_in = sem("l_coef_in")
        ab_in = sem("l_ab_in")
        w_in = sem("l_w_in")
        b_ready = sem("l_b_ready")
        ab_hi = sem("l_ab_hi")
        ab_lo = sem("l_ab_lo")
        folded = sem("l_folded")
        w_sum = sem("l_w_sum")
        w_hi = sem("l_w_hi")
        w_lo = sem("l_w_lo")
        out_ready = sem("l_out_ready")
        added = sem("l_added")
        stored = sem("l_stored")

        with nc.Block() as block:
            @block.sync
            def _(sp):
                sp.dma_start(a_raw[:, :], io["l_a"]).then_inc(ab_in, DMA)
                sp.dma_start(b_raw[:, :], io["l_b"]).then_inc(ab_in, DMA)
                for n in range(LORA // RANK):
                    sp.dma_start(coef[n * RANK:(n + 1) * RANK, :], io["l_coef"][n:n + 1].partition_broadcast(RANK))\
                        .then_inc(coef_in, DMA)
                sp.dma_start(w_raw[:, :, :], io["l_w"].rearrange("(c p) o -> p c o", p=P)).then_inc(w_in, DMA)
                for b in range(B):
                    sp.wait_ge(added, b + 1)
                    sp.dma_start(out[b, :, :], resid[:, b, :]).then_inc(stored, DMA)
                sp.wait_ge(stored, B * DMA)

            @block.tensor
            def _(pe):
                pe.wait_ge(ab_lo, 2)
                for c in range(DC):
                    product(pe, banks[:, c, :], [s[:, tok(c)] for s in a2], [s[:, :] for s in b2], True, True)\
                        .then_inc(folded, 1)
                for b in range(B):
                    if b >= 4:
                        pe.wait_ge(added, b - 3)
                    for c in range(DC):
                        if b == 0:
                            pe.wait_ge(w_lo, c + 1)
                        mm = product(pe, banks[:, 4 + b % 4, :], [s[:, c, tok(b)] for s in xT],
                                     [s[:, c, :] for s in w], c == 0, c == DC - 1)
                    mm.then_inc(out_ready, 1)

            @block.scalar
            def _(act):
                act.wait_ge(ab_in, 2 * DMA)
                nc.scalar.copy(a2[0][:, :], a_raw[:, :]).then_inc(ab_hi, 1)
                act.wait_ge(b_ready, 1)
                nc.scalar.copy(b2[0][:, :], b_scaled[:, :]).then_inc(ab_hi, 1)
                for c in range(DC):
                    act.wait_ge(w_sum, c + 1)
                    nc.scalar.copy(w[0][:, c, :], w_raw[:, c, :]).then_inc(w_hi, 1)

            @block.vector
            def _(dve):
                dve.wait_ge(ab_in, 2 * DMA)
                dve.wait_ge(coef_in, LORA // RANK * DMA)
                dve.tensor_scalar(b_scaled[:, :], b_raw[:, :], coef[:, 0:1], LORA_SCALE, ALU.mult, ALU.mult)\
                    .then_inc(b_ready, 1)
                for n, (src, dst) in enumerate(((a_raw, a2), (b_scaled, b2))):
                    dve.wait_ge(ab_hi, n + 1)
                    dve.tensor_tensor(dst[1][:, :], src[:, :], f32(dst[0][:, :]), ALU.subtract).then_inc(ab_lo, 1)
                dve.wait_ge(w_in, DMA)
                for c in range(DC):
                    dve.wait_ge(folded, c + 1)
                    dve.tensor_tensor(w_raw[:, c, :], banks[:, c, :], w_raw[:, c, :], ALU.add).then_inc(w_sum, 1)
                for c in range(DC):
                    dve.wait_ge(w_hi, c + 1)
                    dve.tensor_tensor(w[1][:, c, :], w_raw[:, c, :], f32(w[0][:, c, :]), ALU.subtract)\
                        .then_inc(w_lo, 1)
                for b in range(B):
                    dve.wait_ge(out_ready, b + 1)
                    dve.tensor_tensor(resid[:, b, :], banks[:, 4 + b % 4, :], resid[:, b, :], ALU.add)\
                        .then_inc(added, 1)


def store_phase(core, out):
    nc = core.nc
    stored = core.sem("stored")
    with nc.Block() as block:
        @block.sync
        def _(sp):
            sp.dma_start(out.rearrange("b p d -> p b d"), core.resid[:, :, :]).then_inc(stored, DMA)
            sp.wait_ge(stored, DMA)


def build(nc, io, out, STAGES=9):
    with ExitStack() as ctx:
        core = Core(nc, ctx)
        normalise_phase(core, "n0", first={"x": io["x"], "ident": io["ident"], "ln_w": io["x_ln_w"], "ctxT": io["ctxT"]})
        if STAGES >= 1:
            cross_attention_phase(core, {"mask": io["x_mask"], "bias": io["x_bias"], "wA": io["x_wA"], "wB": io["x_wB"],
                                         "wV": io["x_wV"], "wO": io["x_wO"]})
        if STAGES >= 2:
            normalise_phase(core, "n1", after=io["f_b_down"])
            ffn_phase(core, io)
        if STAGES >= 3:
            normalise_phase(core, "n2")
            grouped_attention_phase(core, io)
        if STAGES >= 4:
            normalise_phase(core, "n3", after=io["l_bias"])
            lora_phase(core, io, out)
        else:
            store_phase(core, out)


def head_weights(w):
    return w.reshape(DC, P, -1, P).transpose(2, 1, 0, 3)


def pair_columns(w):
    return w.reshape(DC, P, -1, 2 * P).transpose(2, 1, 0, 3).reshape(-1, P, DC * 2 * P)


def pair_rows(w):
    return w.reshape(-1, 2, P, D).transpose(0, 2, 1, 3).reshape(-1, P, 2 * D)


def lay_out(a):
    q = head_weights(a["L0_xattn_w_q"].T)
    k = head_weights(a["L0_xattn_w_k"].T)
    qk = np.stack([q, k], 2).reshape(HEADS, P, 2 * DC * P)
    io = {
        "x": a["x"],
        "ctxT": a["ctx_4096"].reshape(TOK, D).T,
        "ident": np.eye(P, dtype=np.float32),
        "x_ln_w": a["L0_xattn_ln_weight"],
        "x_mask": a["mask_BxSxS2_bk0"],
        "x_bias": a["L0_xattn_position_bias"].reshape(PAIRS, 2, P, P),
        "x_wA": qk[0::2],
        "x_wB": qk[1::2],
        "x_wV": pair_columns(a["L0_xattn_w_v"].T),
        "x_wO": pair_rows(a["L0_xattn_w_out"].T),
    }
    io.update(lay_out_more(a))
    return {n: np.ascontiguousarray(v) for n, v in io.items()}


def lay_out_more(a):
    gate, up, down = (a["L0_ffn_w_" + n].T for n in ("gate", "up", "down"))
    full = FULL * P
    gu = np.stack([head_weights(gate[:, :full]), head_weights(up[:, :full])], 2)
    rest = np.stack([m[:, full:].reshape(DC, P, REST).transpose(1, 0, 2) for m in (gate, up)], 1)
    biases = np.stack([a["L0_ffn_b_gate"], a["L0_ffn_b_up"]], 1)
    inv_freq = np.float32(1.0) / np.float32(10000.0) ** (np.arange(0, P, 2, dtype=np.float32) / np.float32(P))
    phase = np.tile(np.arange(P, dtype=np.float32)[:, None] * inv_freq[None, :], (1, 2)).T
    sign = np.where(np.arange(P) < P // 2, -1, 1).astype(np.float32)[:, None]
    return {
        "f_gu": gu.reshape(FULL, P, 2 * DC * P),
        "f_gu_rest": rest.reshape(P, 2 * DC * REST),
        "f_d": down[:full].reshape(FULL, P, D),
        "f_d_rest": down[full:],
        "f_b": biases[:full].reshape(FULL, P, 2),
        "f_b_rest": biases[full:],
        "f_b_down": a["L0_ffn_b_down"],
        "g_mask": a["mask_1x1xSxS2_bk0"].reshape(P, P),
        "g_cos": np.cos(phase),
        "g_sin": np.sin(phase) * sign,
        "g_wQ": head_weights(a["L1_xattn_Wq"]).reshape(PAIRS, 2, P, DC * P).transpose(0, 2, 1, 3)
        .reshape(PAIRS, P, 2 * DC * P),
        "g_wK": head_weights(a["L1_xattn_Wk"]).reshape(KV_HEADS, P, DC * P),
        "g_wV": pair_columns(a["L1_xattn_Wv"]),
        "g_wO": pair_rows(a["L1_xattn_Wo"]),
        "l_a": a["L1_ffn_lora_A"].reshape(LORA, D),
        "l_b": a["L1_ffn_lora_B"].transpose(0, 2, 1).reshape(LORA, D),
        "l_coef": a["L1_ffn_lora_weights"],
        "l_w": a["L1_ffn_W"].T,
        "l_bias": a["L1_ffn_bias"],
    }


def kernel(**inputs):
    import concourse.bacc as bacc
    from concourse.bass_utils import run_bass_kernel_spmd

    arrays = lay_out({n: np.asarray(v) for n, v in inputs.items()})
    nc = bacc.Bacc("TRN2", target_bir_lowering=False, num_devices=1)
    io = {n: nc.dram_tensor("in_" + n, v.shape, mybir.dt.from_np(v.dtype), kind="ExternalInput").ap()
          for n, v in arrays.items()}
    out = nc.dram_tensor("out", (B, P, D), F32, kind="ExternalOutput").ap()
    build(nc, io, out)
    run = run_bass_kernel_spmd(nc, [{"in_" + n: v for n, v in arrays.items()}], core_ids=[0])
    return np.asarray(run.results[0]["out"])
```

```python
from contextlib import ExitStack

import numpy as np
import concourse.bass as bass
from concourse import mybir

F32 = mybir.dt.float32
F32R = mybir.dt.float32r
U8 = mybir.dt.uint8
ALU = mybir.AluOpType
ACT = mybir.ActivationFunctionType
AX_X = mybir.AxisListType.X

P = 128
B = 8
D = 512
DC = D // P
TOK = B * P
HALF = TOK // 2
HB = B // 2
HEADS = 32
KV_HEADS = 8
PAIRS = HEADS // 2
INTER = 1376
FULL = INTER // P
REST = INTER - FULL * P
LORA = 128
RANK = 16
LORA_SCALE = 2.0
EPS = 1e-5
MASKED = 1e30
LOGIT_CAP = 30.0
ATTN_MULT = 0.08838834764831845
WEIGHTS = 2 * D
DMA = 16


def f32(ap):
    return ap.bitcast(F32)


def product(pe, out, w, x, start, stop):
    pe.matmul(out, w[1], x[0], start=start, stop=False)
    pe.matmul(out, w[0], x[1], start=False, stop=False)
    return pe.matmul(out, w[0], x[0], start=False, stop=stop)


def tok(b, n=1):
    return slice(b * P, (b + n) * P)


class Core:

    KINDS = ("A", "B", "V", "O")

    def __init__(self, nc, ctx):
        self.nc, self.ctx = nc, ctx
        self.banks = ctx.enter_context(nc.psum_tensor("banks", [P, 8, 512], F32))
        self.resid = self.sb(ctx, "resid", [P, B, D], F32)
        self.xT = self.pair(ctx, "xT", [P, DC, TOK])
        self.cT = self.pair(ctx, "cT", [P, DC, TOK])
        self.ident = self.sb(ctx, "ident", [P, P], F32)
        self.raw = {k: self.sb(ctx, "raw" + k, [P, WEIGHTS]) for k in self.KINDS}
        self.wt = {k: self.pair(ctx, "wt" + k, [P, WEIGHTS]) for k in self.KINDS}
        self.stats = self.sb(ctx, "stats", [P, B, 6])
        self.moments = self.sb(ctx, "moments", [P, B, 2])
        self.var_eps = self.sb(ctx, "var_eps", [P, B])
        self.rstd = self.sb(ctx, "rstd", [P, B])
        self.power = self.sb(ctx, "power", [P, B])
        self.normed = self.sb(ctx, "normed", [P, 2, D])
        self.row = self.sb(ctx, "row", [P, D])

    def sb(self, ctx, name, shape, dt=F32):
        return ctx.enter_context(self.nc.sbuf_tensor(name, shape, dt))

    def pair(self, ctx, name, shape):
        return (self.sb(ctx, name + "_hi", shape, F32R), self.sb(ctx, name + "_lo", shape, F32R))

    def sem(self, name):
        return self.ctx.enter_context(self.nc.semaphore(name))


class Early:

    def __init__(self, core, tag, names, loads):
        self.core, self.loads = core, loads
        self.raw_in = {k: core.sem(tag + "_raw_in" + k) for k in names}
        self.w_hi = {k: core.sem(tag + "_w_hi" + k) for k in names}
        self.w_lo = {k: core.sem(tag + "_w_lo" + k) for k in names}

    def load(self, sp, free=None):
        for kind, name, src, n in self.loads:
            for sem, value in (free or {}).get(kind, ()):
                sp.wait_ge(sem, value)
            sp.dma_start(self.core.raw[kind][:, 0:n], src).then_inc(self.raw_in[name], DMA)

    def split_hi(self, act, used=None):
        for kind, name, src, n in self.loads:
            act.wait_ge(self.raw_in[name], DMA)
            if used:
                act.wait_ge(*used[kind])
            self.core.nc.scalar.copy(self.core.wt[kind][0][:, 0:n], self.core.raw[kind][:, 0:n])\
                .then_inc(self.w_hi[name], 1)

    def split_lo(self, pool, kinds=None):
        for kind, name, src, n in self.loads:
            if kinds is not None and kind not in kinds:
                continue
            pool.wait_ge(self.w_hi[name], 1)
            pool.tensor_tensor(self.core.wt[kind][1][:, 0:n], self.core.raw[kind][:, 0:n],
                               f32(self.core.wt[kind][0][:, 0:n]), ALU.subtract).then_inc(self.w_lo[name], 1)


class Norm:

    BANK = 4

    def __init__(self, core, tag, row, complete, banks_free=None):
        self.core, self.row_src, self.complete, self.banks_free = core, row, complete, banks_free
        self.stats_done = core.sem(tag + "_stats_done")
        self.moments_done = core.sem(tag + "_moments_done")
        self.var_ready = core.sem(tag + "_var_ready")
        self.rstd_ready = core.sem(tag + "_rstd_ready")
        self.normed_ready = core.sem(tag + "_normed_ready")
        self.turned = core.sem(tag + "_turned")
        self.hi_ready = core.sem(tag + "_hi_ready")
        self.lo_ready = core.sem(tag + "_lo_ready")
        self.row_in = core.sem(tag + "_row_in")
        self.row_added = core.sem(tag + "_row_added")

    def load_row(self, sp):
        if self.row_src is not None:
            sp.dma_start(self.core.row[:, :], self.row_src.partition_broadcast(P)).then_inc(self.row_in, DMA)

    def statistics(self, dve, b):
        core = self.core
        dve.wait_ge(self.complete[0], self.complete[1] + b + 1)
        dve.bn_stats(core.stats[:, b, :], core.resid[:, b, :]).then_inc(self.stats_done, 1)

    def mean_and_variance(self, dve, b):
        dve.wait_ge(self.stats_done, b + 1)
        dve.bn_aggr(self.core.moments[:, b, :], self.core.stats[:, b, :]).then_inc(self.moments_done, 1)

    def reciprocal_std(self, pool, b):
        core = self.core
        one = slice(b, b + 1)
        pool.wait_ge(self.moments_done, b + 1)
        pool.tensor_scalar(core.var_eps[:, one], core.moments[:, b, 1:2], EPS, None, ALU.add).then_inc(self.var_ready, 1)
        pool.wait_ge(self.var_ready, b + 1)
        pool.tensor_tensor(core.rstd[:, one], core.var_eps[:, one], core.power[:, one], ALU.pow)\
            .then_inc(self.rstd_ready, 1)

    def add_rows(self, pool):
        core = self.core
        pool.wait_ge(self.row_in, DMA)
        for b in range(B):
            pool.tensor_tensor(core.resid[:, b, :], core.resid[:, b, :], core.row[:, :], ALU.add)\
                .then_inc(self.row_added, 1)

    def scale(self, dve, b):
        core = self.core
        dve.wait_ge(self.rstd_ready, b + 1)
        if b >= 2:
            dve.wait_ge(self.turned, b - 1)
        dve.tensor_scalar(core.normed[:, b % 2, :], core.resid[:, b, :], core.moments[:, b, 0:1],
                          core.rstd[:, b:b + 1], ALU.subtract, ALU.mult).then_inc(self.normed_ready, 1)

    def turn(self, pe, b):
        core = self.core
        pe.wait_ge(self.normed_ready, b + 1)
        if b >= 4:
            pe.wait_ge(self.lo_ready, b - 3)
        elif self.banks_free is not None:
            pe.wait_ge(*self.banks_free)
        for c in range(DC):
            mm = pe.transpose(core.banks[:, self.BANK + b % 4, tok(c)], core.normed[:, b % 2, tok(c)], core.ident[:, :])
        mm.then_inc(self.turned, 1)

    def bank(self, b):
        return self.core.banks[:, self.BANK + b % 4, :].rearrange("p (c t) -> p c t", c=DC)

    def high(self, act, b):
        act.wait_ge(self.turned, b + 1)
        self.core.nc.scalar.copy(self.core.xT[0][:, :, tok(b)], self.bank(b)).then_inc(self.hi_ready, 1)

    def low(self, dve, b):
        dve.wait_ge(self.hi_ready, b + 1)
        xT = self.core.xT
        dve.tensor_tensor(xT[1][:, :, tok(b)], self.bank(b), f32(xT[0][:, :, tok(b)]), ALU.subtract)\
            .then_inc(self.lo_ready, 1)


    def weave_tensor(self, pe, step):
        lag = 3
        for b in range(B + lag):
            if b < B:
                step(b)
            if b >= lag:
                self.turn(pe, b - lag)

    def weave_vector(self, dve, step):
        for b in range(B + 4):
            if b < B:
                step(b)
            if b >= 4:
                self.low(dve, b - 4)
            if b < B:
                self.statistics(dve, b)
            if 1 <= b <= B:
                self.scale(dve, b - 1)
            if b < B:
                self.mean_and_variance(dve, b)

    def weave_scalar(self, act):
        for b in range(B):
            self.high(act, b)

    def weave_gpsimd(self, pool, step=None):
        for b in range(B):
            self.reciprocal_std(pool, b)
            if step and b >= 3:
                step(b - 3)


def first_phase(core, io, after):
    nc = core.nc
    resid, xT, cT, ident = core.resid, core.xT, core.cT, core.ident
    stats, moments, var_eps, rstd, power = core.stats, core.moments, core.var_eps, core.rstd, core.power
    normed, ln_w = core.normed, core.row
    with ExitStack() as ctx:
        hidden = core.sb(ctx, "i_hidden", [P, B, D])
        rms = core.sb(ctx, "i_rms", [P, B])
        mean_square = core.sb(ctx, "i_mean_square", [P, B])
        ctx_raw = core.sb(ctx, "i_ctx_raw", [P, DC, TOK])

        x_in = [core.sem(f"i_x_in{n}") for n in range(4)]
        ident_in = core.sem("i_ident_in")
        ln_in = core.sem("i_ln_in")
        ctx_in = [core.sem(f"i_ctx_in{n}") for n in range(DC)]
        ctx_hi = core.sem("i_ctx_hi")
        ctx_lo = core.sem("i_ctx_lo")
        ctx_lo2 = core.sem("i_ctx_lo2")
        power_set = core.sem("i_power_set")
        stats_done = core.sem("i_stats_done")
        moments_done = core.sem("i_moments_done")
        var_ready = core.sem("i_var_ready")
        rstd_ready = core.sem("i_rstd_ready")
        square_steps = core.sem("i_square_steps")
        rms_ready = core.sem("i_rms_ready")
        hidden_ready = core.sem("i_hidden_ready")
        normed_ready = core.sem("i_normed_ready")
        turned = core.sem("i_turned")
        hi_ready = core.sem("i_hi_ready")
        lo_ready = core.sem("i_lo_ready")

        def bank(b):
            return core.banks[:, 4 + b % 4, :].rearrange("p (c t) -> p c t", c=DC)

        with nc.Block() as block:
            @block.sync
            def _(sp):
                x4 = io["x"].rearrange("b p d -> p b d")
                c4 = io["ctxT"].rearrange("(c p) t -> p c t", p=P)
                for n in range(4):
                    sp.dma_start(resid[:, 2 * n:2 * n + 2, :], x4[:, 2 * n:2 * n + 2, :]).then_inc(x_in[n], DMA)
                    if n == 0:
                        sp.dma_start(ln_w[:, :], io["x_ln_w"].partition_broadcast(P)).then_inc(ln_in, DMA)
                        sp.dma_start(ident[:, :], io["ident"]).then_inc(ident_in, DMA)
                after.load(sp)
                for c in range(DC):
                    sp.dma_start(ctx_raw[:, c, :], c4[:, c, :]).then_inc(ctx_in[c], DMA)

            @block.vector
            def _(dve):
                def statistics(n):
                    dve.wait_ge(x_in[n], DMA)
                    for b in (2 * n, 2 * n + 1):
                        dve.bn_stats(stats[:, b, :], resid[:, b, :]).then_inc(stats_done, 1)
                    for b in (2 * n, 2 * n + 1):
                        dve.wait_ge(stats_done, b + 1)
                        dve.bn_aggr(moments[:, b, :], stats[:, b, :]).then_inc(moments_done, 1)

                def hide(b):
                    dve.wait_ge(rstd_ready, b // 2 + 1)
                    dve.tensor_scalar(hidden[:, b, :], resid[:, b, :], moments[:, b, 0:1], rstd[:, b:b + 1],
                                      ALU.subtract, ALU.mult).then_inc(hidden_ready, 1)

                def scale(b):
                    dve.wait_ge(rms_ready, b // 2 + 1)
                    dve.wait_ge(hidden_ready, b + 1)
                    if b >= 2:
                        dve.wait_ge(turned, b - 1)
                    dve.scalar_tensor_tensor(normed[:, b % 2, :], hidden[:, b, :], rms[:, b:b + 1], ln_w[:, :],
                                             ALU.mult, ALU.mult).then_inc(normed_ready, 1)

                def low(b):
                    dve.wait_ge(hi_ready, b + 1)
                    dve.tensor_tensor(xT[1][:, :, tok(b)], bank(b), f32(xT[0][:, :, tok(b)]), ALU.subtract)\
                        .then_inc(lo_ready, 1)

                statistics(0)
                statistics(1)
                for n in range(4):
                    hide(2 * n)
                    hide(2 * n + 1)
                    if n == 0:
                        dve.wait_ge(ln_in, DMA)
                        statistics(2)
                    if n == 1:
                        statistics(3)
                    if n:
                        low(2 * n - 2)
                    scale(2 * n)
                    if n:
                        low(2 * n - 1)
                    scale(2 * n + 1)
                low(B - 2)
                low(B - 1)
                for c in range(3, DC):
                    dve.wait_ge(ctx_hi, c + 1)
                    dve.tensor_tensor(cT[1][:, c, :], ctx_raw[:, c, :], f32(cT[0][:, c, :]), ALU.subtract)\
                        .then_inc(ctx_lo2, 1)

            @block.gpsimd
            def _(pool):
                pool.memset(power[:, :], -0.5).then_inc(power_set, 1)
                pool.wait_ge(power_set, 1)
                for n in range(4):
                    two = slice(2 * n, 2 * n + 2)
                    pool.wait_ge(moments_done, 2 * n + 2)
                    pool.tensor_scalar(var_eps[:, two], moments[:, two, 1], EPS, None, ALU.add).then_inc(var_ready, 1)
                    pool.wait_ge(var_ready, n + 1)
                    pool.tensor_tensor(rstd[:, two], var_eps[:, two], power[:, two], ALU.pow).then_inc(rstd_ready, 1)
                    pool.wait_ge(rstd_ready, n + 1)
                    pool.tensor_tensor(mean_square[:, two], moments[:, two, 1], rstd[:, two], ALU.mult)\
                        .then_inc(square_steps, 1)
                    pool.wait_ge(square_steps, 3 * n + 1)
                    pool.tensor_tensor(mean_square[:, two], mean_square[:, two], rstd[:, two], ALU.mult)\
                        .then_inc(square_steps, 1)
                    pool.wait_ge(square_steps, 3 * n + 2)
                    pool.tensor_scalar(mean_square[:, two], mean_square[:, two], EPS, None, ALU.add)\
                        .then_inc(square_steps, 1)
                    pool.wait_ge(square_steps, 3 * n + 3)
                    pool.tensor_tensor(rms[:, two], mean_square[:, two], power[:, two], ALU.pow).then_inc(rms_ready, 1)
                after.split_lo(pool, ("A",))
                for c in range(3):
                    pool.wait_ge(ctx_hi, c + 1)
                    pool.tensor_tensor(cT[1][:, c, :], ctx_raw[:, c, :], f32(cT[0][:, c, :]), ALU.subtract)\
                        .then_inc(ctx_lo, 1)

            @block.tensor
            def _(pe):
                pe.wait_ge(ident_in, DMA)
                for b in range(B):
                    pe.wait_ge(normed_ready, b + 1)
                    if b >= 4:
                        pe.wait_ge(lo_ready, b - 3)
                    for c in range(DC):
                        mm = pe.transpose(core.banks[:, 4 + b % 4, tok(c)], normed[:, b % 2, tok(c)], ident[:, :])
                    mm.then_inc(turned, 1)

            @block.scalar
            def _(act):
                def high(b):
                    act.wait_ge(turned, b + 1)
                    nc.scalar.copy(xT[0][:, :, tok(b)], bank(b)).then_inc(hi_ready, 1)

                def context(c):
                    act.wait_ge(ctx_in[c], DMA)
                    nc.scalar.copy(cT[0][:, c, :], ctx_raw[:, c, :]).then_inc(ctx_hi, 1)

                high(0)
                high(1)
                after.split_hi(act)
                context(0)
                high(2)
                high(3)
                context(1)
                high(4)
                high(5)
                context(2)
                high(6)
                high(7)
                context(3)


PROJ_BANKS = 4
SCORE_BANK = 4
TURN_BANK = 6
QUARTER_BANK = 4


def cross_attention_phase(core, io, weights_early, norm_row, after):
    nc = core.nc
    resid, xT, cT, ident, banks = core.resid, core.xT, core.cT, core.ident, core.banks
    with ExitStack() as ctx:
        sb, pair, sem = core.sb, core.pair, core.sem
        raw, wt = core.raw, core.wt
        q = pair(ctx, "x_q", [P, TOK])
        k_ = pair(ctx, "x_k", [P, TOK])
        v = pair(ctx, "x_v", [P, B, 2 * P])
        att = pair(ctx, "x_att", [P, 2, TOK])
        pT = pair(ctx, "x_pT", [P, 2, HALF])
        probs = sb(ctx, "x_probs", [P, B, P])
        bias_in = sb(ctx, "x_bias", [P, 2, P])
        biased = sb(ctx, "x_biased", [P, B, P])
        mask8 = sb(ctx, "x_mask8", [P, B, P], U8)
        mask = sb(ctx, "x_mask", [P, B, P])
        some = sb(ctx, "x_some", [P, B])
        top = sb(ctx, "x_top", [P, B])
        total = sb(ctx, "x_total", [P, B])
        inv = sb(ctx, "x_inv", [P, B])

        raw_in, w_hi, w_lo = weights_early.raw_in, weights_early.w_hi, weights_early.w_lo
        bias_loaded = sem("x_bias_loaded")
        mask_in = sem("x_mask_in")
        hidden_ready = sem("x_hidden_ready")
        hidden_added = sem("x_hidden_added")
        mask_ready = sem("x_mask_ready")
        some_ready = sem("x_some_ready")
        biased_ready = sem("x_biased_ready")
        proj_ready = sem("x_proj_ready")
        proj_free = sem("x_proj_free")
        qkv_hi = sem("x_qkv_hi")
        scores_ready = sem("x_scores_ready")
        logits_ready = sem("x_logits_ready")
        top_ready = sem("x_top_ready")
        exp_done = sem("x_exp_done")
        raw_inv = sem("x_raw_inv")
        inv_ready = sem("x_inv_ready")
        probs_ready = sem("x_probs_ready")
        turned = sem("x_turned")
        pT_hi = sem("x_pT_hi")
        pT_lo = sem("x_pT_lo")
        pv_ready = sem("x_pv_ready")
        att_hi = sem("x_att_hi")
        att_lo = sem("x_att_lo")

        PER = 20

        def seq_a(g, n):
            return (PER * g - 8 if not isinstance(g, int) or g else 0) + n

        def is_last(g):
            return isinstance(g, int) and g == PAIRS - 1

        def seq_out(g, n):
            if isinstance(g, int) and g == PAIRS:
                return PER * g - 8 + n
            return PER * g + (4 if is_last(g) else -4) + n

        def seq_v(g, n):
            return PER * g + (-4 if is_last(g) else 4) + n

        def seq_b(g, n):
            return PER * g + (0 if is_last(g) else 8) + n

        norm = Norm(core, "n1", norm_row, (proj_free, seq_out(PAIRS, 0)), (att_lo, 4 * PAIRS))

        def wqk(kind, hl, which, c):
            return wt[kind][hl][:, (which * DC + c) * P:(which * DC + c + 1) * P]

        def loop(engine, body):
            body(0, True, False)
            loop_rest(engine, body)

        def loop_rest(engine, body):
            with engine.Fori(1, PAIRS - 1) as g:
                body(g, False, False)
            body(PAIRS - 1, False, True)

        with nc.Block() as block:
            @block.sync
            def _(sp):
                sp.dma_start(mask8[:, :, :], io["mask"].rearrange("b q k -> q b k")).then_inc(mask_in, DMA)

                def load(kind, g, first):
                    if not first:
                        sp.wait_ge(w_hi[kind], g)
                        sp.wait_ge(w_lo[kind], g)
                    src = io["w" + kind]
                    sp.dma_start(raw[kind][:, :], src[bass.ds(g, 1), :, :].rearrange("o p n -> p (o n)"))\
                        .then_inc(raw_in[kind], DMA)

                def body(g, first, last):
                    if not first:
                        load("A", g, first)
                    if not first:
                        sp.wait_ge(biased_ready, 2 * g)
                    sp.dma_start(bias_in[:, :, :],
                                 io["bias"][bass.ds(g, 1)].rearrange("o h q k -> q (o h) k")).then_inc(bias_loaded, DMA)
                    if not first:
                        load("V", g, first)
                        load("B", g, first)
                    load("O", g, first)

                norm.load_row(sp)
                loop(sp, body)
                after.load(sp, {k: ((w_hi[k], PAIRS), (w_lo[k], PAIRS)) for k in core.KINDS})

            @block.tensor
            def _(pe):
                def bank_free(s):
                    if not isinstance(s, int) or s >= PROJ_BANKS:
                        pe.wait_ge(proj_free, s - PROJ_BANKS + 1)

                def qk(kind, seq, n):
                    which, half = n // 2, n % 2
                    src = xT if which == 0 else cT
                    bank_free(seq)
                    for c in range(DC):
                        mm = product(pe, banks[:, n, :], (wqk(kind, 0, which, c), wqk(kind, 1, which, c)),
                                     [s[:, c, half * HALF:(half + 1) * HALF] for s in src], c == 0, c == DC - 1)
                    mm.then_inc(proj_ready, 1)

                def values(g):
                    pe.wait_ge(w_hi["V"], g + 1)
                    pe.wait_ge(w_lo["V"], g + 1)
                    for n in range(4):
                        bank_free(seq_v(g, n))
                        for t in range(2):
                            b = 2 * n + t
                            for c in range(DC):
                                mm = product(pe, banks[:, n, t * 256:(t + 1) * 256], [s[:, c, tok(b)] for s in cT],
                                             [w[:, c * 256:(c + 1) * 256] for w in wt["V"]], c == 0, c == DC - 1)
                        mm.then_inc(proj_ready, 1)

                def scores(n, j, seq, first=False):
                    pe.wait_ge(proj_free, seq + 1)
                    if not first:
                        pe.wait_ge(top_ready, 2 * n + j - 1)
                    for i in range(HB):
                        b = HB * j + i
                        mm = product(pe, banks[:, SCORE_BANK + j, tok(i)], [s[:, tok(b)] for s in q],
                                     [s[:, tok(b)] for s in k_], True, True)
                    mm.then_inc(scores_ready, 1)

                def turn(n, j, first=False):
                    pe.wait_ge(probs_ready, 2 * n + j + 1)
                    if not first:
                        pe.wait_ge(att_lo, 2 * n + j - 1)
                    for i in range(HB):
                        mm = pe.transpose(banks[:, TURN_BANK + j, tok(i)], probs[:, HB * j + i, :], ident[:, :])
                    mm.then_inc(turned, 1)

                def pv(n, j, slot, g):
                    pe.wait_ge(pT_lo, 2 * n + j + 1)
                    pe.wait_ge(proj_free, seq_v(g, 3) + 1)
                    for i in range(HB):
                        b = HB * j + i
                        mm = product(pe, banks[:, TURN_BANK + j, tok(i)], [s[:, b, tok(slot)] for s in v],
                                     [s[:, j, tok(i)] for s in pT], True, True)
                    mm.then_inc(pv_ready, 1)

                def output(g):
                    pe.wait_ge(w_hi["O"], g)
                    pe.wait_ge(w_lo["O"], g)
                    for b in range(B):
                        output_batch(g, b)

                def output_batch(g, b):
                    if b % HB == 0:
                        pe.wait_ge(att_lo, 4 * g + b // HB - 1)
                    bank_free(seq_out(g, b))
                    for h in range(2):
                        mm = product(pe, banks[:, b % PROJ_BANKS, :], [s[:, h, tok(b)] for s in att],
                                     [w[:, h * D:(h + 1) * D] for w in wt["O"]], h == 0, h == 1)
                    mm.then_inc(proj_ready, 1)

                def body(g, first, last):
                    a, bb = 2 * g, 2 * g + 1
                    pe.wait_ge(w_hi["A"], g + 1)
                    pe.wait_ge(w_lo["A"], g + 1)
                    qk("A", seq_a(g, 0), 0)
                    qk("A", seq_a(g, 1), 1)
                    qk("A", seq_a(g, 2), 2)
                    if not first:
                        turn(a - 1, 0)
                    qk("A", seq_a(g, 3), 3)
                    if not first:
                        turn(a - 1, 1)
                    scores(a, 0, seq_a(g, 2), first)
                    if not first:
                        pv(a - 1, 0, 1, g - 1)
                    scores(a, 1, seq_a(g, 3), first)
                    if not first:
                        pv(a - 1, 1, 1, g - 1)
                        if not last:
                            output(g)
                    values(g)
                    pe.wait_ge(w_hi["B"], g + 1)
                    pe.wait_ge(w_lo["B"], g + 1)
                    qk("B", seq_b(g, 0), 0)
                    turn(a, 0, first)
                    qk("B", seq_b(g, 1), 1)
                    turn(a, 1, first)
                    qk("B", seq_b(g, 2), 2)
                    qk("B", seq_b(g, 3), 3)
                    for half in range(2):
                        if not last:
                            pv(a, half, 0, g)
                        scores(bb, half, seq_b(g, 2 + half))
                    if last:
                        output(g)
                        pv(a, 0, 0, g)
                        pv(a, 1, 0, g)

                loop(pe, body)
                tail = HEADS - 1
                turn(tail, 0)
                turn(tail, 1)
                pv(tail, 0, 1, PAIRS - 1)
                pv(tail, 1, 1, PAIRS - 1)
                pe.wait_ge(w_hi["O"], PAIRS)
                pe.wait_ge(w_lo["O"], PAIRS)
                norm.weave_tensor(pe, lambda b: output_batch(PAIRS, b))

            @block.scalar
            def _(act):
                def exps(n, j):
                    act.wait_ge(top_ready, 2 * n + j + 1)
                    for i in range(HB):
                        b = HB * j + i
                        e = nc.scalar.activation(probs[:, b, :], probs[:, b, :], ACT.Exp, bias=top[:, b:b + 1],
                                                 accum_out=total[:, b:b + 1])
                    e.then_inc(exp_done, 1)

                def keep(dst, bank, seq, done):
                    act.wait_ge(proj_ready, seq + 1)
                    nc.scalar.copy(dst, banks[:, bank, :]).then_inc(done, 1)

                def qk(seq, n, head, first=False):
                    if n == 0 and not first:
                        act.wait_ge(scores_ready, 2 * head)
                    dst = (q if n < 2 else k_)[0]
                    keep(dst[:, (n % 2) * HALF:(n % 2 + 1) * HALF], n, seq, qkv_hi)

                def probs_hi(n, j, first=False):
                    act.wait_ge(turned, 2 * n + j + 1)
                    if not first:
                        act.wait_ge(pv_ready, 2 * n + j - 1)
                    nc.scalar.copy(pT[0][:, j, :], banks[:, TURN_BANK + j, :]).then_inc(pT_hi, 1)

                def attn_hi(n, j, slot):
                    act.wait_ge(pv_ready, 2 * n + j + 1)
                    nc.scalar.copy(att[0][:, slot, j * HALF:(j + 1) * HALF], banks[:, TURN_BANK + j, :])\
                        .then_inc(att_hi, 1)

                def weights(kind, g, used=None):
                    act.wait_ge(raw_in[kind], DMA * (g + 1))
                    if used is not None:
                        act.wait_ge(proj_ready, used + 1)
                    nc.scalar.copy(wt[kind][0][:, :], raw[kind][:, :]).then_inc(w_hi[kind], 1)

                def body(g, first, last):
                    a = 2 * g
                    if not first:
                        exps(a - 1, 0)
                        exps(a - 1, 1)
                    qk(seq_a(g, 0), 0, a, first)
                    qk(seq_a(g, 1), 1, a)
                    qk(seq_a(g, 2), 2, a)
                    if not first:
                        probs_hi(a - 1, 0)
                    qk(seq_a(g, 3), 3, a)
                    if not first:
                        probs_hi(a - 1, 1)
                        attn_hi(a - 1, 0, 1)
                        attn_hi(a - 1, 1, 1)
                    exps(a, 0)
                    exps(a, 1)
                    if not last:
                        weights("A", g + 1, seq_a(g, 3))
                    if not last:
                        weights("O", g, None if first else seq_out(g, 7))
                    for n in range(4):
                        if n == 0 and not first:
                            act.wait_ge(pv_ready, 4 * g)
                        keep(v[0][:, 2 * n:2 * n + 2, :].rearrange("p b f -> p (b f)"), n, seq_v(g, n), qkv_hi)
                    qk(seq_b(g, 0), 0, a + 1)
                    probs_hi(a, 0, first)
                    qk(seq_b(g, 1), 1, a + 1)
                    probs_hi(a, 1, first)
                    qk(seq_b(g, 2), 2, a + 1)
                    qk(seq_b(g, 3), 3, a + 1)
                    if not last:
                        if not first:
                            act.wait_ge(proj_ready, seq_out(g, 7) + 1)
                        attn_hi(a, 0, 0)
                        attn_hi(a, 1, 0)
                        weights("V", g + 1, seq_v(g, 3))
                        weights("B", g + 1, seq_b(g, 3))

                loop(act, body)
                tail = HEADS - 1
                exps(tail, 0)
                exps(tail, 1)
                used = {"A": (proj_ready, seq_a(PAIRS - 1, 3) + 1), "V": (proj_ready, seq_v(PAIRS - 1, 3) + 1)}
                after.split_hi(act, used)
                weights("O", PAIRS - 1, seq_out(PAIRS - 1, 7))
                attn_hi(tail - 1, 0, 0)
                attn_hi(tail - 1, 1, 0)
                probs_hi(tail, 0)
                probs_hi(tail, 1)
                attn_hi(tail, 0, 1)
                attn_hi(tail, 1, 1)
                norm.weave_scalar(act)

            @block.vector
            def _(dve):
                def logits(n, j):
                    dve.wait_ge(scores_ready, 2 * n + j + 1)
                    dve.wait_ge(biased_ready, n + 1)
                    if not isinstance(n, int) or n:
                        dve.wait_ge(turned, 2 * n + j - 1)
                    part = slice(HB * j, HB * (j + 1))
                    bank = banks[:, SCORE_BANK + j, :].rearrange("p (b k) -> p b k", b=HB)
                    dve.tensor_tensor(probs[:, part, :], bank, biased[:, part, :], ALU.add).then_inc(logits_ready, 1)
                    dve.wait_ge(logits_ready, 2 * n + j + 1)
                    dve.tensor_reduce(top[:, part], probs[:, part, :], AX_X, ALU.max, negate=True)\
                        .then_inc(top_ready, 1)

                def inverse(n, j):
                    dve.wait_ge(exp_done, 2 * n + j + 1)
                    part = slice(HB * j, HB * (j + 1))
                    dve.reciprocal(inv[:, part], total[:, part]).then_inc(raw_inv, 1)
                    dve.wait_ge(raw_inv, 2 * n + j + 1)
                    dve.tensor_tensor(inv[:, part], inv[:, part], some[:, part], ALU.mult).then_inc(inv_ready, 1)

                def low(dst, src, hi, done):
                    dve.tensor_tensor(dst, src, f32(hi), ALU.subtract).then_inc(done, 1)

                def keep(dst, bank, nth):
                    dve.wait_ge(qkv_hi, nth + 1)
                    low(dst[1], banks[:, bank, :], dst[0], proj_free)

                def qk(nth, n):
                    src = q if n < 2 else k_
                    keep([s[:, (n % 2) * HALF:(n % 2 + 1) * HALF] for s in src], n, nth)

                def probs_lo(n, j):
                    dve.wait_ge(pT_hi, 2 * n + j + 1)
                    low(pT[1][:, j, :], banks[:, TURN_BANK + j, :], pT[0][:, j, :], pT_lo)

                def attn_lo(n, j, slot):
                    dve.wait_ge(att_hi, 2 * n + j + 1)
                    cut = slice(j * HALF, (j + 1) * HALF)
                    low(att[1][:, slot, cut], banks[:, TURN_BANK + j, :], att[0][:, slot, cut], att_lo)

                def output(g):
                    for b in range(B):
                        output_batch(g, b)

                def output_batch(g, b):
                    dve.wait_ge(proj_ready, seq_out(g, b) + 1)
                    dve.tensor_tensor(resid[:, b, :], banks[:, b % PROJ_BANKS, :], resid[:, b, :], ALU.add)\
                        .then_inc(proj_free, 1)

                def add_hidden(n):
                    if n:
                        dve.wait_ge(hidden_added, 2 * n)
                    for b in (2 * n, 2 * n + 1):
                        dve.tensor_scalar(core.normed[:, b % 2, :], resid[:, b, :], core.moments[:, b, 0:1],
                                          core.rstd[:, b:b + 1], ALU.subtract, ALU.mult).then_inc(hidden_ready, 1)
                    for b in (2 * n, 2 * n + 1):
                        dve.wait_ge(hidden_ready, b + 1)
                        dve.tensor_tensor(resid[:, b, :], resid[:, b, :], core.normed[:, b % 2, :], ALU.add)\
                            .then_inc(hidden_added, 1)

                def body(g, first, last):
                    a = 2 * g
                    if not first:
                        logits(a - 1, 0)
                        logits(a - 1, 1)
                        inverse(a - 1, 0)
                    qk(12 * g, 0)
                    if not first:
                        inverse(a - 1, 1)
                    qk(12 * g + 1, 1)
                    if first:
                        add_hidden(0)
                    qk(12 * g + 2, 2)
                    if not first:
                        probs_lo(a - 1, 0)
                    qk(12 * g + 3, 3)
                    if not first:
                        probs_lo(a - 1, 1)
                    logits(a, 0)
                    if not first:
                        attn_lo(a - 1, 0, 1)
                    logits(a, 1)
                    if not first:
                        attn_lo(a - 1, 1, 1)
                    inverse(a, 0)
                    inverse(a, 1)
                    if first:
                        add_hidden(1)
                    elif not last:
                        output(g)
                    for n in range(4):
                        keep([s[:, 2 * n:2 * n + 2, :].rearrange("p b f -> p (b f)") for s in v], n, 12 * g + 4 + n)
                    if first:
                        add_hidden(2)
                    qk(12 * g + 8, 0)
                    probs_lo(a, 0)
                    qk(12 * g + 9, 1)
                    probs_lo(a, 1)
                    qk(12 * g + 10, 2)
                    qk(12 * g + 11, 3)
                    if not last:
                        attn_lo(a, 0, 0)
                        attn_lo(a, 1, 0)
                    if first:
                        add_hidden(3)

                dve.wait_ge(mask_in, DMA)
                dve.tensor_reduce(some[:, :], mask8[:, :, :], AX_X, ALU.max).then_inc(some_ready, 1)
                dve.wait_ge(some_ready, 1)
                body(0, True, False)
                dve.wait_ge(hidden_added, B)
                loop_rest(dve, body)
                tail = HEADS - 1
                logits(tail, 0)
                logits(tail, 1)
                inverse(tail, 0)
                inverse(tail, 1)
                output(PAIRS - 1)
                attn_lo(tail - 1, 0, 0)
                attn_lo(tail - 1, 1, 0)
                probs_lo(tail, 0)
                probs_lo(tail, 1)
                attn_lo(tail, 0, 1)
                attn_lo(tail, 1, 1)
                norm.weave_vector(dve, lambda b: output_batch(PAIRS, b))

            @block.gpsimd
            def _(pool):
                def weights(kind, g):
                    pool.wait_ge(w_hi[kind], g + 1)
                    pool.tensor_tensor(wt[kind][1][:, :], raw[kind][:, :], f32(wt[kind][0][:, :]), ALU.subtract)\
                        .then_inc(w_lo[kind], 1)

                def bias(n, slot, first=False):
                    pool.wait_ge(bias_loaded, 8 * (n - slot) + DMA)
                    if not first:
                        pool.wait_ge(top_ready, 2 * n)
                    row = bias_in[:, slot, :].unsqueeze(1).to_broadcast([P, B, P])
                    pool.tensor_tensor(biased[:, :, :], mask[:, :, :], row, ALU.add).then_inc(biased_ready, 1)

                def normalise(n, j):
                    pool.wait_ge(inv_ready, 2 * n + j + 1)
                    part = slice(HB * j, HB * (j + 1))
                    rows = inv[:, part].unsqueeze(2).to_broadcast([P, HB, P])
                    pool.tensor_tensor(probs[:, part, :], probs[:, part, :], rows, ALU.mult).then_inc(probs_ready, 1)

                def body(g, first, last):
                    a = 2 * g
                    if not first:
                        normalise(a - 1, 0)
                        normalise(a - 1, 1)
                    if not first:
                        bias(a, 0)
                    normalise(a, 0)
                    normalise(a, 1)
                    if not last:
                        weights("A", g + 1)
                    if not last:
                        weights("O", g)
                    bias(a + 1, 1)
                    if not last:
                        weights("V", g + 1)
                        weights("B", g + 1)

                pool.wait_ge(mask_in, DMA)
                pool.tensor_scalar(mask[:, :, :], mask8[:, :, :], MASKED, -MASKED, ALU.mult, ALU.add)\
                    .then_inc(mask_ready, 1)
                pool.wait_ge(mask_ready, 1)
                bias(0, 0, True)
                weights_early.split_lo(pool, ("V", "B"))
                body(0, True, False)
                loop_rest(pool, body)
                normalise(HEADS - 1, 0)
                normalise(HEADS - 1, 1)
                after.split_lo(pool)
                weights("O", PAIRS - 1)
                norm.weave_gpsimd(pool)
    return norm


def ffn_phase(core, io, before, weights_early, norm_row, after):
    nc = core.nc
    resid, xT, banks = core.resid, core.xT, core.banks
    with ExitStack() as ctx:
        sb, pair, sem = core.sb, core.pair, core.sem
        gu_raw = [core.raw["A"], core.raw["B"]]
        gu = [core.wt["A"], core.wt["B"]]
        d_raw = [core.raw["V"], core.raw["O"]]
        dn = [core.wt["V"], core.wt["O"]]
        gate = sb(ctx, "f_gate", [P, 2, TOK])
        hidden = sb(ctx, "f_hidden", [P, 2, TOK])
        hid = pair(ctx, "f_hid", [P, 2, TOK])
        bias = sb(ctx, "f_bias", [P, 2, 2])

        bias_in = [sem(f"f_bias_in{par}") for par in range(2)]
        gu_in = [weights_early.raw_in["gu"], sem("f_gu_in1")]
        d_in = [weights_early.raw_in["down"], sem("f_d_in1")]
        gu_hi, gu_lo = weights_early.w_hi["gu"], weights_early.w_lo["gu"]
        d_hi, d_lo = weights_early.w_hi["down"], weights_early.w_lo["down"]
        proj_ready = sem("f_proj_ready")
        down_free = sem("f_down_free")
        gate_ready = sem("f_gate_ready")
        hidden_ready = sem("f_hidden_ready")
        hid_hi = sem("f_hid_hi")
        hid_lo = sem("f_hid_lo")

        def seq_gu(c, n):
            return (12 * c - 8 if not isinstance(c, int) or c else 0) + n

        def seq_down(c, n):
            return 12 * c + 8 + n if not isinstance(c, int) or c < FULL else 12 * c + 4 + n

        norm = Norm(core, "n2", norm_row, (down_free, B * FULL), (down_free, B * FULL))

        def down_bank(c, b):
            return b % 4 if isinstance(c, int) and c == FULL else 4 + b % 4

        def rows(c):
            return REST if isinstance(c, int) and c == FULL else P

        def loop(engine, body):
            body(0, 0, 0)
            body(1, 1, 0)
            loop_rest(engine, body)

        def loop_rest(engine, body):
            body(2, 0, 1)
            with engine.Fori(1, FULL // 2 - 1) as i:
                body(2 * i + 1, 1, i)
                body(2 * i + 2, 0, i + 1)
            body(FULL - 1, 1, FULL // 2 - 1)
            body(FULL, 0, FULL // 2)

        with nc.Block() as block:
            @block.sync
            def _(sp):
                def body(c, par, turn):
                    m = rows(c)
                    if not isinstance(c, int) or c >= 2:
                        sp.wait_ge(gu_hi, c - 1)
                        sp.wait_ge(gu_lo, c - 1)
                    src = io["f_gu_rest"] if m == REST else \
                        io["f_gu"][bass.ds(c, 1)].rearrange("o p n -> p (o n)")
                    if not isinstance(c, int) or c:
                        sp.dma_start(gu_raw[par][:, 0:2 * DC * m], src).then_inc(gu_in[par], DMA)
                    if not isinstance(c, int) or c >= 2:
                        sp.wait_ge(d_hi, c - 1)
                        sp.wait_ge(d_lo, c - 1)
                    src = io["f_d_rest"] if m == REST else io["f_d"][bass.ds(c, 1)].rearrange("o p n -> p (o n)")
                    if not isinstance(c, int) or c:
                        sp.dma_start(d_raw[par][0:m, 0:D], src).then_inc(d_in[par], DMA)
                    if not isinstance(c, int) or c >= 2:
                        sp.wait_ge(hidden_ready, 2 * c - 2)
                    src = io["f_b_rest"] if m == REST else io["f_b"][bass.ds(c, 1)].rearrange("o p n -> p (o n)")
                    sp.dma_start(bias[0:m, par, :], src).then_inc(bias_in[par], DMA)

                norm.load_row(sp)
                loop(sp, body)
                after.load(sp, {"B": ((gu_hi, FULL), (gu_lo, FULL)), "O": ((d_hi, FULL), (d_lo, FULL)),
                                "A": ((gu_hi, FULL + 1), (gu_lo, FULL + 1))})

            @block.tensor
            def _(pe):
                def down(c, par):
                    pe.wait_ge(d_hi, c + 1)
                    pe.wait_ge(d_lo, c + 1)
                    for b in range(B):
                        down_batch(c, par, b)

                def down_batch(c, par, b):
                    m = rows(c)
                    if b % HB == 0:
                        pe.wait_ge(hid_lo, 2 * c + b // HB + 1)
                    if not isinstance(c, int) or c or b >= 4:
                        pe.wait_ge(down_free, B * c + b - 3)
                    product(pe, banks[:, down_bank(c, b), :], [s[0:m, par, tok(b)] for s in hid],
                            [w[0:m, 0:D] for w in dn[par]], True, True).then_inc(proj_ready, 1)

                def body(c, par, turn):
                    m = rows(c)
                    pe.wait_ge(gu_hi, c + 1)
                    pe.wait_ge(gu_lo, c + 1)
                    for n in range(4):
                        which, half = n // 2, n % 2
                        if not isinstance(c, int) or c:
                            pe.wait_ge(hidden_ready, 2 * c - 2 + half + 1)
                        for k in range(DC):
                            at = (which * DC + k) * m
                            mm = product(pe, banks[0:m, n, :], [w[:, at:at + m] for w in gu[par]],
                                         [s[:, k, half * HALF:(half + 1) * HALF] for s in xT], k == 0, k == DC - 1)
                        mm.then_inc(proj_ready, 1)
                    if not isinstance(c, int) or c:
                        down(c - 1, 1 - par)

                loop(pe, body)
                pe.wait_ge(d_hi, FULL + 1)
                pe.wait_ge(d_lo, FULL + 1)
                pe.wait_ge(hidden_ready, 2 * FULL + 2)
                norm.weave_tensor(pe, lambda b: down_batch(FULL, 0, b))

            @block.scalar
            def _(act):
                def weights(c, par, turn):
                    m = rows(c)
                    act.wait_ge(gu_in[par], DMA * (turn + 1))
                    if not isinstance(c, int) or c >= 2:
                        act.wait_ge(proj_ready, seq_gu(c - 2, 3) + 1)
                    nc.scalar.copy(gu[par][0][:, 0:2 * DC * m], gu_raw[par][:, 0:2 * DC * m]).then_inc(gu_hi, 1)
                    act.wait_ge(d_in[par], DMA * (turn + 1))
                    if not isinstance(c, int) or c >= 2:
                        act.wait_ge(proj_ready, seq_down(c - 2, 7) + 1)
                    nc.scalar.copy(dn[par][0][0:m, 0:D], d_raw[par][0:m, 0:D]).then_inc(d_hi, 1)

                def body(c, par, turn):
                    m = rows(c)
                    act.wait_ge(bias_in[par], DMA * (turn + 1))
                    for half in range(2):
                        cut = slice(half * HALF, (half + 1) * HALF)
                        act.wait_ge(proj_ready, seq_gu(c, half) + 1)
                        if not isinstance(c, int) or c >= 2:
                            act.wait_ge(hidden_ready, 2 * c - 2 + half - 1)
                        nc.scalar.activation(gate[0:m, par, cut], banks[0:m, half, :], ACT.Silu,
                                             bias=bias[0:m, par, 0:1])\
                            .then_inc(gate_ready, 1)
                    if not isinstance(c, int) or c < FULL:
                        weights(c + 1, 1 - par, turn + par)
                    for half in range(2):
                        cut = slice(half * HALF, (half + 1) * HALF)
                        act.wait_ge(hidden_ready, 2 * c + half + 1)
                        if not isinstance(c, int) or c >= 2:
                            act.wait_ge(proj_ready, seq_down(c - 2, 7) + 1)
                        nc.scalar.copy(hid[0][0:m, par, cut], hidden[0:m, par, cut]).then_inc(hid_hi, 1)

                loop(act, body)
                used = {"B": (proj_ready, seq_gu(FULL - 1, 3) + 1), "O": (proj_ready, seq_down(FULL - 1, 7) + 1),
                        "A": (proj_ready, seq_gu(FULL, 3) + 1)}
                after.split_hi(act, used)
                norm.weave_scalar(act)

            @block.vector
            def _(dve):
                def down(c):
                    for b in range(B):
                        down_batch(c, b)

                def down_batch(c, b):
                    dve.wait_ge(proj_ready, seq_down(c, b) + 1)
                    dve.tensor_tensor(resid[:, b, :], banks[:, down_bank(c, b), :], resid[:, b, :], ALU.add)\
                        .then_inc(down_free, 1)

                def body(c, par, turn):
                    m = rows(c)
                    dve.wait_ge(bias_in[par], DMA * (turn + 1))
                    for half in range(2):
                        cut = slice(half * HALF, (half + 1) * HALF)
                        dve.wait_ge(gate_ready, 2 * c + half + 1)
                        dve.wait_ge(proj_ready, seq_gu(c, 2 + half) + 1)
                        if not isinstance(c, int) or c >= 2:
                            dve.wait_ge(hid_lo, 2 * (c - 2) + half + 1)
                        dve.scalar_tensor_tensor(hidden[0:m, par, cut], banks[0:m, 2 + half, :], bias[0:m, par, 1:2],
                                                 gate[0:m, par, cut], ALU.add, ALU.mult).then_inc(hidden_ready, 1)
                    if not isinstance(c, int) or c:
                        down(c - 1)

                body(0, 0, 0)
                dve.wait_ge(before.row_added, B)
                body(1, 1, 0)
                loop_rest(dve, body)
                norm.weave_vector(dve, lambda b: down_batch(FULL, b))

            @block.gpsimd
            def _(pool):
                def weights(c, par):
                    m = rows(c)
                    n = 2 * DC * m
                    pool.wait_ge(gu_hi, c + 1)
                    pool.tensor_tensor(gu[par][1][:, 0:n], gu_raw[par][:, 0:n], f32(gu[par][0][:, 0:n]), ALU.subtract)\
                        .then_inc(gu_lo, 1)
                    pool.wait_ge(d_hi, c + 1)
                    pool.tensor_tensor(dn[par][1][0:m, 0:D], d_raw[par][0:m, 0:D], f32(dn[par][0][0:m, 0:D]), ALU.subtract)\
                        .then_inc(d_lo, 1)

                def body(c, par, turn):
                    m = rows(c)
                    if not isinstance(c, int) or c < FULL:
                        weights(c + 1, 1 - par)
                    for half in range(2):
                        cut = slice(half * HALF, (half + 1) * HALF)
                        pool.wait_ge(hid_hi, 2 * c + half + 1)
                        pool.tensor_tensor(hid[1][0:m, par, cut], hidden[0:m, par, cut], f32(hid[0][0:m, par, cut]),
                                           ALU.subtract).then_inc(hid_lo, 1)

                before.add_rows(pool)
                loop(pool, body)
                kinds = [load[0] for load in after.loads]
                norm.weave_gpsimd(pool, lambda b: after.split_lo(pool, kinds[b:b + 1]))


GROUPED_BUFFER = {"K": "B", "Q": "O", "V": "A", "O": "V"}


def grouped_attention_phase(core, io, weights_early, norm_row, lora):
    nc = core.nc
    resid, xT, cT, ident, banks = core.resid, core.xT, core.cT, core.ident, core.banks
    ROUNDS = PAIRS // 4
    with ExitStack() as ctx:
        sb, pair, sem = core.sb, core.pair, core.sem
        SIZE = {"Q": 2 * DC * P, "K": DC * P, "V": 2 * DC * P, "O": 2 * D}
        raw = {k: core.raw[GROUPED_BUFFER[k]][:, 0:n] for k, n in SIZE.items()}
        wt = {k: [w[:, 0:n] for w in core.wt[GROUPED_BUFFER[k]]] for k, n in SIZE.items()}
        q = pair(ctx, "g_q", [P, 2, TOK])
        k_ = pair(ctx, "g_k", [P, TOK])
        v = pair(ctx, "g_v", [P, B, 2 * P])
        att = pair(ctx, "g_att", [P, 2, TOK])
        spare = GROUPED_BUFFER["K"]
        pT = [pair(ctx, "g_pT", [P, HALF]), [w[:, SIZE["K"]:] for w in core.wt[spare]]]
        probs = sb(ctx, "g_probs", [P, 2 * B, P])
        swapped = sb(ctx, "g_swapped", [P, 2, HALF])
        turned_by = core.normed
        cos, sin, mask, mask_raw = (core.raw[spare][:, SIZE["K"] + n * P:SIZE["K"] + (n + 1) * P] for n in range(4))
        mask8 = sb(ctx, "g_mask8", [P, P], U8)
        some = sb(ctx, "g_some", [P, 1])
        cap = sb(ctx, "g_cap", [P, 1])
        total = sb(ctx, "g_total", [P, 2 * B])
        inv = sb(ctx, "g_inv", [P, 2 * B])

        lora.place(q, swapped, raw["K"])
        raw_in, w_hi, w_lo = weights_early.raw_in, weights_early.w_hi, weights_early.w_lo
        consts_in = sem("g_consts_in")
        mask_steps = sem("g_mask_steps")
        cap_ready = sem("g_cap_ready")
        mask_ready = sem("g_mask_ready")
        proj_ready = sem("g_proj_ready")
        proj_free = sem("g_proj_free")
        v_hi = sem("g_v_hi")
        swap_done = sem("g_swap_done")
        sin_done = sem("g_sin_done")
        rope_done = sem("g_rope_done")
        qk_hi = sem("g_qk_hi")
        qk_lo = sem("g_qk_lo")
        scores_ready = sem("g_scores_ready")
        tanh_done = sem("g_tanh_done")
        logits_ready = sem("g_logits_ready")
        exp_done = sem("g_exp_done")
        inv_ready = sem("g_inv_ready")
        probs_ready = sem("g_probs_ready")
        turned = sem("g_turned")
        pT_hi = sem("g_pT_hi")
        pT_lo = sem("g_pT_lo")
        pv_ready = sem("g_pv_ready")
        att_hi = sem("g_att_hi")
        att_lo = sem("g_att_lo")

        PER = 56
        Q_AT = (2, 18, 32, 44)
        K_AT = {0: 0, 2: 30}
        OUT_AT = (6, 22, 36, 48)
        V_AT = 14
        ROPES = 20
        ROPE_AT = (0, 6, 10, 16)

        def is_first(r, u):
            return isinstance(r, int) and r == 0 and u == 0

        def seq(r, u, at):
            if is_first(r, u) and at < OUT_AT[0]:
                return at
            return PER * r - 8 + at

        def seq_out(r, u, n):
            return PER * r - 8 + (OUT_AT[u] if not (isinstance(r, int) and r == ROUNDS) else DC) + n

        def out_bank(r, u, n):
            return ((0 if isinstance(r, int) and r == ROUNDS else OUT_AT[u]) + n) % PROJ_BANKS

        FOLD = PER * ROUNDS - 8
        norm = Norm(core, "n3", norm_row, (proj_free, seq_out(ROUNDS, 0, 0)), (att_lo, 4 * PAIRS))

        def ropes(u):
            blocks = [(K_AT[u] + h, None, h) for h in range(2)] if u in K_AT else []
            return blocks + [(Q_AT[u] + 2 * h + s, s, h) for h in range(2) for s in range(2)]

        def rope_of(r, u, slot, half):
            return ROPES * r + ROPE_AT[u] + (2 if u in K_AT else 0) + 2 * half + slot

        def dst(slot, half, hl):
            cut = slice(half * HALF, (half + 1) * HALF)
            return k_[hl][:, cut] if slot is None else q[hl][:, slot, cut]

        def nth_quarter(p, j, back=0):
            n = 4 * (p - back) + j + 1
            return None if isinstance(n, int) and n <= 0 else n

        def bank_quarter(j):
            return banks[:, QUARTER_BANK + j, :].rearrange("p (b h t) -> p b h t", b=2, h=2)

        def att_quarter(hl, j):
            return att[hl][:, :, tok(2 * j, 2)].rearrange("p h (b t) -> p b h t", b=2)

        def quarter(j):
            return slice(4 * j, 4 * j + 4)

        def loop(engine, body):
            for u in range(4):
                body(0, u, u == 0, False)
            with engine.Fori(1, ROUNDS - 1) as r:
                for u in range(4):
                    body(r, u, False, False)
            for u in range(4):
                body(ROUNDS - 1, u, False, u == 3)

        with nc.Block() as block:
            @block.sync
            def _(sp):
                sp.dma_start(mask8[:, :], io["g_mask"]).then_inc(consts_in, DMA)
                sp.dma_start(cos[:, :], io["g_cos"]).then_inc(consts_in, DMA)
                sp.dma_start(sin[:, :], io["g_sin"]).then_inc(consts_in, DMA)

                def load(kind, n):
                    if not isinstance(n, int) or n:
                        sp.wait_ge(w_hi[kind], n)
                        sp.wait_ge(w_lo[kind], n)
                    sp.dma_start(raw[kind], io["g_w" + kind][bass.ds(n, 1)].rearrange("o p n -> p (o n)"))\
                        .then_inc(raw_in[kind], DMA)

                def body(r, u, first, last):
                    final_round = isinstance(r, int) and r == ROUNDS - 1
                    if not last:
                        load("Q", 4 * r + u + 1)
                    if u == 0 or (u == 2 and not final_round):
                        load("K", 2 * r + u // 2 + 1)
                    if u == 1 and not final_round:
                        load("V", r + 1)
                    load("O", 4 * r + u)

                norm.load_row(sp)
                lora.load_coef(sp)
                loop(sp, body)
                lora.load(sp, {"V": ((w_hi["V"], ROUNDS), (w_lo["V"], ROUNDS)),
                               "Q": ((w_hi["Q"], PAIRS), (w_lo["Q"], PAIRS))}, (scores_ready, 4 * PAIRS))

            @block.tensor
            def _(pe):
                def bank_free(s):
                    if not isinstance(s, int) or s >= PROJ_BANKS:
                        pe.wait_ge(proj_free, s - PROJ_BANKS + 1)

                def weights_ready(kind, n):
                    pe.wait_ge(w_hi[kind], n + 1)
                    pe.wait_ge(w_lo[kind], n + 1)

                def project(s, at, kind, slot, half):
                    src = cT if kind == "K" else xT
                    bank_free(s)
                    for c in range(DC):
                        col = (slot * DC + c) * P
                        mm = product(pe, banks[:, at % PROJ_BANKS, :], [w[:, col:col + P] for w in wt[kind]],
                                     [x[:, c, half * HALF:(half + 1) * HALF] for x in src], c == 0, c == DC - 1)
                    mm.then_inc(proj_ready, 1)

                def values(r):
                    weights_ready("V", r)
                    for n in range(4):
                        s = seq(r, 0, V_AT + n)
                        bank_free(s)
                        for t in range(2):
                            for c in range(DC):
                                mm = product(pe, banks[:, (V_AT + n) % PROJ_BANKS, t * 256:(t + 1) * 256],
                                             [x[:, c, tok(2 * n + t)] for x in cT],
                                             [w[:, c * 256:(c + 1) * 256] for w in wt["V"]], c == 0, c == DC - 1)
                        mm.then_inc(proj_ready, 1)

                def scores(p, j, rope, first):
                    pe.wait_ge(qk_lo, rope + 1)
                    if not first:
                        pe.wait_ge(att_lo, nth_quarter(p, j, 1))
                    for t in range(4):
                        b, h = 2 * j + t // 2, t % 2
                        mm = product(pe, banks[:, QUARTER_BANK + j, tok(t)], [s[:, h, tok(b)] for s in q],
                                     [s[:, tok(b)] for s in k_], True, True)
                    mm.then_inc(scores_ready, 1)

                def turn(p, j):
                    pe.wait_ge(probs_ready, nth_quarter(p, j))
                    for t in range(4):
                        mm = pe.transpose(banks[:, QUARTER_BANK + j, tok(t)], probs[:, 4 * j + t, :], ident[:, :])
                    mm.then_inc(turned, 1)

                def pv(p, j, kv):
                    pe.wait_ge(pT_lo, nth_quarter(p, j))
                    for t in range(2):
                        mm = product(pe, banks[:, QUARTER_BANK + j, tok(2 * t, 2)], [s[:, 2 * j + t, tok(kv)] for s in v],
                                     [s[:, tok(2 * t, 2)] for s in pT[j % 2]], True, True)
                    mm.then_inc(pv_ready, 1)

                def output(r, u):
                    weights_ready("O", 4 * r + u - 1)
                    for b in range(B):
                        output_batch(r, u, b)

                def output_batch(r, u, b):
                    if b % 2 == 0:
                        pe.wait_ge(att_lo, nth_quarter(4 * r + u, b // 2, 1))
                    bank_free(seq_out(r, u, b))
                    for h in range(2):
                        mm = product(pe, banks[:, out_bank(r, u, b), :], [x[:, h, tok(b)] for x in att],
                                     [w[:, h * D:(h + 1) * D] for w in wt["O"]], h == 0, h == 1)
                    mm.then_inc(proj_ready, 1)

                def body(r, u, first, last):
                    p = 4 * r + u
                    before_kv = (u - 1) // 2 % 2
                    if u in K_AT:
                        weights_ready("K", 2 * r + u // 2)
                        for half in range(2):
                            project(seq(r, u, K_AT[u] + half), K_AT[u] + half, "K", 0, half)
                    weights_ready("Q", p)
                    for n in range(4):
                        if n == 3 and not first:
                            turn(p - 1, 0)
                            turn(p - 1, 1)
                        project(seq(r, u, Q_AT[u] + n), Q_AT[u] + n, "Q", n % 2, n // 2)
                    if not first:
                        pe.wait_ge(proj_free, seq(r, 0, V_AT + 3) - (PER if u == 0 else 0) + 1)
                        pv(p - 1, 0, before_kv)
                        turn(p - 1, 2)
                        pv(p - 1, 1, before_kv)
                        turn(p - 1, 3)
                    scores(p, 0, rope_of(r, u, 1, 0), first)
                    if not first:
                        pv(p - 1, 2, before_kv)
                    scores(p, 1, rope_of(r, u, 1, 0), first)
                    if not first:
                        pv(p - 1, 3, before_kv)
                    scores(p, 2, rope_of(r, u, 1, 1), first)
                    scores(p, 3, rope_of(r, u, 1, 1), first)
                    if not first:
                        output(r, u)
                    if u == 0:
                        values(r)

                loop(pe, body)
                lora.fold(pe, FOLD, proj_ready, bank_free)
                tail = PAIRS - 1
                turn(tail, 0)
                turn(tail, 1)
                pv(tail, 0, 1)
                turn(tail, 2)
                pv(tail, 1, 1)
                turn(tail, 3)
                pv(tail, 2, 1)
                pv(tail, 3, 1)
                weights_ready("O", PAIRS - 1)
                norm.weave_tensor(pe, lambda b: output_batch(ROUNDS, 0, b))

            @block.scalar
            def _(act):
                def part(j):
                    return probs[:, quarter(j), :].rearrange("p t k -> p (t k)")

                def tanhs(p, j):
                    act.wait_ge(scores_ready, nth_quarter(p, j))
                    nc.scalar.activation(part(j), banks[:, QUARTER_BANK + j, :], ACT.Tanh,
                                         scale=ATTN_MULT / LOGIT_CAP).then_inc(tanh_done, 1)

                def exps(p, j):
                    act.wait_ge(logits_ready, nth_quarter(p, j))
                    for t in range(4 * j, 4 * j + 4):
                        e = nc.scalar.activation(probs[:, t, :], probs[:, t, :], ACT.Exp, accum_out=total[:, t:t + 1])
                    e.then_inc(exp_done, 1)

                def swap(s, at, nth, first):
                    act.wait_ge(proj_ready, s + 1)
                    if not (isinstance(nth, int) and nth < 2):
                        act.wait_ge(rope_done, nth - 1)
                    h = P // 2
                    nc.scalar.copy(swapped[0:h, nth_par(at), :], banks[h:P, at[0] % PROJ_BANKS, :])
                    nc.scalar.copy(swapped[h:P, nth_par(at), :], banks[0:h, at[0] % PROJ_BANKS, :])\
                        .then_inc(swap_done, 1)

                def nth_par(at):
                    return at[1] % 2

                def rotated_hi(block, nth, at):
                    act.wait_ge(rope_done, nth + 1)
                    nc.scalar.copy(dst(block[1], block[2], 0), turned_by[:, nth_par(at), :]).then_inc(qk_hi, 1)

                def probs_hi(p, j):
                    act.wait_ge(turned, nth_quarter(p, j))
                    if nth_quarter(p, j - 2) is not None:
                        act.wait_ge(pv_ready, nth_quarter(p, j - 2))
                    nc.scalar.copy(pT[j % 2][0][:, :], banks[:, QUARTER_BANK + j, :]).then_inc(pT_hi, 1)

                def attn_hi(p, j):
                    act.wait_ge(pv_ready, nth_quarter(p, j))
                    nc.scalar.copy(att_quarter(0, j), bank_quarter(j)).then_inc(att_hi, 1)

                def weights(kind, n, used=None):
                    act.wait_ge(raw_in[kind], DMA * (n + 1))
                    if used is not None:
                        act.wait_ge(proj_ready, used + 1)
                    nc.scalar.copy(wt[kind][0], raw[kind]).then_inc(w_hi[kind], 1)

                def body(r, u, first, last):
                    p = 4 * r + u
                    final_round = isinstance(r, int) and r == ROUNDS - 1
                    blocks = ropes(u)
                    at = [(blk[0], ROPE_AT[u] + i) for i, blk in enumerate(blocks)]
                    nth = [ROPES * r + x[1] for x in at]
                    end = len(blocks) - 1
                    for i, blk in enumerate(blocks):
                        swap(seq(r, u, blk[0]), at[i], nth[i], first)
                        if i == 0 and not first:
                            act.wait_ge(scores_ready, nth_quarter(p, 3, 1))
                        if i and i < end:
                            rotated_hi(blocks[i - 1], nth[i - 1], at[i - 1])
                        if i == end - 1:
                            if not first:
                                probs_hi(p - 1, 0)
                                probs_hi(p - 1, 1)
                    if not first:
                        attn_hi(p - 1, 0)
                        probs_hi(p - 1, 2)
                        attn_hi(p - 1, 1)
                        probs_hi(p - 1, 3)
                    rotated_hi(blocks[end - 1], nth[end - 1], at[end - 1])
                    rotated_hi(blocks[end], nth[end], at[end])
                    if not first:
                        attn_hi(p - 1, 2)
                        attn_hi(p - 1, 3)
                    if not last:
                        weights("Q", p + 1, seq(r, u, Q_AT[u] + 3))
                    if u == 0 or (u == 2 and not final_round):
                        weights("K", 2 * r + u // 2 + 1, seq(r, u, K_AT[u] + 1))
                    softmax(p)
                    if u == 1 and not final_round:
                        weights("V", r + 1, seq(r, 0, V_AT + 3))
                    if last:
                        lora.split_ab_hi(act)
                    weights("O", p, None if first else seq_out(r, u, 7))
                    if u == 0:
                        for n in range(4):
                            act.wait_ge(proj_ready, seq(r, 0, V_AT + n) + 1)
                            nc.scalar.copy(v[0][:, 2 * n:2 * n + 2, :].rearrange("p b f -> p (b f)"),
                                           banks[:, (V_AT + n) % PROJ_BANKS, :]).then_inc(v_hi, 1)

                def softmax(p):
                    tanhs(p, 0)
                    tanhs(p, 1)
                    exps(p, 0)
                    tanhs(p, 2)
                    exps(p, 1)
                    tanhs(p, 3)
                    exps(p, 2)
                    exps(p, 3)

                loop(act, body)
                tail = PAIRS - 1
                probs_hi(tail, 0)
                probs_hi(tail, 1)
                attn_hi(tail, 0)
                probs_hi(tail, 2)
                attn_hi(tail, 1)
                probs_hi(tail, 3)
                attn_hi(tail, 2)
                attn_hi(tail, 3)
                lora.split_w_hi(act, FOLD, proj_free)
                norm.weave_scalar(act)

            @block.vector
            def _(dve):
                def wide(table):
                    return table[:, :].unsqueeze(1).to_broadcast([P, HB, P])

                def logits(p, j):
                    dve.wait_ge(tanh_done, nth_quarter(p, j))
                    part = probs[:, quarter(j), :]
                    dve.scalar_tensor_tensor(part, part, cap[:, 0:1], wide(mask), ALU.mult, ALU.add)\
                        .then_inc(logits_ready, 1)

                def inverse(p, j):
                    dve.wait_ge(exp_done, nth_quarter(p, j))
                    dve.reciprocal(inv[:, quarter(j)], total[:, quarter(j)]).then_inc(inv_ready, 1)

                def rotate_cos(at, par, nth):
                    dve.wait_ge(swap_done, nth + 1)
                    if not (isinstance(nth, int) and nth < 2):
                        dve.wait_ge(qk_lo, nth - 1)
                    bank = banks[:, at % PROJ_BANKS, :].rearrange("p (b t) -> p b t", b=HB)
                    out = turned_by[:, par, :].rearrange("p (b t) -> p b t", b=HB)
                    dve.tensor_tensor(out, bank, wide(cos), ALU.mult).then_inc(proj_free, 1)

                def rotate_add(s, par, nth):
                    dve.wait_ge(sin_done, nth + 1)
                    dve.wait_ge(proj_free, s + 1)
                    dve.tensor_tensor(turned_by[:, par, :], turned_by[:, par, :], swapped[:, par, :], ALU.add)\
                        .then_inc(rope_done, 1)

                def low(out, src, hi, done):
                    dve.tensor_tensor(out, src, f32(hi), ALU.subtract).then_inc(done, 1)

                def rotated_lo(blk, par, nth):
                    dve.wait_ge(qk_hi, nth + 1)
                    low(dst(blk[1], blk[2], 1), turned_by[:, par, :], dst(blk[1], blk[2], 0), qk_lo)

                def probs_lo(p, j):
                    dve.wait_ge(pT_hi, nth_quarter(p, j))
                    low(pT[j % 2][1][:, :], banks[:, QUARTER_BANK + j, :], pT[j % 2][0][:, :], pT_lo)

                def attn_lo(p, j):
                    dve.wait_ge(att_hi, nth_quarter(p, j))
                    low(att_quarter(1, j), bank_quarter(j), att_quarter(0, j), att_lo)

                def output(r, u, b):
                    dve.wait_ge(proj_ready, seq_out(r, u, b) + 1)
                    dve.tensor_tensor(resid[:, b, :], banks[:, out_bank(r, u, b), :], resid[:, b, :],
                                      ALU.add).then_inc(proj_free, 1)

                def body(r, u, first, last):
                    p = 4 * r + u
                    blocks = ropes(u)
                    end = len(blocks) - 1

                    def add(i):
                        rotate_add(seq(r, u, blocks[i][0]), (ROPE_AT[u] + i) % 2, ROPES * r + ROPE_AT[u] + i)

                    def split(i):
                        rotated_lo(blocks[i], (ROPE_AT[u] + i) % 2, ROPES * r + ROPE_AT[u] + i)

                    for i, blk in enumerate(blocks):
                        at = ROPE_AT[u] + i
                        if i and i < end:
                            add(i - 1)
                        rotate_cos(blk[0], at % 2, ROPES * r + at)
                        if i and i < end:
                            split(i - 1)
                        if i == end - 1:
                            if not first:
                                probs_lo(p - 1, 0)
                                probs_lo(p - 1, 1)
                            add(i)
                    if not first:
                        attn_lo(p - 1, 0)
                        probs_lo(p - 1, 2)
                    add(end)
                    if not first:
                        attn_lo(p - 1, 1)
                        probs_lo(p - 1, 3)
                    split(end - 1)
                    split(end)
                    if not first:
                        attn_lo(p - 1, 2)
                        attn_lo(p - 1, 3)
                    done = 0
                    for step, j, outs in ((logits, 0, 0), (logits, 1, 1), (logits, 2, 1), (inverse, 0, 0), (logits, 3, 1),
                                          (inverse, 1, 1), (inverse, 2, 1), (inverse, 3, 3)):
                        step(p, j)
                        for _ in range(outs):
                            if not first:
                                output(r, u, done)
                            if last and done == 5:
                                lora.split_ab_lo(dve)
                            done = done + 1
                    if u == 0:
                        for n in range(4):
                            dve.wait_ge(v_hi, 4 * r + n + 1)
                            cut = [s[:, 2 * n:2 * n + 2, :].rearrange("p b f -> p (b f)") for s in v]
                            low(cut[1], banks[:, (V_AT + n) % PROJ_BANKS, :], cut[0], proj_free)

                dve.wait_ge(consts_in, 3 * DMA)
                dve.tensor_reduce(some[:, :], mask8[:, :], AX_X, ALU.max).then_inc(mask_steps, 1)
                dve.tensor_scalar(mask_raw[:, :], mask8[:, :], MASKED, -MASKED, ALU.mult, ALU.add).then_inc(mask_steps, 1)
                dve.wait_ge(mask_steps, 2)
                dve.tensor_scalar(cap[:, :], some[:, :], LOGIT_CAP, None, ALU.mult).then_inc(cap_ready, 1)
                dve.tensor_scalar(mask[:, :], mask_raw[:, :], some[:, 0:1], None, ALU.mult).then_inc(mask_ready, 1)
                dve.wait_ge(cap_ready, 1)
                dve.wait_ge(mask_ready, 1)
                loop(dve, body)
                tail = PAIRS - 1
                probs_lo(tail, 0)
                probs_lo(tail, 1)
                lora.add_fold(dve, 0, FOLD, proj_ready, proj_free)
                attn_lo(tail, 0)
                probs_lo(tail, 2)
                lora.add_fold(dve, 1, FOLD, proj_ready, proj_free)
                attn_lo(tail, 1)
                probs_lo(tail, 3)
                lora.add_fold(dve, 2, FOLD, proj_ready, proj_free)
                attn_lo(tail, 2)
                attn_lo(tail, 3)
                lora.add_fold(dve, 3, FOLD, proj_ready, proj_free)
                norm.weave_vector(dve, lambda b: output(ROUNDS, 0, b))

            @block.gpsimd
            def _(pool):
                def weights(kind, n):
                    pool.wait_ge(w_hi[kind], n + 1)
                    pool.tensor_tensor(wt[kind][1], raw[kind], f32(wt[kind][0]), ALU.subtract)\
                        .then_inc(w_lo[kind], 1)

                def normalise(p, j):
                    pool.wait_ge(inv_ready, nth_quarter(p, j))
                    rows = inv[:, quarter(j)].unsqueeze(2).to_broadcast([P, 4, P])
                    pool.tensor_tensor(probs[:, quarter(j), :], probs[:, quarter(j), :], rows, ALU.mult)\
                        .then_inc(probs_ready, 1)

                def rotate_sin(par, nth):
                    pool.wait_ge(swap_done, nth + 1)
                    part = swapped[:, par, :].rearrange("p (b t) -> p b t", b=HB)
                    pool.tensor_tensor(part, part, sin[:, :].unsqueeze(1).to_broadcast([P, HB, P]), ALU.mult)\
                        .then_inc(sin_done, 1)

                def body(r, u, first, last):
                    p = 4 * r + u
                    final_round = isinstance(r, int) and r == ROUNDS - 1
                    for i in range(len(ropes(u))):
                        at = ROPE_AT[u] + i
                        rotate_sin(at % 2, ROPES * r + at)
                    if not last:
                        weights("Q", p + 1)
                    if u == 0 or (u == 2 and not final_round):
                        weights("K", 2 * r + u // 2 + 1)
                    for j in range(4):
                        normalise(p, j)
                    if u == 1 and not final_round:
                        weights("V", r + 1)
                    weights("O", p)

                pool.wait_ge(consts_in, 3 * DMA)
                loop(pool, body)
                norm.weave_gpsimd(pool, lambda b: lora.split_w_lo(pool, b) if b < DC else None)
    return norm


class Lora:

    BUFFERS = ("V", "Q")

    def __init__(self, core, io):
        self.core, self.io = core, io
        buffers = [GROUPED_BUFFER[k] for k in self.BUFFERS]
        self.w_raw = [core.raw[buffers[c // 2]][:, c % 2 * D:(c % 2 + 1) * D] for c in range(DC)]
        self.w = [[w[:, c % 2 * D:(c % 2 + 1) * D] for w in core.wt[buffers[c // 2]]] for c in range(DC)]
        self.coef = core.sb(core.ctx, "l_coef", [P, 1])
        sem = core.sem
        self.coef_in = sem("l_coef_in")
        self.ab_in = sem("l_ab_in")
        self.w_in = [sem(f"l_w_in{n}") for n in range(2)]
        self.b_ready = sem("l_b_ready")
        self.ab_hi = sem("l_ab_hi")
        self.ab_lo = sem("l_ab_lo")
        self.w_hi = sem("l_w_hi")
        self.w_lo = sem("l_w_lo")

    def place(self, q, swapped, k_raw):
        self.a_raw, self.b_raw = swapped[:, 0, :], swapped[:, 1, :]
        self.b_scaled = k_raw
        self.a2 = [s[:, 0, 0:D] for s in q]
        self.b2 = [s[:, 1, 0:D] for s in q]

    def load_coef(self, sp):
        for n in range(LORA // RANK):
            sp.dma_start(self.coef[n * RANK:(n + 1) * RANK, :], self.io["l_coef"][n:n + 1].partition_broadcast(RANK))\
                .then_inc(self.coef_in, DMA)

    def load(self, sp, raw_free, q_used):
        w4 = self.io["l_w"].rearrange("(c p) o -> p c o", p=P)
        for n, kind in enumerate(self.BUFFERS):
            for sem, value in raw_free[kind]:
                sp.wait_ge(sem, value)
            whole = self.core.raw[GROUPED_BUFFER[kind]].rearrange("p (c o) -> p c o", c=2)
            sp.dma_start(whole, w4[:, 2 * n:2 * n + 2, :]).then_inc(self.w_in[n], DMA)
        sp.wait_ge(*q_used)
        sp.dma_start(self.a_raw, self.io["l_a"]).then_inc(self.ab_in, DMA)
        sp.dma_start(self.b_raw, self.io["l_b"]).then_inc(self.ab_in, DMA)

    def split_ab_hi(self, act):
        act.wait_ge(self.ab_in, 2 * DMA)
        self.core.nc.scalar.copy(self.a2[0], self.a_raw).then_inc(self.ab_hi, 1)
        act.wait_ge(self.b_ready, 1)
        self.core.nc.scalar.copy(self.b2[0], self.b_scaled).then_inc(self.ab_hi, 1)

    def split_ab_lo(self, dve):
        dve.wait_ge(self.ab_in, 2 * DMA)
        dve.wait_ge(self.coef_in, LORA // RANK * DMA)
        dve.tensor_scalar(self.b_scaled, self.b_raw, self.coef[:, 0:1], LORA_SCALE, ALU.mult, ALU.mult)\
            .then_inc(self.b_ready, 1)
        for n, (src, dst) in enumerate(((self.a_raw, self.a2), (self.b_scaled, self.b2))):
            dve.wait_ge(self.ab_hi, n + 1)
            dve.tensor_tensor(dst[1], src, f32(dst[0]), ALU.subtract).then_inc(self.ab_lo, 1)

    def fold(self, pe, seq, ready, bank_free):
        pe.wait_ge(self.ab_lo, 2)
        for c in range(DC):
            bank_free(seq + c)
            product(pe, self.core.banks[:, c, :], [s[:, tok(c)] for s in self.a2], self.b2, True, True)\
                .then_inc(ready, 1)

    def add_fold(self, dve, c, seq, ready, free):
        dve.wait_ge(self.w_in[c // 2], DMA)
        dve.wait_ge(ready, seq + c + 1)
        dve.tensor_tensor(self.w_raw[c], self.core.banks[:, c, :], self.w_raw[c], ALU.add).then_inc(free, 1)

    def split_w_hi(self, act, seq, free):
        for c in range(DC):
            act.wait_ge(free, seq + c + 1)
            self.core.nc.scalar.copy(self.w[c][0], self.w_raw[c]).then_inc(self.w_hi, 1)

    def split_w_lo(self, pool, c):
        pool.wait_ge(self.w_hi, c + 1)
        pool.tensor_tensor(self.w[c][1], self.w_raw[c], f32(self.w[c][0]), ALU.subtract).then_inc(self.w_lo, 1)


def last_phase(core, before, lora, out):
    resid, xT, banks = core.resid, core.xT, core.banks
    out_ready = core.sem("o_out_ready")
    added = core.sem("o_added")
    stored = core.sem("o_stored")

    with core.nc.Block() as block:
        @block.sync
        def _(sp):
            for b in range(B):
                sp.wait_ge(added, b + 1)
                sp.dma_start(out[b, :, :], resid[:, b, :]).then_inc(stored, DMA)
            sp.wait_ge(stored, B * DMA)

        @block.tensor
        def _(pe):
            for b in range(B):
                if b >= 4:
                    pe.wait_ge(added, b - 3)
                for c in range(DC):
                    mm = product(pe, banks[:, b % 4, :], [s[:, c, tok(b)] for s in xT], lora.w[c], c == 0, c == DC - 1)
                mm.then_inc(out_ready, 1)

        @block.gpsimd
        def _(pool):
            before.add_rows(pool)

        @block.vector
        def _(dve):
            for b in range(B):
                dve.wait_ge(out_ready, b + 1)
                dve.wait_ge(before.row_added, b + 1)
                dve.tensor_tensor(resid[:, b, :], banks[:, b % 4, :], resid[:, b, :], ALU.add).then_inc(added, 1)


def build(nc, io, out):
    def first_of(name):
        return io[name][0:1].rearrange("o p n -> p (o n)")

    with ExitStack() as ctx:
        core = Core(nc, ctx)
        cross = Early(core, "x", core.KINDS, [(k, k, first_of("x_w" + k), WEIGHTS) for k in ("A", "V", "B")])
        ffn = Early(core, "f", ("gu", "down"), [("A", "gu", first_of("f_gu"), WEIGHTS), ("V", "down", first_of("f_d"), D)])
        grouped = Early(core, "g", tuple(GROUPED_BUFFER),
                        [(GROUPED_BUFFER[k], k, first_of("g_w" + k), n) for k, n in (("K", D), ("Q", 2 * D), ("V", 2 * D))])
        lora = Lora(core, io)
        first_phase(core, io, cross)
        norm1 = cross_attention_phase(core, {"mask": io["x_mask"], "bias": io["x_bias"], "wA": io["x_wA"], "wB": io["x_wB"],
                                             "wV": io["x_wV"], "wO": io["x_wO"]}, cross, io["f_b_down"], ffn)
        ffn_phase(core, io, norm1, ffn, None, grouped)
        norm3 = grouped_attention_phase(core, io, grouped, io["l_bias"], lora)
        last_phase(core, norm3, lora, out)


def head_weights(w):
    return w.reshape(DC, P, -1, P).transpose(2, 1, 0, 3)


def pair_columns(w):
    return w.reshape(DC, P, -1, 2 * P).transpose(2, 1, 0, 3).reshape(-1, P, DC * 2 * P)


def pair_rows(w):
    return w.reshape(-1, 2, P, D).transpose(0, 2, 1, 3).reshape(-1, P, 2 * D)


def lay_out(a):
    q = head_weights(a["L0_xattn_w_q"].T)
    k = head_weights(a["L0_xattn_w_k"].T)
    qk = np.stack([q, k], 2).reshape(HEADS, P, 2 * DC * P)
    io = {
        "x": a["x"],
        "ctxT": a["ctx_4096"].reshape(TOK, D).T,
        "ident": np.eye(P, dtype=np.float32),
        "x_ln_w": a["L0_xattn_ln_weight"],
        "x_mask": a["mask_BxSxS2_bk0"],
        "x_bias": a["L0_xattn_position_bias"].reshape(PAIRS, 2, P, P),
        "x_wA": qk[0::2],
        "x_wB": qk[1::2],
        "x_wV": pair_columns(a["L0_xattn_w_v"].T),
        "x_wO": pair_rows(a["L0_xattn_w_out"].T),
    }
    io.update(lay_out_more(a))
    return {n: np.ascontiguousarray(v) for n, v in io.items()}


def lay_out_more(a):
    gate, up, down = (a["L0_ffn_w_" + n].T for n in ("gate", "up", "down"))
    full = FULL * P
    gu = np.stack([head_weights(gate[:, :full]), head_weights(up[:, :full])], 2)
    rest = np.stack([m[:, full:].reshape(DC, P, REST).transpose(1, 0, 2) for m in (gate, up)], 1)
    biases = np.stack([a["L0_ffn_b_gate"], a["L0_ffn_b_up"]], 1)
    inv_freq = np.float32(1.0) / np.float32(10000.0) ** (np.arange(0, P, 2, dtype=np.float32) / np.float32(P))
    phase = np.tile(np.arange(P, dtype=np.float32)[:, None] * inv_freq[None, :], (1, 2)).T
    sign = np.where(np.arange(P) < P // 2, -1, 1).astype(np.float32)[:, None]
    return {
        "f_gu": gu.reshape(FULL, P, 2 * DC * P),
        "f_gu_rest": rest.reshape(P, 2 * DC * REST),
        "f_d": down[:full].reshape(FULL, P, D),
        "f_d_rest": down[full:],
        "f_b": biases[:full].reshape(FULL, P, 2),
        "f_b_rest": biases[full:],
        "f_b_down": a["L0_ffn_b_down"],
        "g_mask": a["mask_1x1xSxS2_bk0"].reshape(P, P),
        "g_cos": np.cos(phase),
        "g_sin": np.sin(phase) * sign,
        "g_wQ": head_weights(a["L1_xattn_Wq"]).reshape(PAIRS, 2, P, DC * P).transpose(0, 2, 1, 3)
        .reshape(PAIRS, P, 2 * DC * P),
        "g_wK": head_weights(a["L1_xattn_Wk"]).reshape(KV_HEADS, P, DC * P),
        "g_wV": pair_columns(a["L1_xattn_Wv"]),
        "g_wO": pair_rows(a["L1_xattn_Wo"]),
        "l_a": a["L1_ffn_lora_A"].reshape(LORA, D),
        "l_b": a["L1_ffn_lora_B"].transpose(0, 2, 1).reshape(LORA, D),
        "l_coef": a["L1_ffn_lora_weights"],
        "l_w": a["L1_ffn_W"].T,
        "l_bias": a["L1_ffn_bias"],
    }


def kernel(**inputs):
    import concourse.bacc as bacc
    from concourse.bass_utils import run_bass_kernel_spmd

    arrays = lay_out({n: np.asarray(v) for n, v in inputs.items()})
    nc = bacc.Bacc("TRN2", target_bir_lowering=False, num_devices=1)
    io = {n: nc.dram_tensor("in_" + n, v.shape, mybir.dt.from_np(v.dtype), kind="ExternalInput").ap()
          for n, v in arrays.items()}
    out = nc.dram_tensor("out", (B, P, D), F32, kind="ExternalOutput").ap()
    build(nc, io, out)
    run = run_bass_kernel_spmd(nc, [{"in_" + n: v for n, v in arrays.items()}], core_ids=[0])
    return np.asarray(run.results[0]["out"])
```
